# Optimizing a Trainium2 kernel written in Bass

```python
import numpy as np
import jax
import jax.numpy as jnp

def _softmax(x, axis=-1):
    return jax.nn.softmax(x, axis=axis)

def _gelu(x):
    return jax.nn.gelu(x, approximate=True)

def _silu(x):
    return jax.nn.silu(x)

def _sigmoid(x):
    return jax.nn.sigmoid(x)

def _layernorm(x, axis=-1, eps=1e-05):
    m = jnp.mean(x, axis=axis, keepdims=True)
    v = jnp.var(x, axis=axis, keepdims=True)
    return (x - m) / jnp.sqrt(v + eps)

def _scatter_add(tgt, idx, src, axis=0):
    return tgt.at[idx].add(src)

def _segment_sum(src, seg, n):
    return jax.ops.segment_sum(src, seg, n)
kernel_name = 'mk_conv_preact_d2_conv_nhwc64_r2_83c83b'

def setup_inputs(seed: int=0):
    np.random.seed(seed)
    _w = jnp.asarray

    def _rec_inputs():
        import jax
        import jax.numpy as jnp
        _gk = jax.random.key(seed)
        x = -0.0003929 + 0.9999 * jax.random.normal(jax.random.fold_in(_gk, 1), (32, 64, 32, 32), jnp.float32)
        return x
    x = _rec_inputs()

    def _L0_conv_setup():
        import jax, jax.numpy as jnp
        import numpy as np
        B, C, H, W = (32, 64, 32, 32)
        WS, SHIFT, HEADS = (8, 4, 4)
        HID = 4 * C
        META_H = 128
        TOK = WS * WS
        NW = H // WS * (W // WS)
        DH = C // HEADS

        def _rel_coords_log():
            idx = np.arange(WS)
            ch, cw = np.meshgrid(idx, idx, indexing='ij')
            coords = np.stack([ch, cw], 0).reshape(2, -1)
            rel = coords[:, :, None] - coords[:, None, :]
            rel = rel.transpose(1, 2, 0).reshape(-1, 2).astype(np.float32)
            return np.sign(rel) * np.log1p(np.abs(rel))

        def _attention_mask():
            m = np.zeros((H, W), np.float32)
            cnt = 0
            for hs in (slice(0, -WS), slice(-WS, -SHIFT), slice(-SHIFT, None)):
                for ws_ in (slice(0, -WS), slice(-WS, -SHIFT), slice(-SHIFT, None)):
                    m[hs, ws_] = cnt
                    cnt += 1
            mw = m.reshape(H // WS, WS, W // WS, WS).transpose(0, 2, 1, 3).reshape(-1, TOK)
            am = mw[:, None, :] - mw[:, :, None]
            return np.where(am != 0, -100.0, 0.0).astype(np.float32)
        _REL = jnp.asarray(_rel_coords_log())
        _MASK = jnp.asarray(_attention_mask())

        def _layer_norm(t, g, b, eps=1e-05):
            mu = t.mean(-1, keepdims=True)
            var = ((t - mu) ** 2).mean(-1, keepdims=True)
            return (t - mu) * jax.lax.rsqrt(var + eps) * g + b

        def _forward(x, qkv_w, qkv_b, proj_w, proj_b, meta_w1, meta_b1, meta_w2, meta_b2, tau, ln1_g, ln1_b, ln2_g, ln2_b, ffn_w1, ffn_b1, ffn_w2, ffn_b2):
            xs = jnp.roll(x, shift=(-SHIFT, -SHIFT), axis=(2, 3))
            xw = xs.transpose(0, 2, 3, 1).reshape(B, H // WS, WS, W // WS, WS, C)
            xw = xw.transpose(0, 1, 3, 2, 4, 5).reshape(B * NW, TOK, C)
            qkv = xw @ qkv_w + qkv_b
            q, k, v = jnp.split(qkv, 3, axis=-1)
            split = lambda t: t.reshape(B * NW, TOK, HEADS, DH).transpose(0, 2, 1, 3)
            q, k, v = (split(q), split(k), split(v))
            scores = jnp.einsum('bhqd,bhkd->bhqk', q, k)
            qn = jnp.linalg.norm(q, axis=-1, keepdims=True)
            kn = jnp.linalg.norm(k, axis=-1, keepdims=True)
            scores = scores / jnp.maximum(qn * kn.transpose(0, 1, 3, 2), 1e-06)
            scores = scores / jnp.clip(tau, 0.01)[None, :, None, None]
            bias = jax.nn.relu(_REL @ meta_w1 + meta_b1) @ meta_w2 + meta_b2
            bias = bias.T.reshape(HEADS, TOK, TOK)
            scores = scores + bias[None]
            scores = scores.reshape(B, NW, HEADS, TOK, TOK) + _MASK[None, :, None]
            attn = jax.nn.softmax(scores.reshape(B * NW, HEADS, TOK, TOK), axis=-1)
            out = jnp.einsum('bhqk,bhkd->bhqd', attn, v)
            out = out.transpose(0, 2, 1, 3).reshape(B * NW, TOK, C)
            out = out @ proj_w + proj_b
            om = out.reshape(B, H // WS, W // WS, WS, WS, C).transpose(0, 1, 3, 2, 4, 5).reshape(B, H, W, C)
            om = jnp.roll(om, shift=(SHIFT, SHIFT), axis=(1, 2))
            xin = x.transpose(0, 2, 3, 1)
            skip = xin + _layer_norm(om, ln1_g, ln1_b)
            ffn = jax.nn.gelu(skip @ ffn_w1 + ffn_b1, approximate=False) @ ffn_w2 + ffn_b2
            out = skip + _layer_norm(ffn, ln2_g, ln2_b)
            return out.transpose(0, 3, 1, 2)
        key = jax.random.key(seed)
        ks = jax.random.split(key, 8)
        s = lambda fan: 1.0 / np.sqrt(fan)
        return {'x': jax.random.normal(ks[0], (B, C, H, W), jnp.float32), 'qkv_w': jax.random.normal(ks[1], (C, 3 * C), jnp.float32) * s(C), 'qkv_b': jnp.zeros((3 * C,), jnp.float32), 'proj_w': jax.random.normal(ks[2], (C, C), jnp.float32) * s(C), 'proj_b': jnp.zeros((C,), jnp.float32), 'meta_w1': jax.random.normal(ks[3], (2, META_H), jnp.float32) * s(2), 'meta_b1': jnp.zeros((META_H,), jnp.float32), 'meta_w2': jax.random.normal(ks[4], (META_H, HEADS), jnp.float32) * s(META_H), 'meta_b2': jnp.zeros((HEADS,), jnp.float32), 'tau': jnp.ones((HEADS,), jnp.float32), 'ln1_g': jnp.ones((C,), jnp.float32), 'ln1_b': jnp.zeros((C,), jnp.float32), 'ln2_g': jnp.ones((C,), jnp.float32), 'ln2_b': jnp.zeros((C,), jnp.float32), 'ffn_w1': jax.random.normal(ks[5], (C, HID), jnp.float32) * s(C), 'ffn_b1': jnp.zeros((HID,), jnp.float32), 'ffn_w2': jax.random.normal(ks[6], (HID, C), jnp.float32) * s(HID), 'ffn_b2': jnp.zeros((C,), jnp.float32)}
    _L0_conv_all = _L0_conv_setup()
    _L0_conv_in = {k: v for k, v in _L0_conv_all.items() if k in ('qkv_w', 'qkv_b', 'proj_w', 'proj_b', 'meta_w1', 'meta_b1', 'meta_w2', 'meta_b2', 'tau', 'ln1_g', 'ln1_b', 'ln2_g', 'ln2_b', 'ffn_w1', 'ffn_b1', 'ffn_w2', 'ffn_b2')}
    del _L0_conv_all

    def _L1_conv_setup():
        import jax, jax.numpy as jnp
        import numpy as np
        N = 32
        CH = 64
        RES = 32
        LRF = 4
        LH = RES // LRF
        LW = RES // LRF
        L = LH * LW
        K = max(1, int(L * 0.1))
        NB = LRF * LRF
        OC = CH // 10 + 1
        INDIM = K * CH + L
        HID = INDIM
        OUTDIM = L * OC
        key = jax.random.key(seed)
        ks = jax.random.split(key, 8)
        x = jax.random.normal(ks[0], (N, CH, RES, RES), jnp.float32)
        conv_w = jax.random.normal(ks[1], (NB, CH), jnp.float32) * 0.05
        W1 = jax.random.normal(ks[2], (INDIM, HID), jnp.float32) * 0.02
        b1 = jnp.zeros((HID,), jnp.float32)
        W2 = jax.random.normal(ks[3], (HID, OUTDIM), jnp.float32) * 0.02
        b2 = jnp.zeros((OUTDIM,), jnp.float32)
        out_w = jax.random.normal(ks[4], (CH, OC), jnp.float32) * 0.05
        return dict(x=x, conv_w=conv_w, W1=W1, b1=b1, W2=W2, b2=b2, out_w=out_w, tau=1)
    _L1_conv_all = _L1_conv_setup()
    _L1_conv_in = {k: v for k, v in _L1_conv_all.items() if k in ('conv_w', 'W1', 'b1', 'W2', 'b2', 'out_w')}
    del _L1_conv_all
    return {'x': x, 'L0_conv_qkv_w': _L0_conv_in['qkv_w'], 'L0_conv_qkv_b': _L0_conv_in['qkv_b'], 'L0_conv_proj_w': _L0_conv_in['proj_w'], 'L0_conv_proj_b': _L0_conv_in['proj_b'], 'L0_conv_meta_w1': _L0_conv_in['meta_w1'], 'L0_conv_meta_b1': _L0_conv_in['meta_b1'], 'L0_conv_meta_w2': _L0_conv_in['meta_w2'], 'L0_conv_meta_b2': _L0_conv_in['meta_b2'], 'L0_conv_tau': _L0_conv_in['tau'], 'L0_conv_ln1_g': _L0_conv_in['ln1_g'], 'L0_conv_ln1_b': _L0_conv_in['ln1_b'], 'L0_conv_ln2_g': _L0_conv_in['ln2_g'], 'L0_conv_ln2_b': _L0_conv_in['ln2_b'], 'L0_conv_ffn_w1': _L0_conv_in['ffn_w1'], 'L0_conv_ffn_b1': _L0_conv_in['ffn_b1'], 'L0_conv_ffn_w2': _L0_conv_in['ffn_w2'], 'L0_conv_ffn_b2': _L0_conv_in['ffn_b2'], 'L1_conv_conv_w': _L1_conv_in['conv_w'], 'L1_conv_W1': _L1_conv_in['W1'], 'L1_conv_b1': _L1_conv_in['b1'], 'L1_conv_W2': _L1_conv_in['W2'], 'L1_conv_b2': _L1_conv_in['b2'], 'L1_conv_out_w': _L1_conv_in['out_w']}

def reference(x, L0_conv_qkv_w, L0_conv_qkv_b, L0_conv_proj_w, L0_conv_proj_b, L0_conv_meta_w1, L0_conv_meta_b1, L0_conv_meta_w2, L0_conv_meta_b2, L0_conv_tau, L0_conv_ln1_g, L0_conv_ln1_b, L0_conv_ln2_g, L0_conv_ln2_b, L0_conv_ffn_w1, L0_conv_ffn_b1, L0_conv_ffn_w2, L0_conv_ffn_b2, L1_conv_conv_w, L1_conv_W1, L1_conv_b1, L1_conv_W2, L1_conv_b2, L1_conv_out_w):
    import jax
    import jax.numpy as jnp

    def _L0_conv_ref(x, qkv_w, qkv_b, proj_w, proj_b, meta_w1, meta_b1, meta_w2, meta_b2, tau, ln1_g, ln1_b, ln2_g, ln2_b, ffn_w1, ffn_b1, ffn_w2, ffn_b2):
        import jax, jax.numpy as jnp
        import numpy as np
        B, C, H, W = (32, 64, 32, 32)
        WS, SHIFT, HEADS = (8, 4, 4)
        HID = 4 * C
        META_H = 128
        TOK = WS * WS
        NW = H // WS * (W // WS)
        DH = C // HEADS

        def _rel_coords_log():
            idx = np.arange(WS)
            ch, cw = np.meshgrid(idx, idx, indexing='ij')
            coords = np.stack([ch, cw], 0).reshape(2, -1)
            rel = coords[:, :, None] - coords[:, None, :]
            rel = rel.transpose(1, 2, 0).reshape(-1, 2).astype(np.float32)
            return np.sign(rel) * np.log1p(np.abs(rel))

        def _attention_mask():
            m = np.zeros((H, W), np.float32)
            cnt = 0
            for hs in (slice(0, -WS), slice(-WS, -SHIFT), slice(-SHIFT, None)):
                for ws_ in (slice(0, -WS), slice(-WS, -SHIFT), slice(-SHIFT, None)):
                    m[hs, ws_] = cnt
                    cnt += 1
            mw = m.reshape(H // WS, WS, W // WS, WS).transpose(0, 2, 1, 3).reshape(-1, TOK)
            am = mw[:, None, :] - mw[:, :, None]
            return np.where(am != 0, -100.0, 0.0).astype(np.float32)
        _REL = jnp.asarray(_rel_coords_log())
        _MASK = jnp.asarray(_attention_mask())

        def _layer_norm(t, g, b, eps=1e-05):
            mu = t.mean(-1, keepdims=True)
            var = ((t - mu) ** 2).mean(-1, keepdims=True)
            return (t - mu) * jax.lax.rsqrt(var + eps) * g + b

        def _forward(x, qkv_w, qkv_b, proj_w, proj_b, meta_w1, meta_b1, meta_w2, meta_b2, tau, ln1_g, ln1_b, ln2_g, ln2_b, ffn_w1, ffn_b1, ffn_w2, ffn_b2):
            xs = jnp.roll(x, shift=(-SHIFT, -SHIFT), axis=(2, 3))
            xw = xs.transpose(0, 2, 3, 1).reshape(B, H // WS, WS, W // WS, WS, C)
            xw = xw.transpose(0, 1, 3, 2, 4, 5).reshape(B * NW, TOK, C)
            qkv = xw @ qkv_w + qkv_b
            q, k, v = jnp.split(qkv, 3, axis=-1)
            split = lambda t: t.reshape(B * NW, TOK, HEADS, DH).transpose(0, 2, 1, 3)
            q, k, v = (split(q), split(k), split(v))
            scores = jnp.einsum('bhqd,bhkd->bhqk', q, k)
            qn = jnp.linalg.norm(q, axis=-1, keepdims=True)
            kn = jnp.linalg.norm(k, axis=-1, keepdims=True)
            scores = scores / jnp.maximum(qn * kn.transpose(0, 1, 3, 2), 1e-06)
            scores = scores / jnp.clip(tau, 0.01)[None, :, None, None]
            bias = jax.nn.relu(_REL @ meta_w1 + meta_b1) @ meta_w2 + meta_b2
            bias = bias.T.reshape(HEADS, TOK, TOK)
            scores = scores + bias[None]
            scores = scores.reshape(B, NW, HEADS, TOK, TOK) + _MASK[None, :, None]
            attn = jax.nn.softmax(scores.reshape(B * NW, HEADS, TOK, TOK), axis=-1)
            out = jnp.einsum('bhqk,bhkd->bhqd', attn, v)
            out = out.transpose(0, 2, 1, 3).reshape(B * NW, TOK, C)
            out = out @ proj_w + proj_b
            om = out.reshape(B, H // WS, W // WS, WS, WS, C).transpose(0, 1, 3, 2, 4, 5).reshape(B, H, W, C)
            om = jnp.roll(om, shift=(SHIFT, SHIFT), axis=(1, 2))
            xin = x.transpose(0, 2, 3, 1)
            skip = xin + _layer_norm(om, ln1_g, ln1_b)
            ffn = jax.nn.gelu(skip @ ffn_w1 + ffn_b1, approximate=False) @ ffn_w2 + ffn_b2
            out = skip + _layer_norm(ffn, ln2_g, ln2_b)
            return out.transpose(0, 3, 1, 2)
        return _forward(x, qkv_w, qkv_b, proj_w, proj_b, meta_w1, meta_b1, meta_w2, meta_b2, tau, ln1_g, ln1_b, ln2_g, ln2_b, ffn_w1, ffn_b1, ffn_w2, ffn_b2)

    def _L1_conv_ref(x, conv_w, W1, b1, W2, b2, out_w, tau):
        import jax, jax.numpy as jnp
        import numpy as np
        N = 32
        CH = 64
        RES = 32
        LRF = 4
        LH = RES // LRF
        LW = RES // LRF
        L = LH * LW
        K = max(1, int(L * 0.1))
        NB = LRF * LRF
        OC = CH // 10 + 1
        INDIM = K * CH + L
        HID = INDIM
        OUTDIM = L * OC
        n, c, H, W = x.shape
        xb = x.reshape(n, c, LRF, LH, LRF, LW).transpose(2, 4, 0, 1, 3, 5)
        xb = xb.reshape(NB, n, c, L)
        scores = jnp.einsum('gbcl,gc->gbl', xb, conv_w)
        e = jnp.exp(scores)
        p = e / jnp.sum(e, axis=-1, keepdims=True)
        _, idx = jax.lax.top_k(p, K)
        mask = jnp.sum(jax.nn.one_hot(idx, L, dtype=p.dtype), axis=2)
        st = jax.lax.stop_gradient(mask - p) + p
        out = st[:, :, None, :] * xb
        idx_s = jnp.sort(idx, axis=-1)
        gath = jnp.take_along_axis(out, idx_s[:, :, None, :], axis=-1)
        feat = jnp.concatenate([gath.transpose(0, 1, 3, 2).reshape(NB, n, K * c), st], axis=-1)
        h = jax.nn.relu(feat @ W1 + b1)
        rec = (h @ W2 + b2).reshape(NB, n, OC, LH, LW)
        grid = rec.reshape(LRF, LRF, n, OC, LH, LW).transpose(2, 3, 0, 4, 1, 5)
        grid = grid.reshape(n, OC, H, W)
        return jnp.einsum('bohw,co->bchw', grid, out_w)

    def _gn(v, G=32, eps=1e-05):
        B_, H_, W_, C_ = v.shape
        g = v.reshape(B_, H_, W_, G, C_ // G)
        m = jnp.mean(g, axis=(1, 2, 4), keepdims=True)
        s = jnp.var(g, axis=(1, 2, 4), keepdims=True)
        return ((g - m) / jnp.sqrt(s + eps)).reshape(v.shape)

    def _ln_c(v, eps=1e-06):
        m = jnp.mean(v, axis=-1, keepdims=True)
        s = jnp.var(v, axis=-1, keepdims=True)
        return (v - m) / jnp.sqrt(s + eps)

    def _ln_t(v, eps=1e-05):
        m = jnp.mean(v, axis=-1, keepdims=True)
        s = jnp.var(v, axis=-1, keepdims=True)
        return (v - m) / jnp.sqrt(s + eps)

    def _to_tokens(v):
        B_, H_, W_, C_ = v.shape
        return v.reshape(B_, H_ * W_, C_)

    def _from_tokens(t, like):
        return t.reshape(like.shape)
    x = x + _L0_conv_ref(_gn(x), L0_conv_qkv_w, L0_conv_qkv_b, L0_conv_proj_w, L0_conv_proj_b, L0_conv_meta_w1, L0_conv_meta_b1, L0_conv_meta_w2, L0_conv_meta_b2, L0_conv_tau, L0_conv_ln1_g, L0_conv_ln1_b, L0_conv_ln2_g, L0_conv_ln2_b, L0_conv_ffn_w1, L0_conv_ffn_b1, L0_conv_ffn_w2, L0_conv_ffn_b2)
    x = x + _L1_conv_ref(_gn(x), L1_conv_conv_w, L1_conv_W1, L1_conv_b1, L1_conv_W2, L1_conv_b2, L1_conv_out_w, 1)
    return x

_drawn_inputs = setup_inputs


def setup_inputs(seed=0):
    import zlib

    import numpy as np

    out = dict(_drawn_inputs(seed))
    spreads = {'L0_conv_qkv_b': (0.0, 0.1),
     'L0_conv_proj_b': (0.0, 0.1),
     'L0_conv_meta_b1': (0.0, 0.769),
     'L0_conv_meta_b2': (0.0, 0.8),
     'L0_conv_tau': (1.0, 0.2),
     'L0_conv_ln1_g': (1.0, 0.2),
     'L0_conv_ln1_b': (0.0, 0.1),
     'L0_conv_ln2_g': (1.0, 0.2),
     'L0_conv_ln2_b': (0.0, 0.1),
     'L0_conv_ffn_b1': (0.0, 0.1),
     'L0_conv_ffn_b2': (0.0, 0.1),
     'L1_conv_b1': (0.0, 0.8),
     'L1_conv_b2': (0.0, 0.8)}
    factors = {'L1_conv_conv_w': 8.0, 'L1_conv_W1': 8.0, 'L1_conv_W2': 8.0, 'L1_conv_out_w': 6.333}
    for name, (base, spread) in spreads.items():
        noise = np.random.default_rng([zlib.crc32(name.encode()), seed]).standard_normal(out[name].shape)
        drawn = base * np.exp(spread * noise) if base else spread * noise
        out[name] = jnp.asarray(drawn.astype(out[name].dtype))
    for name, factor in factors.items():
        out[name] = (out[name] * factor).astype(out[name].dtype)
    return out
```

```python
from contextlib import ExitStack

import numpy as np

import concourse.bass as bass
from concourse import mybir

F32 = mybir.dt.float32
U32 = mybir.dt.uint32
ALU = mybir.AluOpType
ACT = mybir.ActivationFunctionType
X = mybir.AxisListType.X

B, C, H, W = 32, 64, 32, 32
PAIRS = B // 2
PIX = H * W
WS, SHIFT, HEADS = 8, 4, 4
DH = C // HEADS
TOK = WS * WS
UNITS = 2 * PAIRS
COLS = 512
WIN = 8
DUOS = 4 * UNITS
FFN = 4 * C
META = 128
NORM_FLOOR = 1e-18
HALVES = ((0, 64), (64, 128))
EXP_LN = "natural_log_exp_and_others"

BLOCKS = 16
TOP = 6
OC = C // 10 + 1
INDIM = TOP * C + TOK
MT = INDIM // 4
OUTDIM = TOK * OC


def after(eng, sem, count, limit=None):
    if isinstance(count, int):
        if limit is not None:
            count = min(count, limit)
        if count <= 0:
            return
    eng.wait_ge(sem, count)


def there(index, limit):
    return not isinstance(index, int) or 0 <= index < limit


def build(nc, x, qkv_w, qkv_b, proj_w, proj_b, meta_w1, meta_b1, meta_w2, meta_b2, tau, ln1_g, ln1_b,
          ln2_g, ln2_b, ffn_w1, ffn_b1, ffn_w2, ffn_b2, conv_w, mlp_w1, mlp_b1, mlp_w2, mlp_b2, out_w,
          c_ident, c_head, c_image, c_delta, c_rel, c_mask, c_iota, rec_dram, out):
    with ExitStack() as whole:
        def sb(stack, name, shape, dt=F32):
            return stack.enter_context(nc.sbuf_tensor(name, shape, dt))

        def ps(stack, name, shape):
            return stack.enter_context(nc.psum_tensor(name, shape, F32))

        def sem(stack, name):
            return stack.enter_context(nc.semaphore(name))

        xs = sb(whole, "xs", [128, PAIRS, PIX])
        ident = sb(whole, "ident", [128, 128])
        sum_head = sb(whole, "sum_head", [128, 128])
        sum_image = sb(whole, "sum_image", [128, 128])
        mean_image = sb(whole, "mean_image", [128, 128])
        mean_group = sb(whole, "mean_group", [128, 128])

        def group_norm(stage, tag, src, dst, arrive, copy_out=None):
            n = {k: sem(stage, f"{tag}_{k}") for k in
                 ("rowsum", "mean", "centred", "square", "sqsum", "var", "ln", "rstd", "normed")}
            rowsum = sb(stage, f"{tag}_rowsum_sb", [128, 2, W])
            sqsum = sb(stage, f"{tag}_sqsum_sb", [128, 2, W])
            lnvar = sb(stage, f"{tag}_lnvar_sb", [128, 2, W])
            rstd = sb(stage, f"{tag}_rstd_sb", [128, 2, W])
            square = sb(stage, f"{tag}_square_sb", [128, 2, PIX])
            mean_ps = [ps(stage, f"{tag}_mean_ps{k}", [128, COLS]) for k in range(2)]
            var_ps = [ps(stage, f"{tag}_var_ps{k}", [128, COLS]) for k in range(2)]

            def columns(a):
                return a.rearrange("c (h w) -> c w h", w=W)

            def vector(eng, p, k):
                if there(p, PAIRS):
                    arrive(eng, p, k)
                    after(eng, n["mean"], p - 1, PAIRS)
                    eng.tensor_reduce(rowsum[:, k], columns(src[:, p]), X, ALU.add)\
                       .then_inc(n["rowsum"], 1)
                if there(p - 1, PAIRS):
                    after(eng, n["square"], p)
                    after(eng, n["var"], p - 2)
                    eng.tensor_reduce(sqsum[:, 1 - k], columns(square[:, 1 - k]), X, ALU.add)\
                       .then_inc(n["sqsum"], 1)
                if there(p, PAIRS):
                    after(eng, n["mean"], p + 1)
                    eng.tensor_tensor(
                        dst[:, p].rearrange("c (h w) -> c h w", w=W),
                        src[:, p].rearrange("c (h w) -> c h w", w=W),
                        mean_ps[k][:, 0:W].unsqueeze(1).broadcast_to([128, H, W]),
                        ALU.subtract).then_inc(n["centred"], 1)

            def tensor(eng, p, k):
                if there(p, PAIRS):
                    after(eng, n["rowsum"], p + 1)
                    after(eng, n["centred"], p - 1)
                    eng.matmul(mean_ps[k][:, 0:W], mean_group[:, :], rowsum[:, k], start=True, stop=True)\
                       .then_inc(n["mean"], 1)
                if there(p - 1, PAIRS):
                    after(eng, n["sqsum"], p)
                    after(eng, n["ln"], p - 2)
                    eng.matmul(var_ps[1 - k][:, 0:W], mean_group[:, :], sqsum[:, 1 - k],
                               start=True, stop=True).then_inc(n["var"], 1)

            def scalar(eng, p, k):
                if there(p, PAIRS):
                    after(eng, n["centred"], p + 1)
                    after(eng, n["sqsum"], p - 1)
                    eng.activation(square[:, k], dst[:, p], ACT.Square).then_inc(n["square"], 1)
                if there(p - 1, PAIRS):
                    after(eng, n["var"], p)
                    after(eng, n["normed"], p - 2)
                    eng.activation(lnvar[:, 1 - k], var_ps[1 - k][:, 0:W], ACT.Ln, bias=eps[:, 0:1])\
                       .then_inc(n["ln"], 1)
                    eng.wait_ge(n["ln"], p)
                    eng.activation(rstd[:, 1 - k], lnvar[:, 1 - k], ACT.Exp, scale=-0.5)\
                       .then_inc(n["rstd"], 1)

            def pool(eng, p, k):
                if there(p, PAIRS):
                    after(eng, n["rstd"], p + 1)
                    after(eng, n["square"], p + 1)
                    v = dst[:, p].rearrange("c (h w) -> c h w", w=W)
                    eng.tensor_tensor(v, v, rstd[:, k].unsqueeze(1).broadcast_to([128, H, W]),
                                      ALU.mult).then_inc(n["normed"], 1)

            def run(eng, step, flush=True):
                step(eng, 0, 0)
                step(eng, 1, 1)
                with eng.Fori(1, PAIRS // 2) as i:
                    step(eng, 2 * i, 0)
                    step(eng, 2 * i + 1, 1)
                if flush:
                    step(eng, PAIRS, 0)

            return n, run, vector, tensor, scalar, pool, rstd

        attention = whole.enter_context(ExitStack())
        eps = sb(whole, "eps", [128, 2])
        wq, wk, wv, wp = (sb(attention, n, [128, 128]) for n in ("wq", "wk", "wv", "wp"))
        bq, bk, bv, bp = (sb(attention, n, [128, 1]) for n in ("bq", "bk", "bv", "bp"))
        g1, b1 = sb(attention, "g1", [128, 1]), sb(attention, "b1", [128, 1])
        head_scale = sb(attention, "head_scale", [128, HEADS])
        bias_tab = sb(attention, "bias_tab", [128, 4, 2, HEADS, TOK])

        with ExitStack() as stage:
            w_in = sem(stage, "w_in")
            zeroed = sem(stage, "zeroed")
            chain = sem(stage, "chain")
            hid_ps_ready = sem(stage, "hid_ps_ready")
            hid_ready = sem(stage, "hid_ready")
            bias_ready = sem(stage, "bias_ready")
            bp_mean = sem(stage, "bp_mean")
            x_in = [sem(stage, f"x_in{k}") for k in range(2)]
            pw = sb(stage, "pw", [128, C])
            small = sb(stage, "small", [128, 8])
            tau_sb = sb(stage, "tau_sb", [128, HEADS])
            delta = sb(stage, "delta", [128, HEADS])
            rel = sb(stage, "rel", [2, TOK * TOK])
            mw1 = sb(stage, "mw1", [2, META])
            mb1 = sb(stage, "mb1", [META, 1])
            mw2 = sb(stage, "mw2", [META, HEADS])
            mb2 = sb(stage, "mb2", [128, HEADS])
            mask = sb(stage, "mask", [128, 4, 2, TOK])
            hid = sb(stage, "hid", [META, TOK * TOK])
            bias_q = sb(stage, "bias_q", [128, HEADS, TOK])
            hid_ps = [ps(stage, f"hid_ps{k}", [128, COLS]) for k in range(2)]
            bias_ps = ps(stage, "bias_ps", [128, COLS])

            def column(v, lo=0):
                return v[lo:lo + 64].rearrange("(c a) -> c a", a=1)

            def all_rows(v, n):
                return v.rearrange("(a n) -> a n", a=1).broadcast_to([128, n])

            loads = [(ident[:, :], c_ident), (sum_head[:, :], c_head), (sum_image[:, :], c_image),
                     (delta[:, :], c_delta), (rel[:, :], c_rel), (mask[:, :, :, :], c_mask),
                     (mw1[:, :], meta_w1), (mb1[:, :], meta_b1.rearrange("(c a) -> c a", a=1)),
                     (mw2[:, :], meta_w2), (mb2[:, :], all_rows(meta_b2, HEADS)),
                     (tau_sb[:, :], all_rows(tau, HEADS))]
            for lo, hi in HALVES:
                loads += [(wq[lo:hi, lo:hi], qkv_w[:, 0:64]), (wk[lo:hi, lo:hi], qkv_w[:, 64:128]),
                          (wv[lo:hi, lo:hi], qkv_w[:, 128:192]), (pw[lo:hi, :], proj_w),
                          (bq[lo:hi, :], column(qkv_b, 0)), (bk[lo:hi, :], column(qkv_b, 64)),
                          (bv[lo:hi, :], column(qkv_b, 128)), (small[lo:hi, 0:1], column(proj_b)),
                          (g1[lo:hi, :], column(ln1_g)), (b1[lo:hi, :], column(ln1_b))]
            x_pairs = x.rearrange("(a p) c h w -> a c p (h w)", a=2)

            def x_arrives(eng, p, k):
                after(eng, x_in[k], (p // 2 + 1 if isinstance(p, int) else (p - k) // 2 + 1) * 32)

            n1, gn_run, gn_v, gn_t, gn_a, gn_p, _ = group_norm(stage, "gn1", xs, xs, x_arrives)

            with nc.Block() as block:
                @block.sync
                def _(sp):
                    def load_pair(i, k):
                        after(sp, x_in[k], 32 * i)
                        for a, (lo, hi) in enumerate(HALVES):
                            sp.dma_start(xs[lo:hi, 2 * i + k], x_pairs[a, :, 2 * i + k]).then_inc(x_in[k], 16)

                    load_pair(0, 0)
                    load_pair(0, 1)
                    with sp.Fori(1, PAIRS // 2) as i:
                        load_pair(i, 0)
                        load_pair(i, 1)

                @block.scalar
                def _(act):
                    act.preload_act_table_set(EXP_LN)
                    act.wait_ge(zeroed, 1)
                    for dst, src in loads:
                        act.dma_start(dst, src).then_inc(w_in, 16)
                    act.wait_ge(w_in, 16 * len(loads))
                    for n in range(8):
                        act.wait_ge(hid_ps_ready, n + 1)
                        act.activation(hid[:, n * COLS:(n + 1) * COLS], hid_ps[n % 2][:, :], ACT.Relu,
                                       bias=mb1[:, 0:1]).then_inc(hid_ready, 1)
                    act.wait_ge(chain, 4)
                    gn_run(act, gn_a)

                @block.gpsimd
                def _(pool):
                    for t in (wq, wk, wv, wp):
                        last = pool.memset(t[:, :], 0.0)
                    last.then_inc(zeroed, 1)
                    gn_run(pool, gn_p, flush=False)

                @block.vector
                def _(dve):
                    links = [0]

                    def link(ins):
                        links[0] += 1
                        ins.then_inc(chain, 1)
                        dve.wait_ge(chain, links[0])

                    link(dve.memset(eps[:, 0:1], 1e-5))
                    link(dve.memset(eps[:, 1:2], NORM_FLOOR))
                    dve.wait_ge(w_in, 16 * len(loads))
                    link(dve.tensor_scalar(mean_image[:, :], sum_image[:, :], 1.0 / C, None, ALU.mult))
                    link(dve.tensor_scalar(mean_group[:, :], sum_image[:, :], 1.0 / (C * H), None, ALU.mult))
                    gn_run(dve, gn_v)
                    link(dve.tensor_scalar(tau_sb[:, :], tau_sb[:, :], 0.01, None, ALU.max))
                    link(dve.reciprocal(tau_sb[:, :], tau_sb[:, :]))
                    link(dve.tensor_tensor(head_scale[:, :], tau_sb[:, :], delta[:, :], ALU.mult))
                    link(dve.tensor_reduce(small[:, 1:2], pw[:, :], X, ALU.add))
                    link(dve.tensor_scalar(small[:, 2:3], small[:, 1:2], -1.0 / C, None, ALU.mult))
                    for lo, hi in HALVES:
                        link(dve.tensor_scalar(wp[lo:hi, lo:hi], pw[lo:hi, :], small[lo:hi, 2:3], None, ALU.add))
                    dve.wait_ge(bp_mean, 1)
                    link(dve.tensor_tensor(bp[:, :], small[:, 0:1], bias_ps[:, 256:257], ALU.subtract))
                    dve.wait_ge(bias_ready, 1)
                    link(dve.tensor_tensor(
                        bias_q[:, :, :], bias_ps[:, 0:256].rearrange("q (k h) -> q h k", h=HEADS),
                        mb2[:, :].unsqueeze(2).broadcast_to([128, HEADS, TOK]), ALU.add))
                    for kind in range(4):
                        for w in range(2):
                            link(dve.tensor_tensor(
                                bias_tab[:, kind, w], bias_q[:, :, :],
                                mask[:, kind, w].unsqueeze(1).broadcast_to([128, HEADS, TOK]), ALU.add))

                @block.tensor
                def _(pe):
                    pe.wait_ge(w_in, 16 * len(loads))
                    for n in range(8):
                        if n >= 2:
                            pe.wait_ge(hid_ready, n - 1)
                        pe.matmul(hid_ps[n % 2][:, :], mw1[:, :], rel[:, n * COLS:(n + 1) * COLS],
                                  start=True, stop=True).then_inc(hid_ps_ready, 1)
                    pe.wait_ge(hid_ready, 8)
                    by_query = hid[:, :].rearrange("m (q k) -> m k q", k=TOK)
                    pe.wait_ge(chain, 4)
                    pe.matmul(bias_ps[:, 256:257], mean_image[:, :], small[:, 0:1], start=True, stop=True)\
                      .then_inc(bp_mean, 1)
                    for k in range(TOK):
                        for lo, hi in HALVES:
                            last = pe.matmul(bias_ps[lo:hi, HEADS * k:HEADS * (k + 1)], by_query[:, k], mw2[:, :],
                                             start=True, stop=True)
                    last.then_inc(bias_ready, 1)
                    gn_run(pe, gn_t)

        xu = xs[:, :, :].rearrange("c p (j n) -> c (p j) n", j=2)

        def gather_pieces(j):
            for wi in range(2):
                r = 16 * j + WS * wi + SHIFT
                rows = [(r, 0, WS)] if r + WS <= H else [(r, 0, H - r), (0, H - r, WS)]
                for r0, t0, t1 in rows:
                    yield r0, 4, wi, t0, t1, 0, 3, 0, 8
                    yield r0, 28, wi, t0, t1, 3, 4, 0, 4
                    yield r0, 0, wi, t0, t1, 3, 4, 4, 8

        def piece(image, windows, r0, c0, wi, t0, t1, w0, w1, x0, x1):
            img = image.rearrange("c (h w) -> c h w", w=W)[:, r0:r0 + t1 - t0, c0:c0 + (w1 - w0) * (x1 - x0)]
            win = windows.rearrange("c (i j y x) -> c i y j x", i=2, j=4, y=WS)[:, wi, t0:t1, w0:w1, x0:x1]
            return img.rearrange("c h (j x) -> c h j x", x=x1 - x0), win

        with ExitStack() as stage:
            s = {k: sem(stage, k) for k in (
                "xw_ready", "q_ps_ready", "k_ps_ready", "q_ready", "q_sq_ready", "k_ready", "k_sq_ready",
                "q_norm_ps", "k_norm_ps", "q_ln", "k_ln", "q_rnorm", "k_rnorm", "q_spread", "k_scaled",
                "k_spread", "xw_saved", "v_ps_ready", "v_spread", "heads_copied", "proj_ps", "centred",
                "var_ps_ready", "var_ln", "rstd_ready", "normed", "skip_ready",
                "scores", "biased", "row_max", "shifted", "exped", "row_sum", "row_recip", "probs",
                "probs_t", "probs_t_copied", "mixed")}
            xw = [sb(stage, f"xw{j}", [128, COLS]) for j in range(2)]
            q_sb, k_sb, q_sq, k_sq, rq, rk = (sb(stage, n, [128, COLS]) for n in
                                              ("q_sb", "k_sb", "q_sq", "k_sq", "rq", "rk"))
            qd = [sb(stage, f"qd{j}", [128, WIN, 2, TOK]) for j in range(2)]
            kx = [sb(stage, f"kx{j}", [128, WIN, HEADS, TOK]) for j in range(2)]
            vd = [sb(stage, f"vd{j}", [128, WIN, 4, 2 * DH]) for j in range(2)]
            sc = sb(stage, "sc", [128, 4, 2, HEADS, TOK])
            pt = [sb(stage, f"pt{k}", [128, 4, 128]) for k in range(2)]
            mx = sb(stage, "mx", [128, 2, 2 * HEADS])
            sm = sb(stage, "sm", [128, 2, 2 * HEADS])
            rs8 = sb(stage, "rs8", [128, 2, 2 * HEADS])
            ob, cc, csq, rs = (sb(stage, n, [128, COLS]) for n in ("ob", "cc", "csq", "rs"))
            s_ps = [ps(stage, f"s_ps{k}", [128, 2, HEADS, TOK]) for k in range(2)]
            t_ps = [ps(stage, f"t_ps{k}", [128, 4, 128]) for k in range(2)]
            o_ps = ps(stage, "o_ps", [128, COLS])
            qn_ps = ps(stage, "qn_ps", [128, COLS])
            kn_ps = ps(stage, "kn_ps", [128, COLS])
            vv_ps = ps(stage, "vv_ps", [128, COLS])
            zero = sem(stage, "zero")

            def units(eng, slot):
                def both(i):
                    for j in range(2):
                        for q in range(4):
                            slot(eng, 2 * i + j, j, q, 8 * i + 4 * j + q)
                both(-1)
                both(0)
                with eng.Fori(1, PAIRS - 1) as i:
                    both(i)
                both(PAIRS - 1)
                both(PAIRS)

            def tensor_slot(pe, u, j, q, g):
                v, jv = u + 1, 1 - j
                if there(g, DUOS):
                    after(pe, s["biased"], g - 1)
                    if q == 0:
                        after(pe, s["q_spread"], u + 1)
                        after(pe, s["k_spread"], u + 1)
                    for w in range(2):
                        last = pe.matmul(s_ps[g_par(q)][:, w], qd[j][:, 2 * q + w],
                                         kx[j][:, 2 * q + w], start=True, stop=True)
                    last.then_inc(s["scores"], 1)
                if q == 0 and there(v, UNITS):
                    after(pe, s["xw_ready"], v + 1)
                    after(pe, s["centred"], v - 2, UNITS)
                    pe.matmul(qn_ps[:, :], wq[:, :], xw[jv][:, :], start=True, stop=True).then_inc(s["q_ps_ready"], 1)
                    after(pe, s["k_ln"], v)
                    pe.matmul(kn_ps[:, :], wk[:, :], xw[jv][:, :], start=True, stop=True).then_inc(s["k_ps_ready"], 1)
                if q == 0 and there(u - 2, UNITS):
                    after(pe, s["v_spread"], u + 1, UNITS)
                    after(pe, s["centred"], u - 1)
                    pe.matmul(vv_ps[:, :], mean_image[:, :], csq[:, :], start=True, stop=True)\
                      .then_inc(s["var_ps_ready"], 1)
                if q == 1 and there(v, UNITS):
                    after(pe, s["q_sq_ready"], v + 1)
                    pe.matmul(qn_ps[:, :], sum_head[:, :], q_sq[:, :], start=True, stop=True).then_inc(s["q_norm_ps"], 1)
                    after(pe, s["k_sq_ready"], v + 1)
                    pe.matmul(kn_ps[:, :], sum_head[:, :], k_sq[:, :], start=True, stop=True).then_inc(s["k_norm_ps"], 1)
                if q == 2 and there(v, UNITS):
                    after(pe, s["var_ln"], v - 2, UNITS)
                    for t in range(4):
                        last = pe.matmul(vv_ps[:, 128 * t:128 * (t + 1)], xw[jv][:, 128 * t:128 * (t + 1)],
                                         wv[:, :], start=True, stop=True)
                    last.then_inc(s["v_ps_ready"], 1)
                if q == 3 and there(u - 1, UNITS):
                    after(pe, s["q_ln"], v + 1, UNITS)
                    after(pe, s["heads_copied"], u)
                    pe.matmul(qn_ps[:, :], wp[:, :], ob[:, :], start=True, stop=True).then_inc(s["proj_ps"], 1)
                n = g - 2
                if there(n, DUOS):
                    after(pe, s["probs"], n + 1)
                    after(pe, s["probs_t_copied"], n - 1)
                    for w in range(2):
                        for hp in range(2):
                            last = pe.transpose(
                                t_ps[g_par(q)][:, 2 * w + hp],
                                sc[:, (q - 2) % 4, w, 2 * hp:2 * hp + 2].rearrange("c h k -> c (h k)"),
                                ident[:, :])
                    last.then_inc(s["probs_t"], 1)
                n = g - 3
                if there(n, DUOS):
                    m = (q - 3) % 4
                    jn = (1 - j) if q < 3 else j
                    after(pe, s["probs_t_copied"], n + 1)
                    if m == 0:
                        after(pe, s["v_spread"], u + 1)
                        after(pe, s["heads_copied"], u)
                    for w in range(2):
                        for a in range(2):
                            for hp in range(2):
                                at = 2 * a + hp
                                win = 2 * m + w
                                last = pe.matmul(
                                    o_ps[32 * at:32 * at + 32, TOK * win:TOK * (win + 1)],
                                    vd[jn][:, win, at], pt[1 - g_par(q)][:, 2 * w + hp, TOK * a:TOK * (a + 1)],
                                    start=True, stop=True)
                    last.then_inc(s["mixed"], 1)

            def g_par(q):
                return q % 2

            def scalar_slot(act, u, j, q, g):
                v, jv = u + 1, 1 - j
                n = g - 1
                if there(n, DUOS):
                    after(act, s["shifted"], n + 1)
                    t = sc[:, (q - 1) % 4]
                    act.activation(t, t, ACT.Exp).then_inc(s["exped"], 1)
                n = g - 2
                if there(n, DUOS):
                    after(act, s["probs_t"], n + 1)
                    after(act, s["mixed"], n - 1)
                    act.activation(pt[g_par(q)][:, :, :], t_ps[g_par(q)][:, :, :], ACT.Copy)\
                       .then_inc(s["probs_t_copied"], 1)
                if q == 0 and there(v, UNITS):
                    after(act, s["q_ps_ready"], v + 1)
                    after(act, s["q_spread"], v)
                    act.activation(q_sb[:, :], qn_ps[:, :], ACT.Identity, bias=bq[:, 0:1]).then_inc(s["q_ready"], 1)
                    after(act, s["q_norm_ps"], v)
                    act.activation(q_sq[:, :], qn_ps[:, :], ACT.Square, bias=bq[:, 0:1]).then_inc(s["q_sq_ready"], 1)
                    after(act, s["k_ps_ready"], v + 1)
                    after(act, s["k_spread"], v)
                    act.activation(k_sb[:, :], kn_ps[:, :], ACT.Identity, bias=bk[:, 0:1]).then_inc(s["k_ready"], 1)
                    after(act, s["k_norm_ps"], v)
                    act.activation(k_sq[:, :], kn_ps[:, :], ACT.Square, bias=bk[:, 0:1]).then_inc(s["k_sq_ready"], 1)
                if q == 0 and there(u - 2, UNITS):
                    after(act, s["var_ps_ready"], u - 1)
                    after(act, s["normed"], u - 2)
                    act.activation(rs[:, :], vv_ps[:, :], ACT.Ln, bias=eps[:, 0:1]).then_inc(s["var_ln"], 1)
                    act.wait_ge(s["var_ln"], u - 1)
                    act.activation(rs[:, :], rs[:, :], ACT.Exp, scale=-0.5).then_inc(s["rstd_ready"], 1)
                if q == 1 and there(v, UNITS):
                    after(act, s["q_norm_ps"], v + 1)
                    act.activation(rq[:, :], qn_ps[:, :], ACT.Ln, bias=eps[:, 1:2]).then_inc(s["q_ln"], 1)
                    after(act, s["k_norm_ps"], v + 1)
                    after(act, s["k_scaled"], v)
                    act.activation(rk[:, :], kn_ps[:, :], ACT.Ln, bias=eps[:, 1:2]).then_inc(s["k_ln"], 1)
                    act.wait_ge(s["q_ln"], v + 1)
                    act.activation(rq[:, :], rq[:, :], ACT.Exp, scale=-0.5).then_inc(s["q_rnorm"], 1)
                    act.wait_ge(s["k_ln"], v + 1)
                    act.activation(rk[:, :], rk[:, :], ACT.Exp, scale=-0.5).then_inc(s["k_rnorm"], 1)
                if q == 2 and there(v, UNITS):
                    after(act, s["k_scaled"], v + 1)
                    after(act, s["scores"], 4 * v - 4)
                    for h in range(HEADS):
                        last = act.activation(kx[jv][:, :, h], k_sb[:, :].rearrange("c (w k) -> c w k", k=TOK),
                                              ACT.Identity, scale=head_scale[:, h:h + 1])
                    last.then_inc(s["k_spread"], 1)
                if q == 2 and there(u - 1, UNITS):
                    after(act, s["mixed"], 4 * u)
                    after(act, s["proj_ps"], u - 1)
                    act.activation(ob[:, :], o_ps[:, :], ACT.Identity, bias=bv[:, 0:1]).then_inc(s["heads_copied"], 1)
                if q == 3 and there(v, UNITS):
                    after(act, s["xw_ready"], v + 2 if jv == 0 else v + 1)
                    act.activation(xu[:, v], xw[jv][:, :], ACT.Identity, bias=b1[:, 0:1]).then_inc(s["xw_saved"], 1)
                    after(act, s["v_ps_ready"], v + 1)
                    after(act, s["mixed"], 4 * v - 4)
                    vps = vv_ps[:, :].rearrange("c (t a d) -> c t a d", t=4, a=4)
                    for par in range(2):
                        for h2 in range(2):
                            last = act.activation(
                                vd[jv][64 * h2:64 * h2 + 64, par:WIN:2, :, DH * h2:DH * (h2 + 1)],
                                vps[64 * par:64 * par + 64, :, :, DH * h2:DH * (h2 + 1)], ACT.Copy)
                    last.then_inc(s["v_spread"], 1)
                if q == 3 and there(u - 1, UNITS):
                    after(act, s["proj_ps"], u)
                    after(act, s["normed"], u - 1)
                    act.activation(cc[:, :], qn_ps[:, :], ACT.Identity, bias=bp[:, 0:1])
                    after(act, s["var_ps_ready"], u - 1)
                    act.activation(csq[:, :], qn_ps[:, :], ACT.Square, bias=bp[:, 0:1]).then_inc(s["centred"], 1)

            def vector_slot(dve, u, j, q, g):
                v, jv = u + 1, 1 - j
                n = g - 1
                if there(g, DUOS):
                    kind = 2 * (j == 1 and q // 2 == 1) + q % 2
                    after(dve, s["scores"], g + 1)
                    after(dve, s["probs_t"], g - 3)
                    dve.tensor_tensor(sc[:, q], s_ps[g_par(q)][:, :, :, :], bias_tab[:, kind], ALU.add)\
                       .then_inc(s["biased"], 1)
                if there(n, DUOS):
                    after(dve, s["exped"], n + 1)
                    after(dve, s["row_recip"], n - 1)
                    dve.tensor_reduce(sm[:, (q - 1) % 2], sc[:, (q - 1) % 4].rearrange("c w h k -> c (w h) k"),
                                      X, ALU.add).then_inc(s["row_sum"], 1)
                if there(g, DUOS):
                    dve.wait_ge(s["biased"], g + 1)
                    after(dve, s["shifted"], g - 1)
                    dve.tensor_reduce(mx[:, q % 2], sc[:, q].rearrange("c w h k -> c (w h) k"), X, ALU.max)\
                       .then_inc(s["row_max"], 1)
                if there(n, DUOS):
                    dve.wait_ge(s["row_sum"], n + 1)
                    after(dve, s["probs"], n - 1)
                    dve.reciprocal(rs8[:, (q - 1) % 2], sm[:, (q - 1) % 2]).then_inc(s["row_recip"], 1)
                if q == 1 and there(v, UNITS):
                    after(dve, s["q_ready"], v + 1)
                    after(dve, s["q_rnorm"], v + 1)
                    after(dve, s["scores"], 4 * v - 4)
                    for a, (lo, hi) in enumerate(HALVES):
                        last = dve.tensor_tensor(qd[jv][lo:hi, :, a],
                                                 q_sb[lo:hi, :].rearrange("c (w k) -> c w k", k=TOK),
                                                 rq[lo:hi, :].rearrange("c (w k) -> c w k", k=TOK), ALU.mult)
                    last.then_inc(s["q_spread"], 1)
                    after(dve, s["k_sq_ready"], v + 1)
                    after(dve, s["k_rnorm"], v + 1)
                    dve.tensor_tensor(k_sb[:, :], k_sb[:, :], rk[:, :], ALU.mult).then_inc(s["k_scaled"], 1)
                if q == 1 and there(u - 2, UNITS):
                    after(dve, s["rstd_ready"], u - 1)
                    dve.tensor_tensor(cc[:, :], cc[:, :], rs[:, :], ALU.mult).then_inc(s["normed_a"], 1)
                    after(dve, s["xw_saved"], u - 1)
                    dve.wait_ge(s["normed_a"], u - 1)
                    dve.scalar_tensor_tensor(xu[:, u - 2], cc[:, :], g1[:, 0:1], xu[:, u - 2], ALU.mult, ALU.add)\
                       .then_inc(s["normed"], 1)
                if q == 2 and there(u + 2, UNITS):
                    after(dve, s["v_ps_ready"], u + 1)
                    after(dve, s["xw_saved"], u + 1)
                    pair = (u + 2) // 2 if isinstance(u, int) else (u - j) // 2 + 1
                    for pc in gather_pieces(j):
                        img, win = piece(xs[:, pair], xw[j][:, :], *pc)
                        last = dve.tensor_copy(win, img)
                    last.then_inc(s["xw_ready"], 1)

            def pool_slot(pool, u, j, q, g):
                if there(g, DUOS):
                    after(pool, s["row_max"], g + 1)
                    t = sc[:, q].rearrange("c w h k -> c (w h) k")
                    pool.tensor_tensor(t, t, mx[:, q % 2].unsqueeze(2).broadcast_to([128, 2 * HEADS, TOK]),
                                       ALU.subtract).then_inc(s["shifted"], 1)
                n = g - 1
                if there(n, DUOS):
                    after(pool, s["row_recip"], n + 1)
                    t = sc[:, (q - 1) % 4].rearrange("c w h k -> c (w h) k")
                    pool.tensor_tensor(t, t, rs8[:, (q - 1) % 2].unsqueeze(2).broadcast_to([128, 2 * HEADS, TOK]),
                                       ALU.mult).then_inc(s["probs"], 1)

            s["normed_a"] = sem(stage, "normed_a")

            with nc.Block() as block:
                @block.tensor
                def _(pe):
                    pe.wait_ge(zero, 2)
                    units(pe, tensor_slot)

                @block.scalar
                def _(act):
                    act.preload_act_table_set(EXP_LN)
                    act.wait_ge(zero, 2)
                    units(act, scalar_slot)

                @block.vector
                def _(dve):
                    dve.memset(qd[0][:, :, :, :], 0.0)
                    dve.memset(qd[1][:, :, :, :], 0.0).then_inc(zero, 1)
                    dve.wait_ge(zero, 2)
                    units(dve, vector_slot)

                @block.gpsimd
                def _(pool):
                    pool.memset(vd[0][:, :, :, :], 0.0)
                    pool.memset(vd[1][:, :, :, :], 0.0).then_inc(zero, 1)
                    units(pool, pool_slot)
        attention.close()

        x1 = sb(whole, "x1", [128, PAIRS, PIX])
        with ExitStack() as stage:
            s = {k: sem(stage, "f_" + k) for k in (
                "w_in", "chain", "zero", "hid_ps", "gelu", "out_ps", "centred", "var_ps", "ln", "rstd", "normed",
                "update", "skipped", "b2_mean", "x_biased", "done")}
            x_back = [sem(stage, f"x_back{k}") for k in range(2)]
            fw1 = sb(stage, "fw1", [128, 4, 128])
            fw2 = sb(stage, "fw2", [128, 4, 128])
            fw2_in = sb(stage, "fw2_in", [128, 4, C])
            fsum = sb(stage, "fsum", [128, 4, 2])
            fb1 = sb(stage, "fb1", [128, 4])
            fb2 = sb(stage, "fb2", [128, 2])
            g2, b2 = sb(stage, "g2", [128, 1]), sb(stage, "b2", [128, 1])
            hs = sb(stage, "hs", [128, 2, 4, COLS])
            cc = sb(stage, "fcc", [128, 4, COLS])
            csq = sb(stage, "fcsq", [128, 2, COLS])
            rs = sb(stage, "frs", [128, 2, COLS])
            upd = sb(stage, "upd", [128, 2, COLS])
            xr = sb(stage, "xr", [128, 2, PIX])
            h_ps = [ps(stage, f"h_ps{m}", [128, COLS]) for m in range(4)]
            c_ps = [ps(stage, f"c_ps{m}", [128, COLS]) for m in range(2)]
            v_ps = [ps(stage, f"v_ps{m}", [128, COLS]) for m in range(2)]

            loads = []
            for a, (lo, hi) in enumerate(HALVES):
                loads += [(fw1[lo:hi, :, lo:hi], ffn_w1.rearrange("c (m h) -> c m h", m=4)),
                          (fw2_in[lo:hi, :, :], ffn_w2.rearrange("(m h) c -> h m c", m=4)),
                          (fb1[lo:hi, :], ffn_b1),
                          (fb2[lo:hi, 0:1], column(ffn_b2)), (g2[lo:hi, :], column(ln2_g)),
                          (b2[lo:hi, :], column(ln2_b))]

            def steps(eng, step):
                def four(i):
                    for k in range(4):
                        step(eng, 4 * i + k, k)
                four(0)
                with eng.Fori(1, UNITS // 4 - 1) as i:
                    four(i)
                four(UNITS // 4 - 1)
                four(UNITS // 4)

            def tensor_step(pe, u, k):
                if there(u, UNITS):
                    for m in range(4):
                        after(pe, s["gelu"], 4 * u - 3 + m)
                        pe.matmul(h_ps[m][:, :], fw1[:, m], xu[:, u], start=True, stop=True).then_inc(s["hid_ps"], 1)
                if there(u - 1, UNITS):
                    after(pe, s["centred"], u - 2)
                    for m in range(4):
                        after(pe, s["gelu"], 4 * u - 3 + m)
                        last = pe.matmul(c_ps[(k - 1) % 2][:, :], fw2[:, m], hs[:, (k - 1) % 2, m],
                                         start=(m == 0), stop=(m == 3))
                    last.then_inc(s["out_ps"], 1)
                if there(u - 2, UNITS):
                    after(pe, s["centred"], u - 1)
                    after(pe, s["ln"], u - 3)
                    pe.matmul(v_ps[k % 2][:, :], mean_image[:, :], csq[:, k % 2], start=True, stop=True)\
                      .then_inc(s["var_ps"], 1)

            def scalar_step(act, u, k):
                if there(u, UNITS):
                    for m in range(4):
                        after(act, s["hid_ps"], 4 * u + m + 1)
                        after(act, s["out_ps"], u - 1)
                        act.activation(hs[:, k % 2, m], h_ps[m][:, :], ACT.Gelu, bias=fb1[:, m:m + 1])\
                           .then_inc(s["gelu"], 1)
                if there(u - 1, UNITS):
                    after(act, s["out_ps"], u)
                    after(act, s["update"], u - 4)
                    act.activation(cc[:, (k - 1) % 4], c_ps[(k - 1) % 2][:, :], ACT.Identity, bias=fb2[:, 0:1])
                    after(act, s["var_ps"], u - 2)
                    act.activation(csq[:, (k - 1) % 2], c_ps[(k - 1) % 2][:, :], ACT.Square, bias=fb2[:, 0:1])\
                       .then_inc(s["centred"], 1)
                if k % 2 == 1 and there(u - 3, UNITS):
                    act.preload_act_table_set(EXP_LN)
                    for d in (3, 2):
                        after(act, s["var_ps"], u - d + 1)
                        after(act, s["normed"], u - d - 1)
                        act.activation(rs[:, (k - d) % 2], v_ps[(k - d) % 2][:, :], ACT.Ln, bias=eps[:, 0:1])\
                           .then_inc(s["ln"], 1)
                    for d in (3, 2):
                        act.wait_ge(s["ln"], u - d + 1)
                        act.activation(rs[:, (k - d) % 2], rs[:, (k - d) % 2], ACT.Exp, scale=-0.5)\
                           .then_inc(s["rstd"], 1)

            def vector_step(dve, u, k):
                if k % 2 == 1 and there(u - 3, UNITS):
                    for d in (3, 2):
                        after(dve, s["rstd"], u - d + 1)
                        dve.tensor_tensor(cc[:, (k - d) % 4], cc[:, (k - d) % 4], rs[:, (k - d) % 2], ALU.mult)\
                           .then_inc(s["normed"], 1)
                    for d in (3, 2):
                        dve.wait_ge(s["normed"], u - d + 1)
                        after(dve, s["skipped"], u - d - 1)
                        dve.scalar_tensor_tensor(upd[:, (k - d) % 2], cc[:, (k - d) % 4], g2[:, 0:1], xu[:, u - d],
                                                 ALU.mult, ALU.add).then_inc(s["update"], 1)
                    pair = (u - 3) // 2 if isinstance(u, int) else (u - k) // 2 + (k - 3) // 2
                    kp = ((k - 3) // 2) % 2
                    for d in (3, 2):
                        j = 3 - d
                        if j == 0:
                            after(dve, s["x_biased"], pair + 1)
                        dve.wait_ge(s["update"], u - d + 1)
                        for pc in gather_pieces(j):
                            img, win = piece(xr[:, kp], upd[:, (k - d) % 2], *pc)
                            dst, _ = piece(x1[:, pair], upd[:, (k - d) % 2], *pc)
                            last = dve.tensor_tensor(dst, img, win, ALU.add)
                        last.then_inc(s["skipped"], 1)

            def sync_pair(sp, p, k):
                after(sp, s["skipped"], 2 * p - 2)
                for a, (lo, hi) in enumerate(HALVES):
                    sp.dma_start(xr[lo:hi, k], x_pairs[a, :, p]).then_inc(x_back[k], 16)

            def pool_pair(pool, i, k):
                after(pool, x_back[k], 32 * (i + 1))
                pool.tensor_tensor(xr[:, k], xr[:, k], b2[:, 0:1].broadcast_to([128, PIX]), ALU.add).then_inc(s["x_biased"], 1)

            def in_pairs(eng, step, n=PAIRS // 2):
                step(0)
                with eng.Fori(1, n) as i:
                    step(i)

            with nc.Block() as block:
                @block.sync
                def _(sp):
                    sp.wait_ge(s["zero"], 2)
                    for dst, src in loads:
                        sp.dma_start(dst, src).then_inc(s["w_in"], 16)
                    in_pairs(sp, lambda i: (sync_pair(sp, 2 * i, 0), sync_pair(sp, 2 * i + 1, 1)))

                @block.gpsimd
                def _(pool):
                    pool.memset(fw1[:, :, :], 0.0).then_inc(s["zero"], 1)
                    pool.memset(fw2[:, :, :], 0.0).then_inc(s["zero"], 1)
                    pool.wait_ge(s["w_in"], 16 * len(loads))
                    in_pairs(pool, lambda i: (pool_pair(pool, i, 0), pool_pair(pool, i, 1)))

                @block.vector
                def _(dve):
                    links = [0]

                    def link(ins):
                        links[0] += 1
                        ins.then_inc(s["chain"], 1)
                        dve.wait_ge(s["chain"], links[0])

                    dve.wait_ge(s["w_in"], 16 * len(loads))
                    link(dve.tensor_reduce(fsum[:, :, 0], fw2_in[:, :, :], X, ALU.add))
                    link(dve.tensor_scalar(fsum[:, :, 1], fsum[:, :, 0], -1.0 / C, None, ALU.mult))
                    for lo, hi in HALVES:
                        link(dve.tensor_tensor(fw2[lo:hi, :, lo:hi], fw2_in[lo:hi, :, :],
                                               fsum[lo:hi, :, 1].unsqueeze(2).broadcast_to([64, 4, C]), ALU.add))
                    dve.wait_ge(s["b2_mean"], 1)
                    link(dve.tensor_tensor(fb2[:, 0:1], fb2[:, 0:1], c_ps[0][:, 0:1], ALU.subtract))
                    steps(dve, vector_step)

                @block.tensor
                def _(pe):
                    pe.wait_ge(s["w_in"], 16 * len(loads))
                    pe.matmul(c_ps[0][:, 0:1], mean_image[:, :], fb2[:, 0:1], start=True, stop=True)\
                      .then_inc(s["b2_mean"], 1)
                    pe.wait_ge(s["chain"], 5)
                    steps(pe, tensor_step)

                @block.scalar
                def _(act):
                    act.wait_ge(s["w_in"], 16 * len(loads))
                    act.wait_ge(s["chain"], 5)
                    steps(act, scalar_step)

        ys = xs
        yt = xs[:, :, :].rearrange("c p (g n) -> c p g n", g=8)
        scores = sb(whole, "scores_sb", [128, PAIRS, 8, 2])
        with ExitStack() as stage:
            s = {k: sem(stage, "y_" + k) for k in ("w_in", "zero", "turned", "turn_copied", "scored", "score_copied")}
            cw = sb(stage, "cw", [128, 8, 2, 2])
            cw_in = sb(stage, "cw_in", [128, BLOCKS])
            ynow = sb(stage, "ynow", [128, 2, PIX])
            turn_ps = [ps(stage, f"turn_ps{k}", [128, 4, 128]) for k in range(2)]
            score_ps = ps(stage, "score_ps", [128, COLS])
            n2, gn_run, gn_v, gn_t, gn_a, gn_p, rstd2 = group_norm(stage, "gn2", x1, ys, lambda eng, p, k: None)
            tail_ps = score_ps[:, 0:32 * 2].rearrange("c (k n) -> c k n", k=2)

            def blocks(k, gp):
                return ynow[:, k, 128 * gp:128 * (gp + 1)]

            def pool_scale(pool, p, k):
                after(pool, n2["rstd"], p + 1)
                after(pool, n2["square"], p + 1)
                after(pool, s["scored"], p - 1)
                shape = [128, 4, WS, WS]
                for gy in range(4):
                    last = pool.tensor_tensor(
                        ynow[:, k].rearrange("c (y x h w) -> c y x h w", y=4, x=4, h=WS)[:, gy],
                        ys[:, p].rearrange("c (y h x w) -> c y x h w", y=4, x=4, h=WS)[:, gy],
                        rstd2[:, k].rearrange("c (x w) -> c x w", x=4).unsqueeze(2).broadcast_to(shape), ALU.mult)
                last.then_inc(n2["normed"], 1)

            def tensor_turn(pe, p, k):
                gn_t(pe, p, k)
                m, km = p - 2, k
                if not there(m, PAIRS):
                    return
                after(pe, n2["normed"], m + 1)
                for half in range(2):
                    after(pe, s["turn_copied"], 2 * m - 1 + half)
                    for b in range(4):
                        last = pe.transpose(turn_ps[half][:, b], blocks(km, 4 * half + b), ident[:, :])
                    last.then_inc(s["turned"], 1)
                after(pe, s["score_copied"], m)
                for gp in range(8):
                    last = pe.matmul(tail_ps[:, 0, 4 * gp:4 * gp + 4], blocks(km, gp),
                                     cw[:, gp].rearrange("c b a -> c (b a)"), start=True, stop=True)
                last.then_inc(s["scored"], 1)

            def scalar_turn(act, p, k):
                gn_a(act, p, k)
                m = p - 2
                if not there(m, PAIRS):
                    return
                for half in range(2):
                    after(act, s["turned"], 2 * m + 1 + half)
                    act.activation(yt[:, m, 4 * half:4 * half + 4], turn_ps[half][:, :, :], ACT.Copy)\
                       .then_inc(s["turn_copied"], 1)

            def vector_turn(dve, p, k):
                gn_v(dve, p, k)
                m = p - 2
                if not there(m, PAIRS):
                    return
                after(dve, s["scored"], m + 1)
                for b, (lo, hi) in enumerate(HALVES):
                    last = dve.tensor_copy(scores[lo:hi, m],
                                           tail_ps[lo:hi, 0].rearrange("c (g b a) -> c b g a", b=2, a=2)[:, b])
                last.then_inc(s["score_copied"], 1)

            def turns(eng, step):
                for p in range(4):
                    step(eng, p, p % 2)
                with eng.Fori(2, PAIRS // 2) as i:
                    step(eng, 2 * i, 0)
                    step(eng, 2 * i + 1, 1)
                step(eng, PAIRS, 0)
                step(eng, PAIRS + 1, 1)

            with nc.Block() as block:
                @block.sync
                def _(sp):
                    for lo, hi in HALVES:
                        sp.dma_start(cw_in[lo:hi, :], conv_w).then_inc(s["w_in"], 16)

                @block.gpsimd
                def _(pool):
                    pool.memset(cw[:, :, :, :], 0.0).then_inc(s["zero"], 1)
                    pool.wait_ge(s["zero"], 1)
                    pool.wait_ge(s["w_in"], 32)
                    for a, (lo, hi) in enumerate(HALVES):
                        last = pool.tensor_copy(cw[lo:hi].rearrange("c g b a -> c (g b) a")[:, :, a], cw_in[lo:hi, :])
                    last.then_inc(s["zero"], 1)
                    pool_scale(pool, 0, 0)
                    pool_scale(pool, 1, 1)
                    with pool.Fori(1, PAIRS // 2) as i:
                        pool_scale(pool, 2 * i, 0)
                        pool_scale(pool, 2 * i + 1, 1)

                @block.vector
                def _(dve):
                    turns(dve, vector_turn)

                @block.scalar
                def _(act):
                    act.preload_act_table_set(EXP_LN)
                    turns(act, scalar_turn)

                @block.tensor
                def _(pe):
                    pe.wait_ge(s["zero"], 2)
                    turns(pe, tensor_turn)

        with ExitStack() as stage:
            s = {k: sem(stage, "t_" + k) for k in (
                "w_in", "rows", "exped", "pick", "zero", "picked_t", "picked_copied", "st_t", "st_copied", "gathered",
                "feat", "hid_ps", "hid", "rec_ps", "rec", "rec_out", "mixed", "added", "stored")}
            rec_in = sem(stage, "rec_in")
            w1 = sb(stage, "w1", [128, TOP, INDIM])
            w1s = sb(stage, "w1s", [128, INDIM])
            w2 = sb(stage, "w2", [MT, 4, OUTDIM])
            mb = sb(stage, "mb", [MT, 4])
            mb2r = sb(stage, "mb2r", [1, OUTDIM])
            one = sb(stage, "one", [1, 128])
            ow = sb(stage, "ow", [2 * OC, 128])
            iota = sb(stage, "iota", [128, TOK])
            e = sb(stage, "e", [128, 4, TOK])
            pr, st, cm, oh = (sb(stage, n, [128, 4, TOK]) for n in ("pr", "st", "cm", "oh"))
            esum = sb(stage, "esum", [128, 4])
            top = sb(stage, "top", [128, 4, 8])
            tidx = sb(stage, "tidx", [128, 4, 8], U32)
            tidf = sb(stage, "tidf", [128, 4, 8])
            zeros = sb(stage, "zeros", [128, TOK])
            sel = sb(stage, "sel", [128, TOP, 4, TOK])
            r = sb(stage, "r", [128, 2, 2, TOP, 128])
            st_t = sb(stage, "st_t", [128, 2, 256])
            feat = sb(stage, "feat", [128, TOP, 256])
            hid = sb(stage, "mlp_hid", [MT, 4, COLS])
            rec = sb(stage, "rec_sb", [128, 4, OUTDIM])
            grid = yt[0:2 * OC, :, :, :].rearrange("o p g n -> o p (g n)")
            psb = [ps(stage, f"bank{k}", [128, COLS]) for k in range(8)]

            loads = [(w2[:, :, :], mlp_w2.rearrange("(m k) n -> k m n", k=MT)),
                     (mb[:, :], mlp_b1),
                     (mb2r[:, :], mlp_b2.rearrange("(a n) -> a n", a=1)),
                     (iota[:, :], c_iota)]
            for a, (lo, hi) in enumerate(HALVES):
                loads += [(w1[lo:hi, :, :], mlp_w1[0:TOP * C].rearrange("(s c) n -> c s n", c=C)),
                          (w1s[lo:hi, :], mlp_w1[TOP * C:INDIM]),
                          (ow[OC * a:OC * (a + 1), lo:hi], out_w)]
            PROJ = 3

            with nc.Block() as block:
                @block.sync
                def _(sp):
                    sp.wait_ge(s["zero"], 3)
                    for dst, src in loads:
                        sp.dma_start(dst, src).then_inc(s["w_in"], 16)
                    for t in range(4):
                        sp.wait_ge(s["rec"], t + 1)
                        sp.dma_start(rec_dram[128 * t:128 * (t + 1), :], rec[:, t]).then_inc(s["rec_out"], 16)
                    sp.wait_ge(s["rec_out"], 64)
                    sp.wait_ge(s["gathered"], 8)
                    for a in range(2):
                        sp.dma_start(grid[OC * a:OC * (a + 1)].rearrange("o p (g l) -> o (p g) l", l=TOK),
                                     rec_dram[256 * a:256 * (a + 1)].rearrange("r (o l) -> o r l", l=TOK))\
                          .then_inc(rec_in, 16)
                    out_pairs = out.rearrange("(a p) c h w -> a c p (h w)", a=2)

                    def store(p):
                        sp.wait_ge(s["added"], 2 * p + 2)
                        for a, (lo, hi) in enumerate(HALVES):
                            sp.dma_start(out_pairs[a, :, p], x1[lo:hi, p]).then_inc(s["stored"], 16)
                    store(0)
                    with sp.Fori(1, PAIRS) as p:
                        store(p)
                    sp.wait_ge(s["stored"], 32 * PAIRS)

                @block.gpsimd
                def _(pool):
                    pool.memset(ow[:, :], 0.0).then_inc(s["zero"], 1)
                    pool.memset(one[:, :], 1.0).then_inc(s["zero"], 1)
                    pool.memset(st_t[:, :, :], 0.0)
                    pool.memset(r[:, :, :, :, :], 0.0).then_inc(s["zero"], 1)

                @block.vector
                def _(dve):
                    links = [0]

                    def link(ins):
                        links[0] += 1
                        ins.then_inc(s["pick"], 1)
                        dve.wait_ge(s["pick"], links[0])

                    dve.memset(zeros[:, :], 0.0)
                    dve.wait_ge(s["zero"], 3)
                    dve.wait_ge(s["exped"], 2)
                    dve.wait_ge(s["w_in"], 16 * len(loads))
                    full = [128, 4, TOK]
                    link(dve.tensor_reduce(esum[:, :], e[:, :, :], X, ALU.add))
                    link(dve.reciprocal(esum[:, :], esum[:, :]))
                    link(dve.tensor_tensor(pr[:, :, :], e[:, :, :], esum[:, :].unsqueeze(2).broadcast_to(full), ALU.mult))
                    for t in range(4):
                        last = dve.max(top[:, t], pr[:, t])
                    link(last)
                    for t in range(4):
                        last = dve.max_index(tidx[:, t], top[:, t], pr[:, t])
                    link(last)
                    link(dve.tensor_copy(tidf[:, :, :], tidx[:, :, :]))
                    positions = iota[:, :].unsqueeze(1).broadcast_to(full)
                    for k in range(TOP):
                        one_hot = tidf[:, :, k:k + 1].broadcast_to(full)
                        if k == 0:
                            link(dve.tensor_tensor(st[:, :, :], positions, one_hot, ALU.is_equal))
                        else:
                            link(dve.tensor_tensor(oh[:, :, :], positions, one_hot, ALU.is_equal))
                            link(dve.tensor_tensor(st[:, :, :], st[:, :, :], oh[:, :, :], ALU.add))
                    for t in range(4):
                        last = dve.tensor_tensor_scan(cm[:, t], st[:, t], zeros[:, :], 0.0, ALU.add, ALU.add)
                    link(last)
                    link(dve.tensor_tensor(cm[:, :, :], cm[:, :, :], st[:, :, :], ALU.mult))
                    link(dve.tensor_tensor(st[:, :, :], st[:, :, :], pr[:, :, :], ALU.subtract))
                    link(dve.tensor_tensor(st[:, :, :], st[:, :, :], pr[:, :, :], ALU.add))
                    for k in range(TOP):
                        last = dve.scalar_tensor_tensor(sel[:, k].rearrange("c t l -> c (t l)"),
                                                        cm[:, :, :].rearrange("c t l -> c (t l)"), float(k + 1),
                                                        st[:, :, :].rearrange("c t l -> c (t l)"),
                                                        ALU.is_equal, ALU.mult)
                    link(last)
                    assert links[0] == N_PICK
                    for t in range(2):
                        for half in range(2):
                            n = 2 * t + half
                            dve.wait_ge(s["picked_t"], n + 1)
                            for b, (lo, hi) in enumerate(HALVES):
                                last = dve.tensor_copy(
                                    r[lo:hi, t, b, 3 * half:3 * half + 3],
                                    psb[n % 2][lo:hi, 0:384].rearrange("c (s n) -> c s n", s=3))
                            last.then_inc(s["picked_copied"], 1)
                    dve.wait_ge(s["st_t"], 1)
                    for b, (lo, hi) in enumerate(HALVES):
                        last = dve.tensor_copy(st_t[lo:hi].rearrange("c a (n b) -> c a n b", b=2)[:, :, :, b],
                                               psb[2][lo:hi, 0:256].rearrange("c (n a) -> c a n", a=2))
                    last.then_inc(s["st_copied"], 1)
                    for n in range(8):
                        dve.wait_ge(s["gathered"], n + 1)
                        for a, (lo, hi) in enumerate(HALVES):
                            last = dve.tensor_copy(
                                feat[lo:hi, :, 32 * n:32 * (n + 1)].rearrange("c s (m b) -> c m b s", b=2),
                                psb[PROJ + n % 4][lo:hi, 0:384].rearrange("c (m b s a) -> c a m b s", b=2, s=TOP, a=2)[:, a])
                        last.then_inc(s["feat"], 1)
                    for t in range(4):
                        dve.wait_ge(s["rec_ps"], t + 1)
                        dve.tensor_copy(rec[:, t], psb[t % 2][:, 0:OUTDIM]).then_inc(s["rec"], 1)

                    def add(p):
                        for half in range(2):
                            dve.wait_ge(s["mixed"], 2 * p + half + 1)
                            v = x1[:, p, COLS * half:COLS * (half + 1)]
                            dve.tensor_tensor(v, v, psb[4 + half][:, :], ALU.add).then_inc(s["added"], 1)
                    add(0)
                    with dve.Fori(1, PAIRS) as p:
                        add(p)

                @block.scalar
                def _(act):
                    act.preload_act_table_set(EXP_LN)
                    for t in range(2):
                        act.wait_ge(s["rows"], t + 1)
                        act.activation(e[:, 2 * t:2 * t + 2], psb[t][:, 0:128].rearrange("c (b l) -> c b l", b=2),
                                       ACT.Exp).then_inc(s["exped"], 1)
                    act.wait_ge(s["w_in"], 16 * len(loads))
                    for m in range(4):
                        for a in range(2):
                            act.wait_ge(s["hid_ps"], 2 * m + a + 1)
                            act.activation(hid[:, m, 256 * a:256 * (a + 1)], psb[4 * a + m][0:MT, 0:256], ACT.Relu,
                                           bias=mb[:, m:m + 1]).then_inc(s["hid"], 1)

                @block.tensor
                def _(pe):
                    for t in range(2):
                        pe.transpose(psb[t][:, 0:128], scores[:, 8 * t:8 * t + 8].rearrange("c p g a -> c (p g a)"),
                                     ident[:, :]).then_inc(s["rows"], 1)
                    pe.wait_ge(s["pick"], N_PICK)
                    pe.wait_ge(s["exped"], 2)
                    for t in range(2):
                        for half in range(2):
                            n = 2 * t + half
                            if n >= 2:
                                pe.wait_ge(s["picked_copied"], n - 1)
                            for k in range(3):
                                last = pe.transpose(psb[n % 2][:, 128 * k:128 * (k + 1)],
                                                    sel[:, 3 * half + k, 2 * t:2 * t + 2].rearrange("c b l -> c (b l)"),
                                                    ident[:, :])
                            last.then_inc(s["picked_t"], 1)
                    for t in range(2):
                        last = pe.transpose(psb[2][:, 128 * t:128 * (t + 1)],
                                            st[:, 2 * t:2 * t + 2].rearrange("c b l -> c (b l)"), ident[:, :])
                    last.then_inc(s["st_t"], 1)
                    pe.wait_ge(s["picked_copied"], 4)
                    pe.wait_ge(s["zero"], 3)
                    for n in range(8):
                        if n >= 4:
                            pe.wait_ge(s["feat"], n - 3)
                        for m in range(16):
                            p, gp = 2 * n + m // 8, m % 8
                            row = 16 * (p % 8) + 2 * gp
                            last = pe.matmul(psb[PROJ + n % 4][:, 24 * m:24 * (m + 1)], yt[:, p, gp],
                                             r[:, p // 8, :, :, row:row + 2], start=True, stop=True)
                        last.then_inc(s["gathered"], 1)
                    pe.wait_ge(s["feat"], 8)
                    pe.wait_ge(s["st_copied"], 1)
                    pe.wait_ge(s["w_in"], 16 * len(loads))
                    for m in range(4):
                        cols = slice(MT * m, MT * (m + 1))
                        for k in range(TOP):
                            for a, (lo, hi) in enumerate(HALVES):
                                pe.matmul(psb[4 * a + m][0:MT, 0:256], w1[lo:hi, k, cols], feat[lo:hi, k],
                                          start=(k == 0), stop=False)
                        for a in range(2):
                            pe.matmul(psb[4 * a + m][0:MT, 0:256], w1s[:, cols], st_t[:, a],
                                      start=False, stop=True).then_inc(s["hid_ps"], 1)
                    pe.wait_ge(s["hid"], 8)
                    for t in range(4):
                        if t >= 2:
                            pe.wait_ge(s["rec"], t - 1)
                        for m in range(4):
                            pe.matmul(psb[t % 2][:, 0:OUTDIM], hid[:, m, 128 * t:128 * (t + 1)], w2[:, m],
                                      start=(m == 0), stop=False)
                        pe.matmul(psb[t % 2][:, 0:OUTDIM], one[:, :], mb2r[:, :], start=False, stop=True)\
                          .then_inc(s["rec_ps"], 1)
                    pe.wait_ge(rec_in, 32)

                    def mix(p):
                        for half in range(2):
                            after(pe, s["added"], 2 * p - 1 + half)
                            for y in range(2):
                                blk = grid[:, p].rearrange("o (y x h w) -> o y h x w", y=4, x=4, h=8)[:, 2 * half + y]
                                last = pe.matmul(psb[4 + half][:, 256 * y:256 * (y + 1)], ow[:, :], blk,
                                                 start=True, stop=True)
                            last.then_inc(s["mixed"], 1)
                    mix(0)
                    with pe.Fori(1, PAIRS) as p:
                        mix(p)


N_PICK = 3 + 1 + 1 + 1 + (1 + 2 * (TOP - 1)) + 1 + 3 + 1


def shape_constants():
    rows = np.arange(128)
    ident = np.eye(128, dtype=np.float32)
    head = (rows[:, None] // DH == rows[None, :] // DH).astype(np.float32)
    image = (rows[:, None] // C == rows[None, :] // C).astype(np.float32)
    delta = ((rows[:, None] % C) // DH == np.arange(HEADS)[None, :]).astype(np.float32)
    at = np.arange(WS)
    coords = np.stack(np.meshgrid(at, at, indexing="ij"), 0).reshape(2, -1)
    rel = (coords[:, :, None] - coords[:, None, :]).reshape(2, -1).astype(np.float32)
    rel = (np.sign(rel) * np.log1p(np.abs(rel))).astype(np.float32)
    mask = np.zeros((128, 4, 2, TOK), np.float32)
    for kind in range(4):
        for w in range(2):
            low = kind // 2 == 1
            right = kind % 2 == 1 and w == 1
            ty, tx = np.arange(TOK) // WS, np.arange(TOK) % WS
            region = 2 * (low & (ty >= WS - SHIFT)) + (right & (tx >= WS - SHIFT))
            differ = region[:, None] != region[None, :]
            mask[:, kind, w] = np.tile(np.where(differ, -100.0, 0.0), (2, 1))
    iota = np.tile(np.arange(TOK, dtype=np.float32), (128, 1))
    return {"c_ident": ident, "c_head": head, "c_image": image, "c_delta": delta, "c_rel": rel,
            "c_mask": mask, "c_iota": iota}


_L0 = ["qkv_w", "qkv_b", "proj_w", "proj_b", "meta_w1", "meta_b1", "meta_w2", "meta_b2", "tau", "ln1_g", "ln1_b",
       "ln2_g", "ln2_b", "ffn_w1", "ffn_b1", "ffn_w2", "ffn_b2"]
_L1 = ["conv_w", "W1", "b1", "W2", "b2", "out_w"]
_INS = ["x"] + [f"L0_conv_{n}" for n in _L0] + [f"L1_conv_{n}" for n in _L1]


def kernel(**inputs):
    import concourse.bacc as _bacc
    from concourse.bass_utils import run_bass_kernel_spmd as _run

    nc = _bacc.Bacc("TRN2", target_bir_lowering=False, num_devices=1)
    arrays, args = {}, []
    given = {name: np.asarray(inputs[name]) for name in _INS}
    given["L0_conv_ffn_b1"] = given["L0_conv_ffn_b1"].reshape(4, 64).T
    given["L1_conv_b1"] = given["L1_conv_b1"].reshape(4, MT).T
    given["L1_conv_conv_w"] = given["L1_conv_conv_w"].T
    given["L1_conv_out_w"] = given["L1_conv_out_w"].T
    given = {name: np.ascontiguousarray(a) for name, a in given.items()}
    for name, a in (given | shape_constants()).items():
        arrays[f"in_{name}_dram"] = a
        args.append(nc.dram_tensor(f"in_{name}_dram", a.shape, mybir.dt.from_np(a.dtype), kind="ExternalInput").ap())
    args.append(nc.dram_tensor("rec_scratch", (512, OUTDIM), F32, kind="Internal").ap())
    args.append(nc.dram_tensor("out_0_dram", (B, C, H, W), F32, kind="ExternalOutput").ap())
    build(nc, *args)
    r = _run(nc, [arrays], core_ids=[0])
    return r.results[0]["out_0_dram"]
```

```python
from contextlib import ExitStack

import numpy as np

import concourse.bass as bass
from concourse import mybir

F32 = mybir.dt.float32
U32 = mybir.dt.uint32
ALU = mybir.AluOpType
ACT = mybir.ActivationFunctionType
X = mybir.AxisListType.X

B, C, H, W = 32, 64, 32, 32
PAIRS = B // 2
PIX = H * W
WS, SHIFT, HEADS = 8, 4, 4
DH = C // HEADS
TOK = WS * WS
UNITS = 2 * PAIRS
COLS = 512
WIN = 8
DUOS = 4 * UNITS
FFN = 4 * C
META = 128
NORM_FLOOR = 1e-18
HALVES = ((0, 64), (64, 128))
ACT_HEADS, POOL_HEADS = range(0, 3), range(3, 4)
EXP_LN = "natural_log_exp_and_others"

BLOCKS = 16
TOP = 6
OC = C // 10 + 1
INDIM = TOP * C + TOK
MT = INDIM // 4
OUTDIM = TOK * OC


def after(eng, sem, count, limit=None):
    if isinstance(count, int):
        if limit is not None:
            count = min(count, limit)
        if count <= 0:
            return
    eng.wait_ge(sem, count)


def there(index, limit):
    return not isinstance(index, int) or 0 <= index < limit


def build(nc, x, qkv_w, proj_w, meta_w1, meta_b1, meta_w2, meta_b2, tau, ffn_w1, ffn_b1, ffn_w2,
          conv_w, mlp_w1, mlp_b1, mlp_w2, mlp_b2, out_w, c_vecs, c_consts, c_rel, c_mask, c_iota,
          rec_dram, bias_dram, out):
    with ExitStack() as whole:
        def sb(stack, name, shape, dt=F32):
            return stack.enter_context(nc.sbuf_tensor(name, shape, dt))

        def ps(stack, name, shape):
            return stack.enter_context(nc.psum_tensor(name, shape, F32))

        def sem(stack, name):
            return stack.enter_context(nc.semaphore(name))

        xs = sb(whole, "xs", [128, PAIRS, PIX])
        consts = sb(whole, "consts", [128, 3 * 128 + HEADS])
        ident, sum_head, sum_image = (consts[:, 128 * n:128 * (n + 1)] for n in range(3))
        delta = consts[:, 3 * 128:]
        vecs = sb(whole, "vecs", [128, 9])
        bq, bk, bv, proj_bias, g1, b1, g2, b2, ffn_bias = (vecs[:, n:n + 1] for n in range(9))
        mean_image = sb(whole, "mean_image_sb", [128, 128])[:, :]
        mean_group = sb(whole, "mean_group", [128, 128])

        def group_norm(stage, tag, src, dst, arrive, copy_out=None):
            n = {k: sem(stage, f"{tag}_{k}") for k in
                 ("rowsum", "mean", "centred", "square", "sqsum", "var", "ln", "rstd", "normed")}
            rowsum = sb(stage, f"{tag}_rowsum_sb", [128, 2, W])
            sqsum = sb(stage, f"{tag}_sqsum_sb", [128, 2, W])
            lnvar = sb(stage, f"{tag}_lnvar_sb", [128, 2, W])
            rstd = sb(stage, f"{tag}_rstd_sb", [128, 2, W])
            square = sb(stage, f"{tag}_square_sb", [128, 2, PIX])
            mean_ps = [ps(stage, f"{tag}_mean_ps{k}", [128, COLS]) for k in range(2)]
            var_ps = [ps(stage, f"{tag}_var_ps{k}", [128, COLS]) for k in range(2)]

            def columns(a):
                return a.rearrange("c (h w) -> c w h", w=W)

            def vector(eng, p, k):
                if there(p + 1, PAIRS):
                    arrive(eng, p + 1, 1 - k)
                    after(eng, n["mean"], p)
                    eng.tensor_reduce(rowsum[:, 1 - k], columns(src[:, p + 1]), X, ALU.add)\
                       .then_inc(n["rowsum"], 1)
                if there(p - 1, PAIRS):
                    after(eng, n["square"], p)
                    after(eng, n["var"], p - 2)
                    eng.tensor_reduce(sqsum[:, 1 - k], columns(square[:, 1 - k]), X, ALU.add)\
                       .then_inc(n["sqsum"], 1)
                if there(p, PAIRS):
                    after(eng, n["mean"], p + 1)
                    eng.tensor_tensor(
                        dst[:, p].rearrange("c (h w) -> c h w", w=W),
                        src[:, p].rearrange("c (h w) -> c h w", w=W),
                        mean_ps[k][:, 0:W].unsqueeze(1).broadcast_to([128, H, W]),
                        ALU.subtract).then_inc(n["centred"], 1)

            def tensor(eng, p, k):
                if there(p + 1, PAIRS):
                    after(eng, n["rowsum"], p + 2)
                    after(eng, n["centred"], p)
                    eng.matmul(mean_ps[1 - k][:, 0:W], mean_group[:, :], rowsum[:, 1 - k], start=True, stop=True)\
                       .then_inc(n["mean"], 1)
                if there(p - 1, PAIRS):
                    after(eng, n["sqsum"], p)
                    after(eng, n["ln"], p - 2)
                    eng.matmul(var_ps[1 - k][:, 0:W], mean_group[:, :], sqsum[:, 1 - k],
                               start=True, stop=True).then_inc(n["var"], 1)

            def scalar(eng, p, k):
                if there(p, PAIRS):
                    after(eng, n["centred"], p + 1)
                    after(eng, n["sqsum"], p - 1)
                    eng.activation(square[:, k], dst[:, p], ACT.Square).then_inc(n["square"], 1)
                if there(p - 1, PAIRS):
                    after(eng, n["var"], p)
                    after(eng, n["normed"], p - 2)
                    eng.activation(lnvar[:, 1 - k], var_ps[1 - k][:, 0:W], ACT.Ln, bias=eps[:, 0:1])\
                       .then_inc(n["ln"], 1)
                    eng.wait_ge(n["ln"], p)
                    eng.activation(rstd[:, 1 - k], lnvar[:, 1 - k], ACT.Exp, scale=-0.5)\
                       .then_inc(n["rstd"], 1)

            def pool(eng, p, k):
                if there(p, PAIRS):
                    after(eng, n["rstd"], p + 1)
                    after(eng, n["square"], p + 1)
                    v = dst[:, p].rearrange("c (h w) -> c h w", w=W)
                    eng.tensor_tensor(v, v, rstd[:, k].unsqueeze(1).broadcast_to([128, H, W]),
                                      ALU.mult).then_inc(n["normed"], 1)

            def run(eng, step, beside=lambda eng, i, k: None):
                def two(i):
                    for k in range(2):
                        step(eng, 2 * i + k, k)
                        beside(eng, i, k)
                step(eng, -1, 1)
                two(0)
                two(1)
                with eng.Fori(2, PAIRS // 2 - 1) as i:
                    two(i)
                two(PAIRS // 2 - 1)
                step(eng, PAIRS, 0)
                step(eng, PAIRS + 1, 1)

            return n, run, vector, tensor, scalar, pool, rstd

        fw1 = sb(whole, "fw1", [128, 2, 2, 128])
        fw2_in, fw2 = (sb(whole, n, [128, 2, C]) for n in ("fw2_in", "fw2"))
        fb1 = sb(whole, "fb1", [128, 2])
        forward_in = sem(whole, "forward_in")
        attention = whole.enter_context(ExitStack())
        eps = sb(whole, "eps", [128, 2])
        wqkv = sb(attention, "wqkv", [128, 3, 128])
        wq, wk, wv = (wqkv[:, n] for n in range(3))
        wp = sb(attention, "wp", [128, 128])
        bp = sb(attention, "bp", [128, 1])
        head_scale = sb(attention, "head_scale", [128, HEADS])
        bias_tab = sb(attention, "bias_tab", [128, 4, 2, HEADS, TOK])

        with ExitStack() as stage:
            consts_in = sem(stage, "consts_in")
            w_in = sem(stage, "w_in")
            zeroed = sem(stage, "zeroed")
            chain = sem(stage, "chain")
            hid_ps_ready = sem(stage, "hid_ps_ready")
            hid_ready = sem(stage, "hid_ready")
            bias_ps_ready = sem(stage, "bias_ps_ready")
            bias_rows_ready = sem(stage, "bias_rows_ready")
            bias_out = sem(stage, "bias_out")
            bias_in = sem(stage, "bias_in")
            bp_mean = sem(stage, "bp_mean")
            x_in = [sem(stage, f"x_in{k}") for k in range(2)]
            pw = sb(stage, "pw", [128, C])
            small = sb(stage, "small", [128, 2])
            tau_sb = sb(stage, "tau_sb", [128, HEADS])
            rel = sb(stage, "rel", [2, TOK * TOK // COLS, COLS])
            mw1 = sb(stage, "mw1", [2, META])
            mb1 = sb(stage, "mb1", [META, 1])
            mw2 = sb(stage, "mw2", [META, HEADS])
            mb2 = sb(stage, "mb2", [HEADS, 1])
            mask = sb(stage, "mask", [128, 4, 2, TOK])
            hid = sb(stage, "hid", [META, COLS])
            bias_rows = sb(stage, "bias_rows", [HEADS, TOK * TOK // COLS, COLS])
            bias_q = sb(stage, "bias_q", [128, HEADS, TOK])
            hid_ps = ps(stage, "hid_ps", [128, COLS])
            bias_ps = ps(stage, "bias_ps", [128, COLS])
            bp_ps = ps(stage, "bp_ps", [128, COLS])
            CHUNKS = TOK * TOK // COLS
            assert CHUNKS == PAIRS // 2

            def column(v):
                return v.rearrange("(c a) -> c a", a=1)

            loads = [(vecs[:, :], c_vecs), (rel[:, :, :], c_rel), (mw1[:, :], meta_w1), (mb1[:, :], column(meta_b1)),
                     (mw2[:, :], meta_w2), (mb2[:, :], column(meta_b2))]
            for lo, hi in HALVES:
                loads += [(wqkv[lo:hi, :, lo:hi], qkv_w.rearrange("c (t n) -> c t n", t=3)), (pw[lo:hi, :], proj_w)]
            loads += [(mask[:, :, :, :], c_mask),
                      (tau_sb[:, :], tau.rearrange("(a n) -> a n", a=1).broadcast_to([128, HEADS]))]
            x_pairs = x.rearrange("(a p) c h w -> a c p (h w)", a=2)

            def x_arrives(eng, p, k):
                after(eng, x_in[k], ((p - k) // 2 + 1) * 32)

            n1, gn_run, gn_v, gn_t, gn_a, gn_p, _ = group_norm(stage, "gn1", xs, xs, x_arrives)

            def bias_tensor(pe, i, k):
                if k == 0:
                    after(pe, hid_ready, i)
                    if isinstance(i, int):
                        pe.wait_ge(w_in, 16 * len(loads))
                    pe.matmul(hid_ps[:, :], mw1[:, :], rel[:, i], start=True, stop=True)\
                      .then_inc(hid_ps_ready, 1)
                else:
                    after(pe, hid_ready, i + 1)
                    after(pe, bias_rows_ready, i)
                    pe.matmul(bias_ps[0:HEADS, :], mw2[:, :], hid[:, :], start=True, stop=True)\
                      .then_inc(bias_ps_ready, 1)

            def bias_scalar(act, i, k):
                if k == 0:
                    if isinstance(i, int):
                        act.wait_ge(w_in, 16 * len(loads))
                    after(act, hid_ps_ready, i + 1)
                    after(act, bias_ps_ready, i)
                    act.activation(hid[:, :], hid_ps[:, :], ACT.Relu, bias=mb1[:, 0:1]).then_inc(hid_ready, 1)
                else:
                    after(act, bias_ps_ready, i + 1)
                    act.activation(bias_rows[:, i], bias_ps[0:HEADS, :], ACT.Identity,
                                   bias=mb2[:, 0:1]).then_inc(bias_rows_ready, 1)

            with nc.Block() as block:
                @block.sync
                def _(sp):
                    def load_pair(i, k):
                        after(sp, x_in[k], 32 * i)
                        for a, (lo, hi) in enumerate(HALVES):
                            sp.dma_start(xs[lo:hi, 2 * i + k], x_pairs[a, :, 2 * i + k]).then_inc(x_in[k], 16)

                    sp.dma_start(consts[:, :], c_consts).then_inc(consts_in, 16)
                    load_pair(0, 0)
                    load_pair(0, 1)
                    with sp.Fori(1, PAIRS // 2) as i:
                        load_pair(i, 0)
                        load_pair(i, 1)
                    sp.wait_ge(bias_rows_ready, CHUNKS)
                    sp.dma_start(bias_dram, bias_rows[:, :, :].rearrange("h n m -> h (n m)")).then_inc(bias_out, 16)
                    sp.wait_ge(bias_out, 16)
                    for lo, hi in HALVES:
                        sp.dma_start(bias_q[lo:hi], bias_dram.rearrange("h (q k) -> q h k", k=TOK)).then_inc(bias_in, 16)

                @block.scalar
                def _(act):
                    act.preload_act_table_set(EXP_LN)
                    act.wait_ge(zeroed, 1)
                    for dst, src in loads:
                        act.dma_start(dst, src).then_inc(w_in, 16)
                    act.wait_ge(chain, 4)
                    gn_run(act, gn_a, beside=bias_scalar)

                @block.gpsimd
                def _(pool):
                    pool.memset(wqkv[:, :, :], 0.0)
                    pool.memset(wp[:, :], 0.0).then_inc(zeroed, 1)
                    gn_run(pool, gn_p)

                @block.vector
                def _(dve):
                    links = [0]

                    def link(ins):
                        links[0] += 1
                        ins.then_inc(chain, 1)
                        dve.wait_ge(chain, links[0])

                    link(dve.memset(eps[:, 0:1], 1e-5))
                    link(dve.memset(eps[:, 1:2], NORM_FLOOR))
                    dve.wait_ge(consts_in, 16)
                    link(dve.tensor_scalar(mean_image, sum_image, 1.0 / C, None, ALU.mult))
                    link(dve.tensor_scalar(mean_group[:, :], sum_image, 1.0 / (C * H), None, ALU.mult))
                    gn_run(dve, gn_v)
                    dve.wait_ge(w_in, 16 * len(loads))
                    link(dve.tensor_scalar(tau_sb[:, :], tau_sb[:, :], 0.01, None, ALU.max))
                    link(dve.reciprocal(tau_sb[:, :], tau_sb[:, :]))
                    link(dve.tensor_tensor(head_scale[:, :], tau_sb[:, :], delta, ALU.mult))
                    link(dve.tensor_reduce(small[:, 0:1], pw[:, :], X, ALU.add))
                    link(dve.tensor_scalar(small[:, 1:2], small[:, 0:1], -1.0 / C, None, ALU.mult))
                    for lo, hi in HALVES:
                        link(dve.tensor_scalar(wp[lo:hi, lo:hi], pw[lo:hi, :], small[lo:hi, 1:2], None, ALU.add))
                    dve.wait_ge(bp_mean, 1)
                    link(dve.tensor_tensor(bp[:, :], proj_bias, bp_ps[:, 0:1], ALU.subtract))
                    dve.wait_ge(bias_in, 32)
                    for kind in range(4):
                        for w in range(2):
                            last = dve.tensor_tensor(
                                bias_tab[:, kind, w], bias_q[:, :, :],
                                mask[:, kind, w].unsqueeze(1).broadcast_to([128, HEADS, TOK]), ALU.add)
                    link(last)

                @block.tensor
                def _(pe):
                    pe.wait_ge(chain, 4)
                    gn_run(pe, gn_t, beside=bias_tensor)
                    pe.matmul(bp_ps[:, 0:1], mean_image, proj_bias, start=True, stop=True).then_inc(bp_mean, 1)

        xu = xs[:, :, :].rearrange("c p (j n) -> c (p j) n", j=2)

        def gather_pieces(j):
            for wi in range(2):
                r = 16 * j + WS * wi + SHIFT
                rows = [(r, 0, WS)] if r + WS <= H else [(r, 0, H - r), (0, H - r, WS)]
                for r0, t0, t1 in rows:
                    yield r0, 4, wi, t0, t1, 0, 3, 0, 8
                    yield r0, 28, wi, t0, t1, 3, 4, 0, 4
                    yield r0, 0, wi, t0, t1, 3, 4, 4, 8

        def piece(image, windows, r0, c0, wi, t0, t1, w0, w1, x0, x1):
            img = image.rearrange("c (h w) -> c h w", w=W)[:, r0:r0 + t1 - t0, c0:c0 + (w1 - w0) * (x1 - x0)]
            win = windows.rearrange("c (i j y x) -> c i y j x", i=2, j=4, y=WS)[:, wi, t0:t1, w0:w1, x0:x1]
            return img.rearrange("c h (j x) -> c h j x", x=x1 - x0), win

        forward_loads = [(fw1[lo:hi, a], ffn_w1.rearrange("c (m h) -> c m h", m=2)) for a, (lo, hi) in enumerate(HALVES)]
        forward_loads += [(fw2_in[:, :, :], ffn_w2.rearrange("(m h) c -> h m c", m=2)), (fb1[:, :], ffn_b1)]

        with ExitStack() as stage:
            s = {k: sem(stage, k) for k in (
                "xw_ready", "q_ps_ready", "k_ps_ready", "q_ready", "q_sq_ready", "k_ready", "k_sq_ready",
                "q_norm_ps", "k_norm_ps", "q_ln", "k_ln", "q_rnorm", "k_rnorm", "q_spread", "k_scaled",
                "k_spread", "k_spread_b", "scaled", "xw_saved", "v_ps_ready", "v_spread", "heads_copied", "proj_ps", "centred",
                "var_ps_ready", "var_ln", "rstd_ready", "normed", "skip_ready",
                "scores", "biased", "row_max", "shifted", "exped", "row_sum", "row_recip", "probs",
                "probs_t", "probs_t_copied", "mixed")}
            xw = [sb(stage, f"xw{j}", [128, COLS]) for j in range(2)]
            q_sb, k_sb = ([sb(stage, f"{n}{j}", [128, COLS]) for j in range(2)] for n in ("q_sb", "k_sb"))
            q_sq, k_sq, rq, rk = (sb(stage, n, [128, COLS]) for n in ("q_sq", "k_sq", "rq", "rk"))
            qd = [sb(stage, f"qd{j}", [128, WIN, 2, TOK]) for j in range(2)]
            kx = [sb(stage, f"kx{j}", [128, WIN, HEADS, TOK]) for j in range(2)]
            vd = [sb(stage, f"vd{j}", [128, WIN, 4, 2 * DH]) for j in range(2)]
            sc = sb(stage, "sc", [128, 8, 2, HEADS, TOK])
            pt = [sb(stage, f"pt{k}", [128, 4, 128]) for k in range(2)]
            mx = sb(stage, "mx", [128, 2, 2 * HEADS])
            sm = sb(stage, "sm", [128, 2, 2 * HEADS])
            rs8 = sb(stage, "rs8", [128, 2, 2 * HEADS])
            ob, csq, rs = (sb(stage, n, [128, COLS]) for n in ("ob", "csq", "rs"))
            cc = [sb(stage, f"cc{j}", [128, COLS]) for j in range(2)]
            s_ps = [ps(stage, f"s_ps{k}", [128, 2, HEADS, TOK]) for k in range(2)]
            t_ps = [ps(stage, f"t_ps{k}", [128, 4, 128]) for k in range(2)]
            o_ps = ps(stage, "o_ps", [128, COLS])
            qn_ps = ps(stage, "qn_ps", [128, COLS])
            kn_ps = ps(stage, "kn_ps", [128, COLS])
            vv_ps = ps(stage, "vv_ps", [128, COLS])
            zero = sem(stage, "zero")
            forward_zero = sem(stage, "forward_zero")

            def units(eng, slot):
                def both(i):
                    for j in range(2):
                        for q in range(4):
                            slot(eng, 2 * i + j, j, q, 8 * i + 4 * j + q)
                for i in (-1, 0, 1):
                    both(i)
                with eng.Fori(2, PAIRS - 1) as i:
                    both(i)
                for i in (PAIRS - 1, PAIRS, PAIRS + 1):
                    both(i)

            def tensor_slot(pe, u, j, q, g):
                if q == 0 and there(u, UNITS):
                    after(pe, s["xw_ready"], u + 1)
                    after(pe, s["v_spread"], u)
                    after(pe, s["var_ln"], u - 2, UNITS)
                    for t in range(4):
                        last = pe.matmul(vv_ps[:, 128 * t:128 * (t + 1)], xw[j][:, 128 * t:128 * (t + 1)],
                                         wv, start=True, stop=True)
                    last.then_inc(s["v_ps_ready"], 1)
                n = g - 5
                if there(n, DUOS):
                    m = (q - 1) % 4
                    jn = j if q == 0 else 1 - j
                    after(pe, s["probs_t_copied"], n + 1)
                    if m == 0:
                        after(pe, s["v_spread"], u)
                        after(pe, s["heads_copied"], u - 1)
                    for w in range(2):
                        for a in range(2):
                            for hp in range(2):
                                at = 2 * a + hp
                                win = 2 * m + w
                                last = pe.matmul(
                                    o_ps[32 * at:32 * at + 32, TOK * win:TOK * (win + 1)],
                                    vd[jn][:, win, at], pt[(q + 1) % 2][:, 2 * w + hp, TOK * a:TOK * (a + 1)],
                                    start=True, stop=True)
                    last.then_inc(s["mixed"], 1)
                if q == 1 and there(u + 2, UNITS):
                    after(pe, s["xw_ready"], u + 3)
                    after(pe, s["q_ln"], u + 2)
                    pe.matmul(qn_ps[:, :], wq, xw[j][:, :], start=True, stop=True).then_inc(s["q_ps_ready"], 1)
                    after(pe, s["k_ln"], u + 2)
                    pe.matmul(kn_ps[:, :], wk, xw[j][:, :], start=True, stop=True).then_inc(s["k_ps_ready"], 1)
                if q == 2 and there(u - 2, UNITS):
                    after(pe, s["q_sq_ready"], u + 3, UNITS)
                    after(pe, s["heads_copied"], u - 1)
                    pe.matmul(qn_ps[:, :], wp[:, :], ob[:, :], start=True, stop=True).then_inc(s["proj_ps"], 1)
                if q == 3 and there(u - 2, UNITS):
                    after(pe, s["v_spread"], u + 1, UNITS)
                    after(pe, s["centred"], u - 1)
                    pe.matmul(vv_ps[:, :], mean_image, csq[:, :], start=True, stop=True)\
                      .then_inc(s["var_ps_ready"], 1)
                if q == 3 and there(u + 2, UNITS):
                    after(pe, s["q_sq_ready"], u + 3)
                    after(pe, s["centred"], u - 1)
                    pe.matmul(qn_ps[:, :], sum_head, q_sq[:, :], start=True, stop=True).then_inc(s["q_norm_ps"], 1)
                n = g - 3
                if there(n, DUOS):
                    after(pe, s["probs"], n + 1)
                    after(pe, s["probs_t_copied"], n - 1)
                    for w in range(2):
                        for hp in range(2):
                            last = pe.transpose(
                                t_ps[(q + 1) % 2][:, 2 * w + hp],
                                sc[:, (4 * j + q - 3) % 8, w, 2 * hp:2 * hp + 2].rearrange("c h k -> c (h k)"),
                                ident)
                    last.then_inc(s["probs_t"], 1)
                n = g + 1
                if there(n, DUOS):
                    m = (q + 1) % 4
                    jn = j if q < 3 else 1 - j
                    after(pe, s["biased"], n - 1)
                    if m == 0:
                        after(pe, s["q_spread"], u + 2)
                        after(pe, s["k_spread"], u + 2)
                        after(pe, s["k_spread_b"], u + 2)
                    for w in range(2):
                        last = pe.matmul(s_ps[(q + 1) % 2][:, w], qd[jn][:, 2 * m + w],
                                         kx[jn][:, 2 * m + w], start=True, stop=True)
                    last.then_inc(s["scores"], 1)
                if q == 2 and there(u + 2, UNITS):
                    after(pe, s["k_sq_ready"], u + 3)
                    pe.matmul(kn_ps[:, :], sum_head, k_sq[:, :], start=True, stop=True).then_inc(s["k_norm_ps"], 1)

            def spread_keys(eng, put, u, j, heads, done):
                after(eng, s["k_scaled"], u + 2)
                after(eng, s["scores"], 4 * u)
                for h in heads:
                    last = put(kx[1 - j][:, :, h], k_sb[1 - j][:, :].rearrange("c (w k) -> c w k", k=TOK), h)
                last.then_inc(s[done], 1)

            def scalar_slot(act, u, j, q, g):
                n = g - 4
                if there(n, DUOS):
                    after(act, s["probs_t"], n + 1)
                    after(act, s["mixed"], n - 1)
                    act.activation(pt[q % 2][:, :, :], t_ps[q % 2][:, :, :], ACT.Copy)\
                       .then_inc(s["probs_t_copied"], 1)
                n = g - 1
                if there(n, DUOS):
                    after(act, s["shifted"], n + 1)
                    t = sc[:, (4 * j + q - 1) % 8]
                    act.activation(t, t, ACT.Exp).then_inc(s["exped"], 1)
                if q == 0 and there(u - 2, UNITS):
                    after(act, s["mixed"], 4 * u - 4)
                    after(act, s["proj_ps"], u - 2)
                    act.activation(ob[:, :], o_ps[:, :], ACT.Identity, bias=bv).then_inc(s["heads_copied"], 1)
                if q == 0 and there(u + 1, UNITS):
                    after(act, s["q_norm_ps"], u + 2)
                    after(act, s["q_spread"], u + 1)
                    act.activation(rq[:, :], qn_ps[:, :], ACT.Ln, bias=eps[:, 1:2]).then_inc(s["q_ln"], 1)
                    after(act, s["k_norm_ps"], u + 2)
                    after(act, s["k_scaled"], u + 1)
                    act.activation(rk[:, :], kn_ps[:, :], ACT.Ln, bias=eps[:, 1:2]).then_inc(s["k_ln"], 1)
                    act.wait_ge(s["q_ln"], u + 2)
                    act.activation(rq[:, :], rq[:, :], ACT.Exp, scale=-0.5).then_inc(s["q_rnorm"], 1)
                    act.wait_ge(s["k_ln"], u + 2)
                    act.activation(rk[:, :], rk[:, :], ACT.Exp, scale=-0.5).then_inc(s["k_rnorm"], 1)
                if q == 1 and there(u + 2, UNITS):
                    after(act, s["q_ps_ready"], u + 3)
                    after(act, s["q_spread"], u + 1)
                    act.activation(q_sb[j][:, :], qn_ps[:, :], ACT.Identity, bias=bq).then_inc(s["q_ready"], 1)
                    after(act, s["q_norm_ps"], u + 2)
                    act.activation(q_sq[:, :], qn_ps[:, :], ACT.Square, bias=bq).then_inc(s["q_sq_ready"], 1)
                    after(act, s["k_ps_ready"], u + 3)
                    after(act, s["k_spread"], u + 1)
                    after(act, s["k_spread_b"], u + 1)
                    act.activation(k_sb[j][:, :], kn_ps[:, :], ACT.Identity, bias=bk).then_inc(s["k_ready"], 1)
                if q == 2 and there(u - 2, UNITS):
                    after(act, s["proj_ps"], u - 1)
                    after(act, s["var_ps_ready"], u - 2)
                    act.activation(csq[:, :], qn_ps[:, :], ACT.Square, bias=bp[:, 0:1])
                    after(act, s["normed"], u - 3)
                    act.activation(cc[j][:, :], qn_ps[:, :], ACT.Identity, bias=bp[:, 0:1]).then_inc(s["centred"], 1)
                if q == 2 and there(u + 1, UNITS):
                    spread_keys(act, lambda out, keys, h: act.activation(
                        out, keys, ACT.Identity, scale=head_scale[:, h:h + 1]), u, j, ACT_HEADS, "k_spread")
                if q == 3 and there(u - 2, UNITS):
                    after(act, s["var_ps_ready"], u - 1)
                    after(act, s["scaled"], u - 2)
                    act.activation(rs[:, :], vv_ps[:, :], ACT.Ln, bias=eps[:, 0:1]).then_inc(s["var_ln"], 1)
                    act.wait_ge(s["var_ln"], u - 1)
                    act.activation(rs[:, :], rs[:, :], ACT.Exp, scale=-0.5).then_inc(s["rstd_ready"], 1)
                if q == 3 and there(u + 1, UNITS):
                    after(act, s["xw_ready"], u + 3 if j == 1 else u + 2, UNITS)
                    act.activation(xu[:, u + 1], xw[1 - j][:, :], ACT.Identity, bias=b1).then_inc(s["xw_saved"], 1)

            def vector_slot(dve, u, j, q, g):
                n = g - 1
                if there(g, DUOS):
                    kind = 2 * (j == 1 and q // 2 == 1) + q % 2
                    after(dve, s["scores"], g + 1)
                    after(dve, s["probs_t"], g - 7)
                    dve.tensor_tensor(sc[:, 4 * j + q], s_ps[q % 2][:, :, :, :], bias_tab[:, kind], ALU.add)\
                       .then_inc(s["biased"], 1)
                if there(g, DUOS):
                    dve.wait_ge(s["biased"], g + 1)
                    after(dve, s["shifted"], g - 1)
                    dve.tensor_reduce(mx[:, q % 2], sc[:, 4 * j + q].rearrange("c w h k -> c (w h) k"), X, ALU.max)\
                       .then_inc(s["row_max"], 1)
                if q == 0 and there(u + 2, UNITS):
                    after(dve, s["v_ps_ready"], u + 1)
                    after(dve, s["xw_saved"], u + 1)
                    pair = (u + 2) // 2 if isinstance(u, int) else (u - j) // 2 + 1
                    for pc in gather_pieces(j):
                        img, win = piece(xs[:, pair], xw[j][:, :], *pc)
                        last = dve.tensor_copy(win, img)
                    last.then_inc(s["xw_ready"], 1)
                if there(n, DUOS):
                    after(dve, s["exped"], n + 1)
                    after(dve, s["row_recip"], n - 1)
                    dve.tensor_reduce(sm[:, (q - 1) % 2], sc[:, (4 * j + q - 1) % 8].rearrange("c w h k -> c (w h) k"),
                                      X, ALU.add).then_inc(s["row_sum"], 1)
                if q == 3 and there(u - 3, UNITS):
                    after(dve, s["xw_saved"], u - 2)
                    after(dve, s["scaled"], u - 2)
                    dve.scalar_tensor_tensor(xu[:, u - 3], cc[1 - j][:, :], g1, xu[:, u - 3], ALU.mult, ALU.add)\
                       .then_inc(s["normed"], 1)
                if q == 1 and there(u, UNITS):
                    after(dve, s["v_ps_ready"], u + 1)
                    after(dve, s["mixed"], 4 * u - 4)
                    vps = vv_ps[:, :].rearrange("c (t a d) -> c t a d", t=4, a=4)
                    for par in range(2):
                        for h2 in range(2):
                            last = dve.tensor_copy(
                                vd[j][64 * h2:64 * h2 + 64, par:WIN:2, :, DH * h2:DH * (h2 + 1)],
                                vps[64 * par:64 * par + 64, :, :, DH * h2:DH * (h2 + 1)])
                    last.then_inc(s["v_spread"], 1)
                if q == 1 and there(u + 1, UNITS):
                    after(dve, s["k_ready"], u + 2)
                    after(dve, s["k_sq_ready"], u + 2)
                    after(dve, s["k_rnorm"], u + 2)
                    dve.tensor_tensor(k_sb[1 - j][:, :], k_sb[1 - j][:, :], rk[:, :], ALU.mult).then_inc(s["k_scaled"], 1)
                if q == 2 and there(u + 1, UNITS):
                    after(dve, s["q_ready"], u + 2)
                    after(dve, s["q_rnorm"], u + 2)
                    after(dve, s["scores"], 4 * u)
                    for a, (lo, hi) in enumerate(HALVES):
                        last = dve.tensor_tensor(qd[1 - j][lo:hi, :, a],
                                                 q_sb[1 - j][lo:hi, :].rearrange("c (w k) -> c w k", k=TOK),
                                                 rq[lo:hi, :].rearrange("c (w k) -> c w k", k=TOK), ALU.mult)
                    last.then_inc(s["q_spread"], 1)
                if there(n, DUOS):
                    dve.wait_ge(s["row_sum"], n + 1)
                    after(dve, s["probs"], n - 1)
                    dve.reciprocal(rs8[:, (q - 1) % 2], sm[:, (q - 1) % 2]).then_inc(s["row_recip"], 1)

            def pool_slot(pool, u, j, q, g):
                n = g - 2
                if there(n, DUOS):
                    after(pool, s["row_recip"], n + 1)
                    t = sc[:, (4 * j + q - 2) % 8].rearrange("c w h k -> c (w h) k")
                    pool.tensor_tensor(t, t, rs8[:, q % 2].unsqueeze(2).broadcast_to([128, 2 * HEADS, TOK]),
                                       ALU.mult).then_inc(s["probs"], 1)
                if q == 2 and there(u + 1, UNITS):
                    spread_keys(pool, lambda out, keys, h: pool.tensor_tensor(
                        out, keys, head_scale[:, h:h + 1].unsqueeze(2).broadcast_to([128, WIN, TOK]), ALU.mult),
                        u, j, POOL_HEADS, "k_spread_b")
                if there(g, DUOS):
                    after(pool, s["row_max"], g + 1)
                    t = sc[:, 4 * j + q].rearrange("c w h k -> c (w h) k")
                    pool.tensor_tensor(t, t, mx[:, q % 2].unsqueeze(2).broadcast_to([128, 2 * HEADS, TOK]),
                                       ALU.subtract).then_inc(s["shifted"], 1)
                if q == 0 and there(u - 3, UNITS):
                    after(pool, s["rstd_ready"], u - 2)
                    pool.tensor_tensor(cc[1 - j][:, :], cc[1 - j][:, :], rs[:, :], ALU.mult).then_inc(s["scaled"], 1)
                if q == 1 and there(u + 2, UNITS):
                    after(pool, s["k_ready"], u + 3)
                    after(pool, s["k_norm_ps"], u + 2)
                    pool.tensor_tensor(k_sq[:, :], k_sb[j][:, :], k_sb[j][:, :], ALU.mult).then_inc(s["k_sq_ready"], 1)

            with nc.Block() as block:
                @block.tensor
                def _(pe):
                    pe.wait_ge(zero, 2)
                    units(pe, tensor_slot)

                @block.scalar
                def _(act):
                    act.preload_act_table_set(EXP_LN)
                    act.wait_ge(zero, 2)
                    units(act, scalar_slot)

                @block.vector
                def _(dve):
                    dve.memset(qd[0][:, :, :, :], 0.0)
                    dve.memset(qd[1][:, :, :, :], 0.0).then_inc(zero, 1)
                    dve.wait_ge(zero, 2)
                    units(dve, vector_slot)

                @block.sync
                def _(sp):
                    sp.wait_ge(forward_zero, 1)
                    for dst, src in forward_loads:
                        sp.dma_start(dst, src).then_inc(forward_in, 16)

                @block.gpsimd
                def _(pool):
                    pool.memset(fw1[:, :, :, :], 0.0).then_inc(forward_zero, 1)
                    pool.memset(vd[0][:, :, :, :], 0.0)
                    pool.memset(vd[1][:, :, :, :], 0.0).then_inc(zero, 1)
                    units(pool, pool_slot)
        attention.close()

        x1 = sb(whole, "x1", [128, PAIRS, PIX])
        with ExitStack() as stage:
            s = {k: sem(stage, "f_" + k) for k in (
                "chain", "hid_ps", "gelu", "out_ps", "centred", "var_ps", "ln", "rstd", "normed",
                "update", "skipped", "b2_mean", "x_biased", "done")}
            FORWARD_LINKS = 4
            x_back = [sem(stage, f"x_back{k}") for k in range(2)]
            fsum = sb(stage, "fsum", [128, 2, 2])
            fb2 = sb(stage, "fb2", [128, 1])
            hs = sb(stage, "hs", [128, 2, 4, COLS])
            cc = sb(stage, "fcc", [128, 4, COLS])
            csq = sb(stage, "fcsq", [128, 2, COLS])
            rs = sb(stage, "frs", [128, 2, COLS])
            upd = sb(stage, "upd", [128, 2, COLS])
            xr = sb(stage, "xr", [128, 2, PIX])
            h_ps = [ps(stage, f"h_ps{m}", [128, COLS]) for m in range(4)]
            c_ps = [ps(stage, f"c_ps{m}", [128, COLS]) for m in range(2)]
            v_ps = [ps(stage, f"v_ps{m}", [128, COLS]) for m in range(2)]

            def steps(eng, step):
                def four(i):
                    for k in range(4):
                        step(eng, 4 * i + k, k)
                four(0)
                four(1)
                with eng.Fori(2, UNITS // 4 - 1) as i:
                    four(i)
                four(UNITS // 4 - 1)
                four(UNITS // 4)

            def tensor_step(pe, u, k):
                if there(u, UNITS):
                    for m in range(4):
                        after(pe, s["gelu"], 4 * u - 3 + m)
                        pe.matmul(h_ps[m][:, :], fw1[:, m % 2, m // 2], xu[:, u], start=True, stop=True).then_inc(s["hid_ps"], 1)
                if there(u - 1, UNITS):
                    after(pe, s["centred"], u - 2)
                    if isinstance(u, int) and u == 1:
                        pe.wait_ge(s["chain"], FORWARD_LINKS)
                    for m in range(4):
                        after(pe, s["gelu"], 4 * u - 3 + m)
                        lo, hi = HALVES[m % 2]
                        last = pe.matmul(c_ps[(k - 1) % 2][lo:hi, :], fw2[:, m // 2], hs[:, (k - 1) % 2, m],
                                         start=(m < 2), stop=(m >= 2))
                    last.then_inc(s["out_ps"], 1)
                if there(u - 2, UNITS):
                    after(pe, s["centred"], u - 1)
                    after(pe, s["ln"], u - 3)
                    pe.matmul(v_ps[k % 2][:, :], mean_image, csq[:, k % 2], start=True, stop=True)\
                      .then_inc(s["var_ps"], 1)

            def scalar_step(act, u, k):
                if there(u, UNITS):
                    for m in range(4):
                        after(act, s["hid_ps"], 4 * u + m + 1)
                        after(act, s["out_ps"], u - 1)
                        act.activation(hs[:, k % 2, m], h_ps[m][:, :], ACT.Gelu, bias=fb1[:, m // 2:m // 2 + 1])\
                           .then_inc(s["gelu"], 1)
                if there(u - 1, UNITS):
                    after(act, s["out_ps"], u)
                    after(act, s["update"], u - 4)
                    act.activation(cc[:, (k - 1) % 4], c_ps[(k - 1) % 2][:, :], ACT.Identity, bias=fb2[:, 0:1])
                    after(act, s["var_ps"], u - 2)
                    act.activation(csq[:, (k - 1) % 2], c_ps[(k - 1) % 2][:, :], ACT.Square, bias=fb2[:, 0:1])\
                       .then_inc(s["centred"], 1)
                if k % 2 == 1 and there(u - 3, UNITS):
                    act.preload_act_table_set(EXP_LN)
                    for d in (3, 2):
                        after(act, s["var_ps"], u - d + 1)
                        after(act, s["normed"], u - d - 1)
                        act.activation(rs[:, (k - d) % 2], v_ps[(k - d) % 2][:, :], ACT.Ln, bias=eps[:, 0:1])\
                           .then_inc(s["ln"], 1)
                    for d in (3, 2):
                        act.wait_ge(s["ln"], u - d + 1)
                        act.activation(rs[:, (k - d) % 2], rs[:, (k - d) % 2], ACT.Exp, scale=-0.5)\
                           .then_inc(s["rstd"], 1)

            def vector_step(dve, u, k):
                if k % 2 == 1 and there(u - 3, UNITS):
                    for d in (3, 2):
                        after(dve, s["rstd"], u - d + 1)
                        dve.tensor_tensor(cc[:, (k - d) % 4], cc[:, (k - d) % 4], rs[:, (k - d) % 2], ALU.mult)\
                           .then_inc(s["normed"], 1)
                    for d in (3, 2):
                        dve.wait_ge(s["normed"], u - d + 1)
                        after(dve, s["skipped"], u - d - 1)
                        dve.scalar_tensor_tensor(upd[:, (k - d) % 2], cc[:, (k - d) % 4], g2, xu[:, u - d],
                                                 ALU.mult, ALU.add).then_inc(s["update"], 1)
                    pair = (u - 3) // 2 if isinstance(u, int) else (u - k) // 2 + (k - 3) // 2
                    kp = ((k - 3) // 2) % 2
                    for d in (3, 2):
                        j = 3 - d
                        if j == 0:
                            after(dve, s["x_biased"], pair + 1)
                        dve.wait_ge(s["update"], u - d + 1)
                        for pc in gather_pieces(j):
                            img, win = piece(xr[:, kp], upd[:, (k - d) % 2], *pc)
                            dst, _ = piece(x1[:, pair], upd[:, (k - d) % 2], *pc)
                            last = dve.tensor_tensor(dst, img, win, ALU.add)
                        last.then_inc(s["skipped"], 1)

            def sync_pair(sp, p, k):
                after(sp, s["skipped"], 2 * p - 2)
                for a, (lo, hi) in enumerate(HALVES):
                    sp.dma_start(xr[lo:hi, k], x_pairs[a, :, p]).then_inc(x_back[k], 16)

            def pool_pair(pool, i, k):
                after(pool, x_back[k], 32 * (i + 1))
                pool.tensor_tensor(xr[:, k], xr[:, k], b2.broadcast_to([128, PIX]), ALU.add).then_inc(s["x_biased"], 1)

            def in_pairs(eng, step, n=PAIRS // 2):
                step(0)
                with eng.Fori(1, n) as i:
                    step(i)

            with nc.Block() as block:
                @block.sync
                def _(sp):
                    in_pairs(sp, lambda i: (sync_pair(sp, 2 * i, 0), sync_pair(sp, 2 * i + 1, 1)))

                @block.gpsimd
                def _(pool):
                    in_pairs(pool, lambda i: (pool_pair(pool, i, 0), pool_pair(pool, i, 1)))

                @block.vector
                def _(dve):
                    links = [0]

                    def link(ins):
                        links[0] += 1
                        ins.then_inc(s["chain"], 1)
                        dve.wait_ge(s["chain"], links[0])

                    dve.wait_ge(forward_in, 16 * len(forward_loads))
                    link(dve.tensor_reduce(fsum[:, :, 0], fw2_in[:, :, :], X, ALU.add))
                    link(dve.tensor_scalar(fsum[:, :, 1], fsum[:, :, 0], -1.0 / C, None, ALU.mult))
                    link(dve.tensor_tensor(fw2[:, :, :], fw2_in[:, :, :],
                                           fsum[:, :, 1].unsqueeze(2).broadcast_to([128, 2, C]), ALU.add))
                    dve.wait_ge(s["b2_mean"], 1)
                    link(dve.tensor_tensor(fb2[:, :], ffn_bias, c_ps[0][:, 0:1], ALU.subtract))
                    steps(dve, vector_step)

                @block.tensor
                def _(pe):
                    pe.wait_ge(forward_in, 16 * len(forward_loads))
                    pe.matmul(c_ps[0][:, 0:1], mean_image, ffn_bias, start=True, stop=True)\
                      .then_inc(s["b2_mean"], 1)
                    steps(pe, tensor_step)

                @block.scalar
                def _(act):
                    act.wait_ge(forward_in, 16 * len(forward_loads))
                    act.wait_ge(s["chain"], FORWARD_LINKS)
                    steps(act, scalar_step)

        ys = xs
        yt = xs[:, :, :].rearrange("c p (g n) -> c p g n", g=8)
        scores = sb(whole, "scores_sb", [128, PAIRS, 8, 2])
        raw_scores = sb(whole, "raw_scores", [128, PAIRS, 8, 2 * 2])
        with ExitStack() as stage:
            s = {k: sem(stage, "y_" + k) for k in ("w_in", "zero", "turned", "turn_copied")}
            TURN = 128 + 4
            turn = sb(stage, "turn", [128, 8, TURN])
            cw_in = sb(stage, "cw_in", [128, BLOCKS])
            ynow = sb(stage, "ynow", [128, 2, PIX])
            turn_ps = [ps(stage, f"turn_ps{k}", [128, 2, TURN]) for k in range(4)]
            n2, gn_run, gn_v, gn_t, gn_a, gn_p, rstd2 = group_norm(stage, "gn2", x1, ys, lambda eng, p, k: None)

            def blocks(k, gp):
                return ynow[:, k, 128 * gp:128 * (gp + 1)]

            def pool_scale(pool, p, k):
                if not there(p, PAIRS):
                    return
                after(pool, n2["rstd"], p + 1)
                after(pool, n2["square"], p + 1)
                after(pool, s["turned"], 4 * (p - 1))
                shape = [128, 4, WS, WS]
                for gy in range(4):
                    last = pool.tensor_tensor(
                        ynow[:, k].rearrange("c (y x h w) -> c y x h w", y=4, x=4, h=WS)[:, gy],
                        ys[:, p].rearrange("c (y h x w) -> c y x h w", y=4, x=4, h=WS)[:, gy],
                        rstd2[:, k].rearrange("c (x w) -> c x w", x=4).unsqueeze(2).broadcast_to(shape), ALU.mult)
                last.then_inc(n2["normed"], 1)

            def tensor_turn(pe, p, k):
                gn_t(pe, p, k)
                m = p - 2
                if not there(m, PAIRS):
                    return
                after(pe, n2["normed"], m + 1)
                for b in range(4):
                    after(pe, s["turn_copied"], 4 * m - 3 + b)
                    for c in range(2):
                        last = pe.matmul(turn_ps[b][:, c], blocks(k, 2 * b + c), turn[:, 2 * b + c],
                                         start=True, stop=True)
                    last.then_inc(s["turned"], 1)

            def scalar_turn(act, p, k):
                gn_a(act, p, k)
                m = p - 2
                if not there(m, PAIRS):
                    return
                for b in range(4):
                    after(act, s["turned"], 4 * m + 1 + b)
                    act.activation(yt[:, m, 2 * b:2 * b + 2], turn_ps[b][:, :, 0:128], ACT.Copy)
                    act.activation(raw_scores[:, m, 2 * b:2 * b + 2], turn_ps[b][:, :, 128:TURN], ACT.Copy)\
                       .then_inc(s["turn_copied"], 1)

            with nc.Block() as block:
                @block.sync
                def _(sp):
                    for lo, hi in HALVES:
                        sp.dma_start(cw_in[lo:hi, :], conv_w).then_inc(s["w_in"], 16)

                @block.gpsimd
                def _(pool):
                    pool.memset(turn[:, :, :], 0.0).then_inc(s["zero"], 1)
                    pool.wait_ge(s["zero"], 1)
                    pool.wait_ge(s["w_in"], 32)
                    pool.tensor_copy(turn[:, :, 0:128], ident.unsqueeze(1).broadcast_to([128, 8, 128]))\
                        .then_inc(s["zero"], 1)
                    for a, (lo, hi) in enumerate(HALVES):
                        pool.wait_ge(s["zero"], 2 + a)
                        pool.tensor_copy(
                            turn[lo:hi, :, 128:TURN].rearrange("c g (b a) -> c g b a", a=2)[:, :, :, a],
                            cw_in[lo:hi, :].rearrange("c (g b) -> c g b", b=2)).then_inc(s["zero"], 1)
                    gn_run(pool, pool_scale)

                @block.vector
                def _(dve):
                    gn_run(dve, gn_v)

                @block.scalar
                def _(act):
                    act.preload_act_table_set(EXP_LN)
                    gn_run(act, scalar_turn)

                @block.tensor
                def _(pe):
                    pe.wait_ge(s["zero"], 4)
                    gn_run(pe, tensor_turn)

        with ExitStack() as stage:
            s = {k: sem(stage, "t_" + k) for k in (
                "w_in", "own", "rows", "exped", "pick", "zero", "picked_t", "picked_copied", "st_t", "st_copied", "gathered",
                "feat", "hid_ps", "hid", "rec_ps", "rec", "rec_out", "mixed", "added", "stored")}
            rec_in = sem(stage, "rec_in")
            w1 = sb(stage, "w1", [128, TOP, INDIM])
            w1s = sb(stage, "w1s", [128, INDIM])
            w2 = sb(stage, "w2", [MT, 4, OUTDIM])
            mb = sb(stage, "mb", [MT, 4])
            mb2r = sb(stage, "mb2r", [1, OUTDIM])
            one = sb(stage, "one", [1, 128])
            ow = sb(stage, "ow", [2 * OC, 128])
            iota = sb(stage, "iota", [128, TOK])
            e = sb(stage, "e", [128, 4, TOK])
            pr, st, cm, oh = (sb(stage, n, [128, 4, TOK]) for n in ("pr", "st", "cm", "oh"))
            esum = sb(stage, "esum", [128, 4])
            top = sb(stage, "top", [128, 4, 8])
            tidx = sb(stage, "tidx", [128, 4, 8], U32)
            tidf = sb(stage, "tidf", [128, 4, 8])
            zeros = sb(stage, "zeros", [128, TOK])
            sel = sb(stage, "sel", [128, TOP, 4, TOK])
            r = sb(stage, "r", [128, 2, 2, TOP, 128])
            st_t = sb(stage, "st_t", [128, 2, 256])
            feat = sb(stage, "feat", [128, TOP, 256])
            hid = sb(stage, "mlp_hid", [MT, 4, COLS])
            rec = sb(stage, "rec_sb", [128, 4, OUTDIM])
            grid = yt[0:2 * OC, :, :, :].rearrange("o p g n -> o p (g n)")
            psb = [ps(stage, f"bank{k}", [128, COLS]) for k in range(8)]

            loads = [(w2[:, :, :], mlp_w2.rearrange("(m k) n -> k m n", k=MT)),
                     (mb[:, :], mlp_b1),
                     (mb2r[:, :], mlp_b2.rearrange("(a n) -> a n", a=1)),
                     (iota[:, :], c_iota)]
            for a, (lo, hi) in enumerate(HALVES):
                loads += [(w1[lo:hi, :, :], mlp_w1[0:TOP * C].rearrange("(s c) n -> c s n", c=C)),
                          (w1s[lo:hi, :], mlp_w1[TOP * C:INDIM]),
                          (ow[OC * a:OC * (a + 1), lo:hi], out_w)]
            PROJ = 3

            with nc.Block() as block:
                @block.sync
                def _(sp):
                    sp.wait_ge(s["zero"], 3)
                    for dst, src in loads:
                        sp.dma_start(dst, src).then_inc(s["w_in"], 16)
                    for t in range(4):
                        sp.wait_ge(s["rec"], t + 1)
                        sp.dma_start(rec_dram[128 * t:128 * (t + 1), :], rec[:, t]).then_inc(s["rec_out"], 16)
                    sp.wait_ge(s["rec_out"], 64)
                    sp.wait_ge(s["gathered"], 8)
                    for a in range(2):
                        sp.dma_start(grid[OC * a:OC * (a + 1)].rearrange("o p (g l) -> o (p g) l", l=TOK),
                                     rec_dram[256 * a:256 * (a + 1)].rearrange("r (o l) -> o r l", l=TOK))\
                          .then_inc(rec_in, 16)
                    out_pairs = out.rearrange("(a p) c h w -> a c p (h w)", a=2)

                    def store(p):
                        sp.wait_ge(s["added"], 2 * p + 2)
                        for a, (lo, hi) in enumerate(HALVES):
                            sp.dma_start(out_pairs[a, :, p], x1[lo:hi, p]).then_inc(s["stored"], 16)
                    store(0)
                    with sp.Fori(1, PAIRS) as p:
                        store(p)
                    sp.wait_ge(s["stored"], 32 * PAIRS)

                @block.gpsimd
                def _(pool):
                    pool.memset(ow[:, :], 0.0).then_inc(s["zero"], 1)
                    pool.memset(one[:, :], 1.0).then_inc(s["zero"], 1)
                    pool.memset(st_t[:, :, :], 0.0)
                    pool.memset(r[:, :, :, :, :], 0.0).then_inc(s["zero"], 1)

                @block.vector
                def _(dve):
                    links = [0]

                    def link(ins):
                        links[0] += 1
                        ins.then_inc(s["pick"], 1)
                        dve.wait_ge(s["pick"], links[0])

                    for b, (lo, hi) in enumerate(HALVES):
                        last = dve.tensor_copy(scores[lo:hi], raw_scores[lo:hi, :, :, 2 * b:2 * b + 2])
                    last.then_inc(s["own"], 1)
                    dve.memset(zeros[:, :], 0.0)
                    dve.wait_ge(s["zero"], 3)
                    dve.wait_ge(s["exped"], 2)
                    dve.wait_ge(s["w_in"], 16 * len(loads))
                    full = [128, 4, TOK]
                    link(dve.tensor_reduce(esum[:, :], e[:, :, :], X, ALU.add))
                    link(dve.reciprocal(esum[:, :], esum[:, :]))
                    link(dve.tensor_tensor(pr[:, :, :], e[:, :, :], esum[:, :].unsqueeze(2).broadcast_to(full), ALU.mult))
                    for t in range(4):
                        last = dve.max(top[:, t], pr[:, t])
                    link(last)
                    for t in range(4):
                        last = dve.max_index(tidx[:, t], top[:, t], pr[:, t])
                    link(last)
                    link(dve.tensor_copy(tidf[:, :, :], tidx[:, :, :]))
                    positions = iota[:, :].unsqueeze(1).broadcast_to(full)
                    for k in range(TOP):
                        one_hot = tidf[:, :, k:k + 1].broadcast_to(full)
                        if k == 0:
                            link(dve.tensor_tensor(st[:, :, :], positions, one_hot, ALU.is_equal))
                        else:
                            link(dve.tensor_tensor(oh[:, :, :], positions, one_hot, ALU.is_equal))
                            link(dve.tensor_tensor(st[:, :, :], st[:, :, :], oh[:, :, :], ALU.add))
                    for t in range(4):
                        last = dve.tensor_tensor_scan(cm[:, t], st[:, t], zeros[:, :], 0.0, ALU.add, ALU.add)
                    link(last)
                    link(dve.tensor_tensor(cm[:, :, :], cm[:, :, :], st[:, :, :], ALU.mult))
                    link(dve.tensor_tensor(st[:, :, :], st[:, :, :], pr[:, :, :], ALU.subtract))
                    link(dve.tensor_tensor(st[:, :, :], st[:, :, :], pr[:, :, :], ALU.add))
                    for k in range(TOP):
                        last = dve.scalar_tensor_tensor(sel[:, k].rearrange("c t l -> c (t l)"),
                                                        cm[:, :, :].rearrange("c t l -> c (t l)"), float(k + 1),
                                                        st[:, :, :].rearrange("c t l -> c (t l)"),
                                                        ALU.is_equal, ALU.mult)
                    link(last)
                    assert links[0] == N_PICK
                    for t in range(2):
                        for half in range(2):
                            n = 2 * t + half
                            dve.wait_ge(s["picked_t"], n + 1)
                            for b, (lo, hi) in enumerate(HALVES):
                                last = dve.tensor_copy(
                                    r[lo:hi, t, b, 3 * half:3 * half + 3],
                                    psb[n % 2][lo:hi, 0:384].rearrange("c (s n) -> c s n", s=3))
                            last.then_inc(s["picked_copied"], 1)
                    dve.wait_ge(s["st_t"], 1)
                    for b, (lo, hi) in enumerate(HALVES):
                        last = dve.tensor_copy(st_t[lo:hi].rearrange("c a (n b) -> c a n b", b=2)[:, :, :, b],
                                               psb[2][lo:hi, 0:256].rearrange("c (n a) -> c a n", a=2))
                    last.then_inc(s["st_copied"], 1)
                    for n in range(8):
                        dve.wait_ge(s["gathered"], n + 1)
                        for a, (lo, hi) in enumerate(HALVES):
                            last = dve.tensor_copy(
                                feat[lo:hi, :, 32 * n:32 * (n + 1)].rearrange("c s (m b) -> c m b s", b=2),
                                psb[PROJ + n % 4][lo:hi, 0:384].rearrange("c (m b s a) -> c a m b s", b=2, s=TOP, a=2)[:, a])
                        last.then_inc(s["feat"], 1)
                    for t in range(4):
                        dve.wait_ge(s["rec_ps"], t + 1)
                        dve.tensor_copy(rec[:, t], psb[t % 2][:, 0:OUTDIM]).then_inc(s["rec"], 1)

                    def add(p):
                        for half in range(2):
                            dve.wait_ge(s["mixed"], 2 * p + half + 1)
                            v = x1[:, p, COLS * half:COLS * (half + 1)]
                            dve.tensor_tensor(v, v, psb[4 + half][:, :], ALU.add).then_inc(s["added"], 1)
                    add(0)
                    with dve.Fori(1, PAIRS) as p:
                        add(p)

                @block.scalar
                def _(act):
                    act.preload_act_table_set(EXP_LN)
                    for t in range(2):
                        act.wait_ge(s["rows"], t + 1)
                        act.activation(e[:, 2 * t:2 * t + 2], psb[t][:, 0:128].rearrange("c (b l) -> c b l", b=2),
                                       ACT.Exp).then_inc(s["exped"], 1)
                    act.wait_ge(s["w_in"], 16 * len(loads))
                    for m in range(4):
                        for a in range(2):
                            act.wait_ge(s["hid_ps"], 2 * m + a + 1)
                            act.activation(hid[:, m, 256 * a:256 * (a + 1)], psb[4 * a + m][0:MT, 0:256], ACT.Relu,
                                           bias=mb[:, m:m + 1]).then_inc(s["hid"], 1)

                @block.tensor
                def _(pe):
                    pe.wait_ge(s["own"], 1)
                    for t in range(2):
                        pe.transpose(psb[t][:, 0:128], scores[:, 8 * t:8 * t + 8].rearrange("c p g a -> c (p g a)"),
                                     ident).then_inc(s["rows"], 1)
                    pe.wait_ge(s["pick"], N_PICK)
                    pe.wait_ge(s["exped"], 2)
                    for t in range(2):
                        for half in range(2):
                            n = 2 * t + half
                            if n >= 2:
                                pe.wait_ge(s["picked_copied"], n - 1)
                            for k in range(3):
                                last = pe.transpose(psb[n % 2][:, 128 * k:128 * (k + 1)],
                                                    sel[:, 3 * half + k, 2 * t:2 * t + 2].rearrange("c b l -> c (b l)"),
                                                    ident)
                            last.then_inc(s["picked_t"], 1)
                    for t in range(2):
                        last = pe.transpose(psb[2][:, 128 * t:128 * (t + 1)],
                                            st[:, 2 * t:2 * t + 2].rearrange("c b l -> c (b l)"), ident)
                    last.then_inc(s["st_t"], 1)
                    pe.wait_ge(s["picked_copied"], 4)
                    pe.wait_ge(s["zero"], 3)
                    for n in range(8):
                        if n >= 4:
                            pe.wait_ge(s["feat"], n - 3)
                        for m in range(16):
                            p, gp = 2 * n + m // 8, m % 8
                            row = 16 * (p % 8) + 2 * gp
                            last = pe.matmul(psb[PROJ + n % 4][:, 24 * m:24 * (m + 1)], yt[:, p, gp],
                                             r[:, p // 8, :, :, row:row + 2], start=True, stop=True)
                        last.then_inc(s["gathered"], 1)
                    pe.wait_ge(s["feat"], 8)
                    pe.wait_ge(s["st_copied"], 1)
                    pe.wait_ge(s["w_in"], 16 * len(loads))
                    for m in range(4):
                        cols = slice(MT * m, MT * (m + 1))
                        for k in range(TOP):
                            for a, (lo, hi) in enumerate(HALVES):
                                pe.matmul(psb[4 * a + m][0:MT, 0:256], w1[lo:hi, k, cols], feat[lo:hi, k],
                                          start=(k == 0), stop=False)
                        for a in range(2):
                            pe.matmul(psb[4 * a + m][0:MT, 0:256], w1s[:, cols], st_t[:, a],
                                      start=False, stop=True).then_inc(s["hid_ps"], 1)
                    pe.wait_ge(s["hid"], 8)
                    for t in range(4):
                        if t >= 2:
                            pe.wait_ge(s["rec"], t - 1)
                        for m in range(4):
                            pe.matmul(psb[t % 2][:, 0:OUTDIM], hid[:, m, 128 * t:128 * (t + 1)], w2[:, m],
                                      start=(m == 0), stop=False)
                        pe.matmul(psb[t % 2][:, 0:OUTDIM], one[:, :], mb2r[:, :], start=False, stop=True)\
                          .then_inc(s["rec_ps"], 1)
                    pe.wait_ge(rec_in, 32)

                    def mix(p):
                        for half in range(2):
                            after(pe, s["added"], 2 * p - 1 + half)
                            for y in range(2):
                                blk = grid[:, p].rearrange("o (y x h w) -> o y h x w", y=4, x=4, h=8)[:, 2 * half + y]
                                last = pe.matmul(psb[4 + half][:, 256 * y:256 * (y + 1)], ow[:, :], blk,
                                                 start=True, stop=True)
                            last.then_inc(s["mixed"], 1)
                    mix(0)
                    with pe.Fori(1, PAIRS) as p:
                        mix(p)


N_PICK = 3 + 1 + 1 + 1 + (1 + 2 * (TOP - 1)) + 1 + 3 + 1


def shape_constants():
    rows = np.arange(128)
    ident = np.eye(128, dtype=np.float32)
    head = (rows[:, None] // DH == rows[None, :] // DH).astype(np.float32)
    image = (rows[:, None] // C == rows[None, :] // C).astype(np.float32)
    delta = ((rows[:, None] % C) // DH == np.arange(HEADS)[None, :]).astype(np.float32)
    at = np.arange(WS)
    coords = np.stack(np.meshgrid(at, at, indexing="ij"), 0).reshape(2, -1)
    rel = (coords[:, :, None] - coords[:, None, :]).reshape(2, -1).astype(np.float32)
    rel = (np.sign(rel) * np.log1p(np.abs(rel))).astype(np.float32).reshape(2, -1, COLS)
    mask = np.zeros((128, 4, 2, TOK), np.float32)
    for kind in range(4):
        for w in range(2):
            low = kind // 2 == 1
            right = kind % 2 == 1 and w == 1
            ty, tx = np.arange(TOK) // WS, np.arange(TOK) % WS
            region = 2 * (low & (ty >= WS - SHIFT)) + (right & (tx >= WS - SHIFT))
            differ = region[:, None] != region[None, :]
            mask[:, kind, w] = np.tile(np.where(differ, -100.0, 0.0), (2, 1))
    iota = np.tile(np.arange(TOK, dtype=np.float32), (128, 1))
    return {"c_consts": np.concatenate([ident, head, image, delta], axis=1), "c_rel": rel, "c_mask": mask,
            "c_iota": iota}


_L0 = ["qkv_w", "proj_w", "meta_w1", "meta_b1", "meta_w2", "meta_b2", "tau", "ffn_w1", "ffn_b1", "ffn_w2"]
_VECTORS = ["qkv_b", "proj_b", "ln1_g", "ln1_b", "ln2_g", "ln2_b", "ffn_b2"]
_L1 = ["conv_w", "W1", "b1", "W2", "b2", "out_w"]
_INS = ["x"] + [f"L0_conv_{n}" for n in _L0] + [f"L1_conv_{n}" for n in _L1]


def kernel(**inputs):
    import concourse.bacc as _bacc
    from concourse.bass_utils import run_bass_kernel_spmd as _run

    nc = _bacc.Bacc("TRN2", target_bir_lowering=False, num_devices=1)
    arrays, args = {}, []
    given = {name: np.asarray(inputs[name]) for name in _INS}
    vectors = {name: np.asarray(inputs[f"L0_conv_{name}"]) for name in _VECTORS}
    given["L0_conv_ffn_b1"] = given["L0_conv_ffn_b1"].reshape(2, 128).T
    vectors = np.concatenate([vectors[name].reshape(-1, C) for name in _VECTORS]).T
    vectors = np.ascontiguousarray(np.tile(vectors, (2, 1)))
    given["L1_conv_b1"] = given["L1_conv_b1"].reshape(4, MT).T
    given["L1_conv_conv_w"] = given["L1_conv_conv_w"].T
    given["L1_conv_out_w"] = given["L1_conv_out_w"].T
    given = {name: np.ascontiguousarray(a) for name, a in given.items()}
    for name, a in (given | {"c_vecs": vectors} | shape_constants()).items():
        arrays[f"in_{name}_dram"] = a
        args.append(nc.dram_tensor(f"in_{name}_dram", a.shape, mybir.dt.from_np(a.dtype), kind="ExternalInput").ap())
    args.append(nc.dram_tensor("rec_scratch", (512, OUTDIM), F32, kind="Internal").ap())
    args.append(nc.dram_tensor("bias_scratch", (HEADS, TOK * TOK), F32, kind="Internal").ap())
    args.append(nc.dram_tensor("out_0_dram", (B, C, H, W), F32, kind="ExternalOutput").ap())
    build(nc, *args)
    r = _run(nc, [arrays], core_ids=[0])
    return r.results[0]["out_0_dram"]
```

```python
from contextlib import ExitStack

import numpy as np

import concourse.bass as bass
from concourse import mybir

F32 = mybir.dt.float32
U32 = mybir.dt.uint32
ALU = mybir.AluOpType
ACT = mybir.ActivationFunctionType
X = mybir.AxisListType.X

B, C, H, W = 32, 64, 32, 32
PAIRS = B // 2
PIX = H * W
WS, SHIFT, HEADS = 8, 4, 4
DH = C // HEADS
TOK = WS * WS
UNITS = 2 * PAIRS
COLS = 512
WIN = 8
DUOS = 4 * UNITS
FFN = 4 * C
META = 128
SPAN = 2 * WS - 1
NORM_FLOOR = 1e-18
HALVES = ((0, 64), (64, 128))
ACT_HEADS, POOL_HEADS = range(0, 3), range(3, 4)
EXP_LN = "natural_log_exp_and_others"

BLOCKS = 16
TOP = 6
OC = C // 10 + 1
INDIM = TOP * C + TOK
MT = INDIM // 4
OUTDIM = TOK * OC


def after(eng, sem, count, limit=None):
    if isinstance(count, int):
        if limit is not None:
            count = min(count, limit)
        if count <= 0:
            return
    eng.wait_ge(sem, count)


def there(index, limit):
    return not isinstance(index, int) or 0 <= index < limit


def build(nc, x, qkv_w, proj_w, meta_w1, meta_b1, meta_w2, meta_b2, tau, ffn_w1, ffn_b1, ffn_w2,
          conv_w, mlp_w1, mlp_b1, mlp_w2, mlp_b2, out_w, c_vecs, c_consts, c_rel, c_mask, c_iota,
          rec_dram, bias_dram, out):
    with ExitStack() as whole:
        def sb(stack, name, shape, dt=F32):
            return stack.enter_context(nc.sbuf_tensor(name, shape, dt))

        def ps(stack, name, shape):
            return stack.enter_context(nc.psum_tensor(name, shape, F32))

        def sem(stack, name):
            return stack.enter_context(nc.semaphore(name))

        xs = sb(whole, "xs", [128, PAIRS, PIX])
        consts = sb(whole, "consts", [128, 3 * 128 + HEADS])
        ident, sum_head, sum_image = (consts[:, 128 * n:128 * (n + 1)] for n in range(3))
        delta = consts[:, 3 * 128:]
        vecs = sb(whole, "vecs", [128, 9])
        bq, bk, bv, proj_bias, g1, b1, g2, b2, ffn_bias = (vecs[:, n:n + 1] for n in range(9))
        mean_image = sb(whole, "mean_image_sb", [128, 128])[:, :]
        mean_group = sb(whole, "mean_group", [128, 128])

        def columns(a):
            return a.rearrange("c (h w) -> c w h", w=W)

        def group_norm(stage, tag, src, dst, arrive):
            n = {k: sem(stage, f"{tag}_{k}") for k in
                 ("rowsum", "mean", "centred", "square", "sqsum", "var", "ln", "rstd", "normed")}
            sqsum = sb(stage, f"{tag}_sqsum_sb", [128, 2, W])
            lnvar = sb(stage, f"{tag}_lnvar_sb", [128, 2, W])
            rstd = sb(stage, f"{tag}_rstd_sb", [128, 2, W])
            square = sb(stage, f"{tag}_square_sb", [128, 2, PIX])
            rowsum = sb(stage, f"{tag}_rowsum_sb", [128, 2, W])
            mean_ps = [ps(stage, f"{tag}_mean_ps{k}", [128, COLS]) for k in range(2)]
            var_ps = [ps(stage, f"{tag}_var_ps{k}", [128, COLS]) for k in range(2)]

            def vector(eng, p, k):
                if there(p + 1, PAIRS):
                    arrive(eng, p + 1, 1 - k)
                    after(eng, n["mean"], p)
                    eng.tensor_reduce(rowsum[:, 1 - k], columns(src[:, p + 1]), X, ALU.add)\
                       .then_inc(n["rowsum"], 1)
                if there(p, PAIRS):
                    after(eng, n["mean"], p + 1)
                    eng.tensor_tensor(
                        dst[:, p].rearrange("c (h w) -> c h w", w=W),
                        src[:, p].rearrange("c (h w) -> c h w", w=W),
                        mean_ps[k][:, 0:W].unsqueeze(1).broadcast_to([128, H, W]),
                        ALU.subtract).then_inc(n["centred"], 1)
                if there(p - 1, PAIRS):
                    after(eng, n["square"], p)
                    after(eng, n["var"], p - 2)
                    eng.tensor_reduce(sqsum[:, 1 - k], columns(square[:, 1 - k]), X, ALU.add)\
                       .then_inc(n["sqsum"], 1)

            def tensor(eng, p, k):
                if there(p + 1, PAIRS):
                    after(eng, n["rowsum"], p + 2)
                    after(eng, n["centred"], p)
                    eng.matmul(mean_ps[1 - k][:, 0:W], mean_group[:, :], rowsum[:, 1 - k], start=True, stop=True)\
                       .then_inc(n["mean"], 1)
                if there(p - 1, PAIRS):
                    after(eng, n["sqsum"], p)
                    after(eng, n["ln"], p - 2)
                    eng.matmul(var_ps[1 - k][:, 0:W], mean_group[:, :], sqsum[:, 1 - k],
                               start=True, stop=True).then_inc(n["var"], 1)

            def scalar(eng, p, k):
                if there(p, PAIRS):
                    after(eng, n["centred"], p + 1)
                    after(eng, n["sqsum"], p - 1)
                    eng.activation(square[:, k], dst[:, p], ACT.Square).then_inc(n["square"], 1)
                if there(p - 1, PAIRS):
                    after(eng, n["var"], p)
                    after(eng, n["normed"], p - 2)
                    eng.activation(lnvar[:, 1 - k], var_ps[1 - k][:, 0:W], ACT.Ln, bias=eps[:, 0:1])\
                       .then_inc(n["ln"], 1)
                    eng.wait_ge(n["ln"], p)
                    eng.activation(rstd[:, 1 - k], lnvar[:, 1 - k], ACT.Exp, scale=-0.5)\
                       .then_inc(n["rstd"], 1)

            def pool(eng, p, k):
                if there(p, PAIRS):
                    after(eng, n["rstd"], p + 1)
                    after(eng, n["square"], p + 1)
                    v = dst[:, p].rearrange("c (h w) -> c h w", w=W)
                    eng.tensor_tensor(v, v, rstd[:, k].unsqueeze(1).broadcast_to([128, H, W]),
                                      ALU.mult).then_inc(n["normed"], 1)

            def run(eng, step, first=None, early=None):
                def two(i):
                    for k in range(2):
                        step(eng, 2 * i + k, k)
                step(eng, -1, 1)
                if first:
                    first(eng)
                two(0)
                two(1)
                if early:
                    early(eng)
                with eng.Fori(2, PAIRS // 2 - 1) as i:
                    two(i)
                two(PAIRS // 2 - 1)
                step(eng, PAIRS, 0)
                step(eng, PAIRS + 1, 1)

            return n, run, vector, tensor, scalar, pool, rstd

        fw1 = sb(whole, "fw1", [128, 2, 2, 128])
        fw2_in, fw2 = (sb(whole, n, [128, 2, C]) for n in ("fw2_in", "fw2"))
        fb1 = sb(whole, "fb1", [128, 2])
        forward_in = sem(whole, "forward_in")
        attention = whole.enter_context(ExitStack())
        eps = sb(whole, "eps", [128, 2])
        wqkv = sb(attention, "wqkv", [128, 3, 128])
        wq, wk, wv = (wqkv[:, n] for n in range(3))
        wp = sb(attention, "wp", [128, 128])
        bp = sb(attention, "bp", [128, 1])
        head_scale = sb(attention, "head_scale", [128, HEADS])
        bias_tab = sb(attention, "bias_tab", [128, 4, 2, HEADS, TOK])

        with ExitStack() as stage:
            consts_in = sem(stage, "consts_in")
            w_in = sem(stage, "w_in")
            meta_in = sem(stage, "meta_in")
            by_dist_ready = sem(stage, "by_dist_ready")
            by_dy_ready = sem(stage, "by_dy_ready")
            zeroed = sem(stage, "zeroed")
            chain = sem(stage, "chain")
            hid_ps_ready = sem(stage, "hid_ps_ready")
            hid_ready = sem(stage, "hid_ready")
            bias_ps_ready = sem(stage, "bias_ps_ready")
            bias_rows_ready = sem(stage, "bias_rows_ready")
            bias_out = sem(stage, "bias_out")
            bias_in = sem(stage, "bias_in")
            bp_mean = sem(stage, "bp_mean")
            x_in = [sem(stage, f"x_in{k}") for k in range(2)]
            pw = sb(stage, "pw", [128, C])
            small = sb(stage, "small", [128, 2])
            tau_sb = sb(stage, "tau_sb", [128, HEADS])
            rel = sb(stage, "rel", [2, SPAN * SPAN])
            mw1 = sb(stage, "mw1", [2, META])
            mb1 = sb(stage, "mb1", [META, 1])
            mw2 = sb(stage, "mw2", [META, HEADS])
            mb2 = sb(stage, "mb2", [HEADS, 1])
            mask = sb(stage, "mask", [128, 4, 2, TOK])
            hid = sb(stage, "hid", [META, SPAN * SPAN])
            by_dist = sb(stage, "by_dist", [HEADS, SPAN, SPAN])
            by_dy = sb(stage, "by_dy", [HEADS, SPAN, WS, WS])
            bias_rows = sb(stage, "bias_rows", [HEADS, WS, WS, WS, WS])
            bias_q = sb(stage, "bias_q", [128, HEADS, TOK])
            hid_ps = ps(stage, "hid_ps", [128, COLS])
            bias_ps = ps(stage, "bias_ps", [128, COLS])
            bp_ps = ps(stage, "bp_ps", [128, COLS])

            def column(v):
                return v.rearrange("(c a) -> c a", a=1)

            meta_loads = [(rel[:, :], c_rel), (mw1[:, :], meta_w1), (mb1[:, :], column(meta_b1)),
                          (mw2[:, :], meta_w2), (mb2[:, :], column(meta_b2))]
            loads = [(vecs[:, :], c_vecs)]
            for lo, hi in HALVES:
                loads += [(wqkv[lo:hi, :, lo:hi], qkv_w.rearrange("c (t n) -> c t n", t=3)), (pw[lo:hi, :], proj_w)]
            loads += [(mask[:, :, :, :], c_mask),
                      (tau_sb[:, :], tau.rearrange("(a n) -> a n", a=1).broadcast_to([128, HEADS]))]
            x_pairs = x.rearrange("(a p) c h w -> a c p (h w)", a=2)

            def x_arrives(eng, p, k):
                after(eng, x_in[k], ((p - k) // 2 + 1) * 32)

            n1, gn_run, gn_v, gn_t, gn_a, gn_p, _ = group_norm(stage, "gn1", xs, xs, x_arrives)

            def bias_tensor(pe):
                pe.wait_ge(hid_ready, 1)
                pe.matmul(bias_ps[0:HEADS, 0:SPAN * SPAN], mw2[:, :], hid[:, :], start=True, stop=True)\
                  .then_inc(bias_ps_ready, 1)

            def bias_scalar(act):
                act.wait_ge(hid_ps_ready, 1)
                act.activation(hid[:, :], hid_ps[:, 0:SPAN * SPAN], ACT.Relu, bias=mb1[:, 0:1]).then_inc(hid_ready, 1)
                act.wait_ge(bias_ps_ready, 1)
                act.activation(by_dist[:, :, :].rearrange("h y x -> h (y x)"), bias_ps[0:HEADS, 0:SPAN * SPAN],
                               ACT.Identity, bias=mb2[:, 0:1]).then_inc(by_dist_ready, 1)
                act.wait_ge(by_dist_ready, 1)
                for qx in range(WS):
                    first = WS - 1 - qx
                    last = act.activation(by_dy[:, :, qx], by_dist[:, :, first:first + WS], ACT.Copy)
                last.then_inc(by_dy_ready, 1)

            def bias_spread(act):
                act.wait_ge(by_dy_ready, 1)
                for qy in range(WS):
                    first = WS - 1 - qy
                    last = act.activation(bias_rows[:, qy].rearrange("h x v u -> h v x u"),
                                          by_dy[:, first:first + WS], ACT.Copy)
                last.then_inc(bias_rows_ready, 1)
                act.wait_ge(bias_rows_ready, 1)
                act.dma_start(bias_dram, bias_rows[:, :, :, :, :].rearrange("h q x v u -> h (q x v u)"))\
                   .then_inc(bias_out, 16)

            def weights_there(eng):
                eng.wait_ge(w_in, 16 * len(loads))

            def prepare_tensor(pe):
                weights_there(pe)
                pe.matmul(bp_ps[:, 0:1], mean_image, proj_bias, start=True, stop=True).then_inc(bp_mean, 1)

            with nc.Block() as block:
                @block.sync
                def _(sp):
                    def load_pair(i, k):
                        after(sp, x_in[k], 32 * i)
                        for a, (lo, hi) in enumerate(HALVES):
                            sp.dma_start(xs[lo:hi, 2 * i + k], x_pairs[a, :, 2 * i + k]).then_inc(x_in[k], 16)

                    sp.dma_start(consts[:, :], c_consts).then_inc(consts_in, 16)
                    load_pair(0, 0)
                    load_pair(0, 1)
                    with sp.Fori(1, PAIRS // 2) as i:
                        load_pair(i, 0)
                        load_pair(i, 1)
                    sp.wait_ge(bias_out, 16)
                    for lo, hi in HALVES:
                        sp.dma_start(bias_q[lo:hi], bias_dram.rearrange("h (q k) -> q h k", k=TOK)).then_inc(bias_in, 16)

                @block.scalar
                def _(act):
                    act.preload_act_table_set(EXP_LN)
                    for dst, src in meta_loads:
                        act.dma_start(dst, src).then_inc(meta_in, 16)
                    act.wait_ge(meta_in, 16 * len(meta_loads))
                    bias_scalar(act)
                    act.wait_ge(chain, 4)
                    gn_run(act, gn_a, early=bias_spread)

                @block.gpsimd
                def _(pool):
                    pool.memset(wqkv[:, :, :], 0.0)
                    pool.memset(wp[:, :], 0.0).then_inc(zeroed, 1)
                    pool.wait_ge(zeroed, 1)
                    for dst, src in loads:
                        pool.dma_start(dst, src).then_inc(w_in, 16)
                    gn_run(pool, gn_p)

                @block.vector
                def _(dve):
                    links = [0]

                    def link(ins):
                        links[0] += 1
                        ins.then_inc(chain, 1)
                        dve.wait_ge(chain, links[0])

                    link(dve.memset(eps[:, 0:1], 1e-5))
                    link(dve.memset(eps[:, 1:2], NORM_FLOOR))
                    dve.wait_ge(consts_in, 16)
                    link(dve.tensor_scalar(mean_image, sum_image, 1.0 / C, None, ALU.mult))
                    link(dve.tensor_scalar(mean_group[:, :], sum_image, 1.0 / (C * H), None, ALU.mult))

                    gn_run(dve, gn_v)
                    weights_there(dve)
                    link(dve.tensor_scalar(tau_sb[:, :], tau_sb[:, :], 0.01, None, ALU.max))
                    link(dve.reciprocal(tau_sb[:, :], tau_sb[:, :]))
                    link(dve.tensor_tensor(head_scale[:, :], tau_sb[:, :], delta, ALU.mult))
                    link(dve.tensor_reduce(small[:, 0:1], pw[:, :], X, ALU.add))
                    link(dve.tensor_scalar(small[:, 1:2], small[:, 0:1], -1.0 / C, None, ALU.mult))
                    for lo, hi in HALVES:
                        link(dve.tensor_scalar(wp[lo:hi, lo:hi], pw[lo:hi, :], small[lo:hi, 1:2], None, ALU.add))
                    dve.wait_ge(bp_mean, 1)
                    link(dve.tensor_tensor(bp[:, :], proj_bias, bp_ps[:, 0:1], ALU.subtract))
                    dve.wait_ge(bias_in, 32)
                    for kind in range(4):
                        for w in range(2):
                            last = dve.tensor_tensor(
                                bias_tab[:, kind, w], bias_q[:, :, :],
                                mask[:, kind, w].unsqueeze(1).broadcast_to([128, HEADS, TOK]), ALU.add)
                    link(last)

                @block.tensor
                def _(pe):
                    pe.wait_ge(meta_in, 16 * len(meta_loads))
                    pe.matmul(hid_ps[:, 0:SPAN * SPAN], mw1[:, :], rel[:, :], start=True, stop=True)\
                      .then_inc(hid_ps_ready, 1)
                    pe.wait_ge(chain, 4)
                    gn_run(pe, gn_t, first=bias_tensor, early=prepare_tensor)

        xu = xs[:, :, :].rearrange("c p (j n) -> c (p j) n", j=2)

        def gather_pieces(j):
            for wi in range(2):
                r = 16 * j + WS * wi + SHIFT
                rows = [(r, 0, WS)] if r + WS <= H else [(r, 0, H - r), (0, H - r, WS)]
                for r0, t0, t1 in rows:
                    yield r0, 4, wi, t0, t1, 0, 3, 0, 8
                    yield r0, 28, wi, t0, t1, 3, 4, 0, 4
                    yield r0, 0, wi, t0, t1, 3, 4, 4, 8

        def piece(image, windows, r0, c0, wi, t0, t1, w0, w1, x0, x1):
            img = image.rearrange("c (h w) -> c h w", w=W)[:, r0:r0 + t1 - t0, c0:c0 + (w1 - w0) * (x1 - x0)]
            win = windows.rearrange("c (i j y x) -> c i y j x", i=2, j=4, y=WS)[:, wi, t0:t1, w0:w1, x0:x1]
            return img.rearrange("c h (j x) -> c h j x", x=x1 - x0), win

        forward_loads = [(fw1[lo:hi, a], ffn_w1.rearrange("c (m h) -> c m h", m=2)) for a, (lo, hi) in enumerate(HALVES)]
        forward_loads += [(fw2_in[:, :, :], ffn_w2.rearrange("(m h) c -> h m c", m=2)), (fb1[:, :], ffn_b1)]

        with ExitStack() as stage:
            s = {k: sem(stage, k) for k in (
                "xw_ready", "q_ps_ready", "k_ps_ready", "q_ready", "q_sq_ready", "k_ready", "k_sq_ready",
                "q_norm_ps", "k_norm_ps", "q_ln", "k_ln", "q_rnorm", "k_rnorm", "q_spread", "k_scaled",
                "k_spread", "k_spread_b", "scaled", "xw_saved", "v_ps_ready", "v_spread", "heads_copied", "proj_ps", "centred",
                "var_ps_ready", "var_ln", "rstd_ready", "normed", "skip_ready",
                "scores", "biased", "row_max", "shifted", "exped", "row_sum", "row_recip", "probs",
                "probs_t", "probs_t_copied", "mixed")}
            xw = [sb(stage, f"xw{j}", [128, COLS]) for j in range(2)]
            q_sb, k_sb = ([sb(stage, f"{n}{j}", [128, COLS]) for j in range(2)] for n in ("q_sb", "k_sb"))
            q_sq, k_sq, rq, rk = (sb(stage, n, [128, COLS]) for n in ("q_sq", "k_sq", "rq", "rk"))
            qd = [sb(stage, f"qd{j}", [128, WIN, 2, TOK]) for j in range(2)]
            kx = [sb(stage, f"kx{j}", [128, WIN, HEADS, TOK]) for j in range(2)]
            vd = [sb(stage, f"vd{j}", [128, WIN, 4, 2 * DH]) for j in range(2)]
            sc = sb(stage, "sc", [128, 8, 2, HEADS, TOK])
            pt = [sb(stage, f"pt{k}", [128, 4, 128]) for k in range(2)]
            mx = sb(stage, "mx", [128, 2, 2 * HEADS])
            sm = sb(stage, "sm", [128, 2, 2 * HEADS])
            rs8 = sb(stage, "rs8", [128, 2, 2 * HEADS])
            ob, csq, rs = (sb(stage, n, [128, COLS]) for n in ("ob", "csq", "rs"))
            cc = [sb(stage, f"cc{j}", [128, COLS]) for j in range(2)]
            s_ps = [ps(stage, f"s_ps{k}", [128, 2, HEADS, TOK]) for k in range(2)]
            t_ps = [ps(stage, f"t_ps{k}", [128, 4, 128]) for k in range(2)]
            o_ps = ps(stage, "o_ps", [128, COLS])
            qn_ps = ps(stage, "qn_ps", [128, COLS])
            kn_ps = ps(stage, "kn_ps", [128, COLS])
            vv_ps = ps(stage, "vv_ps", [128, COLS])
            zero = sem(stage, "zero")
            forward_zero = sem(stage, "forward_zero")

            def units(eng, slot):
                def both(i):
                    for j in range(2):
                        for q in range(4):
                            slot(eng, 2 * i + j, j, q, 8 * i + 4 * j + q)
                for i in (-1, 0, 1):
                    both(i)
                with eng.Fori(2, PAIRS - 1) as i:
                    both(i)
                for i in (PAIRS - 1, PAIRS, PAIRS + 1):
                    both(i)

            def tensor_slot(pe, u, j, q, g):
                if q == 0 and there(u, UNITS):
                    after(pe, s["xw_ready"], u + 1)
                    after(pe, s["v_spread"], u)
                    after(pe, s["var_ln"], u - 2, UNITS)
                    for t in range(4):
                        last = pe.matmul(vv_ps[:, 128 * t:128 * (t + 1)], xw[j][:, 128 * t:128 * (t + 1)],
                                         wv, start=True, stop=True)
                    last.then_inc(s["v_ps_ready"], 1)
                n = g - 5
                if there(n, DUOS):
                    m = (q - 1) % 4
                    jn = j if q == 0 else 1 - j
                    after(pe, s["probs_t_copied"], n + 1)
                    if m == 0:
                        after(pe, s["v_spread"], u)
                        after(pe, s["heads_copied"], u - 1)
                    for w in range(2):
                        for a in range(2):
                            for hp in range(2):
                                at = 2 * a + hp
                                win = 2 * m + w
                                last = pe.matmul(
                                    o_ps[32 * at:32 * at + 32, TOK * win:TOK * (win + 1)],
                                    vd[jn][:, win, at], pt[(q + 1) % 2][:, 2 * w + hp, TOK * a:TOK * (a + 1)],
                                    start=True, stop=True)
                    last.then_inc(s["mixed"], 1)
                if q == 1 and there(u + 2, UNITS):
                    after(pe, s["xw_ready"], u + 3)
                    after(pe, s["q_ln"], u + 2)
                    pe.matmul(qn_ps[:, :], wq, xw[j][:, :], start=True, stop=True).then_inc(s["q_ps_ready"], 1)
                    after(pe, s["k_ln"], u + 2)
                    pe.matmul(kn_ps[:, :], wk, xw[j][:, :], start=True, stop=True).then_inc(s["k_ps_ready"], 1)
                if q == 2 and there(u - 2, UNITS):
                    after(pe, s["q_ready"], u + 3, UNITS)
                    after(pe, s["heads_copied"], u - 1)
                    pe.matmul(qn_ps[:, :], wp[:, :], ob[:, :], start=True, stop=True).then_inc(s["proj_ps"], 1)
                if q == 3 and there(u - 2, UNITS):
                    after(pe, s["v_spread"], u + 1, UNITS)
                    after(pe, s["centred"], u - 1)
                    pe.matmul(vv_ps[:, :], mean_image, csq[:, :], start=True, stop=True)\
                      .then_inc(s["var_ps_ready"], 1)
                if q == 3 and there(u + 2, UNITS):
                    after(pe, s["q_sq_ready"], u + 3)
                    after(pe, s["centred"], u - 1)
                    pe.matmul(qn_ps[:, :], sum_head, q_sq[:, :], start=True, stop=True).then_inc(s["q_norm_ps"], 1)
                n = g - 3
                if there(n, DUOS):
                    after(pe, s["probs"], n + 1)
                    after(pe, s["probs_t_copied"], n - 1)
                    for w in range(2):
                        for hp in range(2):
                            last = pe.transpose(
                                t_ps[(q + 1) % 2][:, 2 * w + hp],
                                sc[:, (4 * j + q - 3) % 8, w, 2 * hp:2 * hp + 2].rearrange("c h k -> c (h k)"),
                                ident)
                    last.then_inc(s["probs_t"], 1)
                n = g + 1
                if there(n, DUOS):
                    m = (q + 1) % 4
                    jn = j if q < 3 else 1 - j
                    after(pe, s["biased"], n - 1)
                    if m == 0:
                        after(pe, s["q_spread"], u + 2)
                        after(pe, s["k_spread"], u + 2)
                        after(pe, s["k_spread_b"], u + 2)
                    for w in range(2):
                        last = pe.matmul(s_ps[(q + 1) % 2][:, w], qd[jn][:, 2 * m + w],
                                         kx[jn][:, 2 * m + w], start=True, stop=True)
                    last.then_inc(s["scores"], 1)
                if q == 2 and there(u + 2, UNITS):
                    after(pe, s["k_sq_ready"], u + 3)
                    pe.matmul(kn_ps[:, :], sum_head, k_sq[:, :], start=True, stop=True).then_inc(s["k_norm_ps"], 1)

            def spread_keys(eng, put, u, j, heads, done):
                after(eng, s["k_scaled"], u + 2)
                after(eng, s["scores"], 4 * u)
                for h in heads:
                    last = put(kx[1 - j][:, :, h], k_sb[1 - j][:, :].rearrange("c (w k) -> c w k", k=TOK), h)
                last.then_inc(s[done], 1)

            def scalar_slot(act, u, j, q, g):
                n = g - 4
                if there(n, DUOS):
                    after(act, s["probs_t"], n + 1)
                    after(act, s["mixed"], n - 1)
                    act.activation(pt[q % 2][:, :, :], t_ps[q % 2][:, :, :], ACT.Copy)\
                       .then_inc(s["probs_t_copied"], 1)
                n = g - 1
                if there(n, DUOS):
                    after(act, s["shifted"], n + 1)
                    t = sc[:, (4 * j + q - 1) % 8]
                    act.activation(t, t, ACT.Exp).then_inc(s["exped"], 1)
                if q == 0 and there(u - 2, UNITS):
                    after(act, s["mixed"], 4 * u - 4)
                    after(act, s["proj_ps"], u - 2)
                    act.activation(ob[:, :], o_ps[:, :], ACT.Identity, bias=bv).then_inc(s["heads_copied"], 1)
                if q == 0 and there(u + 1, UNITS):
                    after(act, s["q_norm_ps"], u + 2)
                    after(act, s["q_spread"], u + 1)
                    act.activation(rq[:, :], qn_ps[:, :], ACT.Ln, bias=eps[:, 1:2]).then_inc(s["q_ln"], 1)
                    after(act, s["k_norm_ps"], u + 2)
                    after(act, s["k_scaled"], u + 1)
                    act.activation(rk[:, :], kn_ps[:, :], ACT.Ln, bias=eps[:, 1:2]).then_inc(s["k_ln"], 1)
                    act.wait_ge(s["q_ln"], u + 2)
                    act.activation(rq[:, :], rq[:, :], ACT.Exp, scale=-0.5).then_inc(s["q_rnorm"], 1)
                    act.wait_ge(s["k_ln"], u + 2)
                    act.activation(rk[:, :], rk[:, :], ACT.Exp, scale=-0.5).then_inc(s["k_rnorm"], 1)
                if q == 1 and there(u + 2, UNITS):
                    after(act, s["q_ps_ready"], u + 3)
                    after(act, s["q_spread"], u + 1)
                    act.activation(q_sb[j][:, :], qn_ps[:, :], ACT.Identity, bias=bq).then_inc(s["q_ready"], 1)
                    after(act, s["k_ps_ready"], u + 3)
                    after(act, s["k_spread"], u + 1)
                    after(act, s["k_spread_b"], u + 1)
                    act.activation(k_sb[j][:, :], kn_ps[:, :], ACT.Identity, bias=bk).then_inc(s["k_ready"], 1)
                    act.wait_ge(s["q_ready"], u + 3)
                    after(act, s["q_norm_ps"], u + 2)
                    act.activation(q_sq[:, :], q_sb[j][:, :], ACT.Square).then_inc(s["q_sq_ready"], 1)
                if q == 2 and there(u - 2, UNITS):
                    after(act, s["proj_ps"], u - 1)
                    after(act, s["var_ps_ready"], u - 2)
                    act.activation(csq[:, :], qn_ps[:, :], ACT.Square, bias=bp[:, 0:1])
                    after(act, s["normed"], u - 3)
                    act.activation(cc[j][:, :], qn_ps[:, :], ACT.Identity, bias=bp[:, 0:1]).then_inc(s["centred"], 1)
                if q == 2 and there(u + 1, UNITS):
                    spread_keys(act, lambda out, keys, h: act.activation(
                        out, keys, ACT.Identity, scale=head_scale[:, h:h + 1]), u, j, ACT_HEADS, "k_spread")
                if q == 3 and there(u - 2, UNITS):
                    after(act, s["var_ps_ready"], u - 1)
                    after(act, s["scaled"], u - 2)
                    act.activation(rs[:, :], vv_ps[:, :], ACT.Ln, bias=eps[:, 0:1]).then_inc(s["var_ln"], 1)
                    act.wait_ge(s["var_ln"], u - 1)
                    act.activation(rs[:, :], rs[:, :], ACT.Exp, scale=-0.5).then_inc(s["rstd_ready"], 1)
                if q == 3 and there(u + 1, UNITS):
                    after(act, s["xw_ready"], u + 3 if j == 1 else u + 2, UNITS)
                    act.activation(xu[:, u + 1], xw[1 - j][:, :], ACT.Identity, bias=b1).then_inc(s["xw_saved"], 1)

            def vector_slot(dve, u, j, q, g):
                n = g - 1
                if there(g, DUOS):
                    kind = 2 * (j == 1 and q // 2 == 1) + q % 2
                    after(dve, s["scores"], g + 1)
                    after(dve, s["probs_t"], g - 7)
                    dve.tensor_tensor(sc[:, 4 * j + q], s_ps[q % 2][:, :, :, :], bias_tab[:, kind], ALU.add)\
                       .then_inc(s["biased"], 1)
                if there(g, DUOS):
                    dve.wait_ge(s["biased"], g + 1)
                    after(dve, s["shifted"], g - 1)
                    dve.tensor_reduce(mx[:, q % 2], sc[:, 4 * j + q].rearrange("c w h k -> c (w h) k"), X, ALU.max)\
                       .then_inc(s["row_max"], 1)
                if q == 0 and there(u + 2, UNITS):
                    after(dve, s["v_ps_ready"], u + 1)
                    after(dve, s["xw_saved"], u + 1)
                    pair = (u + 2) // 2 if isinstance(u, int) else (u - j) // 2 + 1
                    for pc in gather_pieces(j):
                        img, win = piece(xs[:, pair], xw[j][:, :], *pc)
                        last = dve.tensor_copy(win, img)
                    last.then_inc(s["xw_ready"], 1)
                if there(n, DUOS):
                    after(dve, s["exped"], n + 1)
                    after(dve, s["row_recip"], n - 1)
                    dve.tensor_reduce(sm[:, (q - 1) % 2], sc[:, (4 * j + q - 1) % 8].rearrange("c w h k -> c (w h) k"),
                                      X, ALU.add).then_inc(s["row_sum"], 1)
                if q == 3 and there(u - 3, UNITS):
                    after(dve, s["xw_saved"], u - 2)
                    after(dve, s["scaled"], u - 2)
                    dve.scalar_tensor_tensor(xu[:, u - 3], cc[1 - j][:, :], g1, xu[:, u - 3], ALU.mult, ALU.add)\
                       .then_inc(s["normed"], 1)
                if q == 1 and there(u, UNITS):
                    after(dve, s["v_ps_ready"], u + 1)
                    after(dve, s["mixed"], 4 * u - 4)
                    vps = vv_ps[:, :].rearrange("c (t a d) -> c t a d", t=4, a=4)
                    for par in range(2):
                        for h2 in range(2):
                            last = dve.tensor_copy(
                                vd[j][64 * h2:64 * h2 + 64, par:WIN:2, :, DH * h2:DH * (h2 + 1)],
                                vps[64 * par:64 * par + 64, :, :, DH * h2:DH * (h2 + 1)])
                    last.then_inc(s["v_spread"], 1)
                if q == 1 and there(u + 1, UNITS):
                    after(dve, s["k_ready"], u + 2)
                    after(dve, s["k_sq_ready"], u + 2)
                    after(dve, s["k_rnorm"], u + 2)
                    dve.tensor_tensor(k_sb[1 - j][:, :], k_sb[1 - j][:, :], rk[:, :], ALU.mult).then_inc(s["k_scaled"], 1)
                if q == 2 and there(u + 1, UNITS):
                    if isinstance(u, int) and u == -1:
                        dve.wait_ge(zero, 1)
                    after(dve, s["q_ready"], u + 2)
                    after(dve, s["q_rnorm"], u + 2)
                    after(dve, s["scores"], 4 * u)
                    for a, (lo, hi) in enumerate(HALVES):
                        last = dve.tensor_tensor(qd[1 - j][lo:hi, :, a],
                                                 q_sb[1 - j][lo:hi, :].rearrange("c (w k) -> c w k", k=TOK),
                                                 rq[lo:hi, :].rearrange("c (w k) -> c w k", k=TOK), ALU.mult)
                    last.then_inc(s["q_spread"], 1)
                if there(n, DUOS):
                    dve.wait_ge(s["row_sum"], n + 1)
                    after(dve, s["probs"], n - 1)
                    dve.reciprocal(rs8[:, (q - 1) % 2], sm[:, (q - 1) % 2]).then_inc(s["row_recip"], 1)

            def pool_slot(pool, u, j, q, g):
                n = g - 2
                if there(n, DUOS):
                    after(pool, s["row_recip"], n + 1)
                    t = sc[:, (4 * j + q - 2) % 8].rearrange("c w h k -> c (w h) k")
                    pool.tensor_tensor(t, t, rs8[:, q % 2].unsqueeze(2).broadcast_to([128, 2 * HEADS, TOK]),
                                       ALU.mult).then_inc(s["probs"], 1)
                if q == 2 and there(u + 1, UNITS):
                    spread_keys(pool, lambda out, keys, h: pool.tensor_tensor(
                        out, keys, head_scale[:, h:h + 1].unsqueeze(2).broadcast_to([128, WIN, TOK]), ALU.mult),
                        u, j, POOL_HEADS, "k_spread_b")
                if there(g, DUOS):
                    after(pool, s["row_max"], g + 1)
                    t = sc[:, 4 * j + q].rearrange("c w h k -> c (w h) k")
                    pool.tensor_tensor(t, t, mx[:, q % 2].unsqueeze(2).broadcast_to([128, 2 * HEADS, TOK]),
                                       ALU.subtract).then_inc(s["shifted"], 1)
                if q == 0 and there(u - 3, UNITS):
                    after(pool, s["rstd_ready"], u - 2)
                    pool.tensor_tensor(cc[1 - j][:, :], cc[1 - j][:, :], rs[:, :], ALU.mult).then_inc(s["scaled"], 1)
                if q == 1 and there(u + 2, UNITS):
                    after(pool, s["k_ready"], u + 3)
                    after(pool, s["k_norm_ps"], u + 2)
                    pool.tensor_tensor(k_sq[:, :], k_sb[j][:, :], k_sb[j][:, :], ALU.mult).then_inc(s["k_sq_ready"], 1)

            with nc.Block() as block:
                @block.tensor
                def _(pe):
                    units(pe, tensor_slot)

                @block.scalar
                def _(act):
                    act.preload_act_table_set(EXP_LN)
                    units(act, scalar_slot)

                @block.vector
                def _(dve):
                    units(dve, vector_slot)

                @block.sync
                def _(sp):
                    sp.wait_ge(forward_zero, 1)
                    for dst, src in forward_loads:
                        sp.dma_start(dst, src).then_inc(forward_in, 16)

                @block.gpsimd
                def _(pool):
                    for operand in (*qd, *vd):
                        last = pool.memset(operand[:, :, :, :], 0.0)
                    last.then_inc(zero, 1)
                    pool.memset(fw1[:, :, :, :], 0.0).then_inc(forward_zero, 1)
                    units(pool, pool_slot)
        attention.close()

        TURN = 128 + 4
        turn = sb(whole, "turn", [128, 8, TURN])
        cw_in = sb(whole, "cw_in", [128, BLOCKS])
        sqsums = sb(whole, "sqsums", [128, PAIRS, W])

        x1 = sb(whole, "x1", [128, PAIRS, PIX])
        with ExitStack() as stage:
            s = {k: sem(stage, "f_" + k) for k in (
                "w_in", "zero", "chain", "rowsum", "mean_ps", "less_mean", "square", "last_square", "sqsum", "hid_ps",
                "gelu", "out_ps", "centred", "var_ps", "ln", "rstd", "normed",
                "update", "skipped", "b2_mean", "x_biased", "done")}
            FORWARD_LINKS = 4
            x_back = [sem(stage, f"x_back{k}") for k in range(2)]
            fsum = sb(stage, "fsum", [128, 2, 2])
            fb2 = sb(stage, "fb2", [128, 1])
            rowsum = sb(stage, "rowsum", [128, PAIRS, W])
            square = sb(stage, "square", [128, 2, PIX])
            hs = sb(stage, "hs", [128, 2, 4, COLS])
            cc = sb(stage, "fcc", [128, 4, COLS])
            csq = sb(stage, "fcsq", [128, 2, COLS])
            rs = sb(stage, "frs", [128, 2, COLS])
            upd = sb(stage, "upd", [128, 2, COLS])
            xr = sb(stage, "xr", [128, 2, PIX])
            h_ps = [ps(stage, f"h_ps{m}", [128, COLS]) for m in range(4)]
            c_ps = ps(stage, "c_ps", [128, COLS])
            mean_ps = ps(stage, "mean_ps", [128, COLS])
            v_ps = [ps(stage, f"v_ps{m}", [128, COLS]) for m in range(2)]

            def steps(eng, step):
                def four(i):
                    for k in range(4):
                        step(eng, 4 * i + k, k, 2 * i)
                four(0)
                four(1)
                with eng.Fori(2, UNITS // 4 - 1) as i:
                    four(i)
                for i in range(UNITS // 4 - 1, UNITS // 4 + 2):
                    four(i)

            def tensor_step(pe, u, k, pairs):
                if there(u, UNITS):
                    for m in range(4):
                        after(pe, s["gelu"], 4 * u - 3 + m)
                        pe.matmul(h_ps[m][:, :], fw1[:, m % 2, m // 2], xu[:, u], start=True, stop=True).then_inc(s["hid_ps"], 1)
                if there(u - 1, UNITS):
                    after(pe, s["centred"], u - 1)
                    if isinstance(u, int) and u == 1:
                        pe.wait_ge(s["chain"], FORWARD_LINKS)
                    for m in range(4):
                        after(pe, s["gelu"], 4 * u - 3 + m)
                        lo, hi = HALVES[m % 2]
                        last = pe.matmul(c_ps[lo:hi, :], fw2[:, m // 2], hs[:, (k - 1) % 2, m],
                                         start=(m < 2), stop=(m >= 2))
                    last.then_inc(s["out_ps"], 1)
                if there(u - 2, UNITS):
                    after(pe, s["centred"], u - 1)
                    after(pe, s["ln"], u - 3)
                    pe.matmul(v_ps[k % 2][:, :], mean_image, csq[:, k % 2], start=True, stop=True)\
                      .then_inc(s["var_ps"], 1)
                if k % 2 == 1 and there(u - 5, UNITS):
                    pair = pairs + (k - 5) // 2
                    after(pe, s["rowsum"], pair + 1)
                    after(pe, s["less_mean"], pair)
                    pe.matmul(mean_ps[:, 0:W], mean_group[:, :], rowsum[:, pair], start=True, stop=True)\
                      .then_inc(s["mean_ps"], 1)

            def scalar_step(act, u, k, pairs):
                if there(u, UNITS):
                    for m in range(4):
                        after(act, s["hid_ps"], 4 * u + m + 1)
                        after(act, s["out_ps"], u - 1)
                        act.activation(hs[:, k % 2, m], h_ps[m][:, :], ACT.Gelu, bias=fb1[:, m // 2:m // 2 + 1])\
                           .then_inc(s["gelu"], 1)
                if there(u - 1, UNITS):
                    after(act, s["out_ps"], u)
                    after(act, s["update"], u - 4)
                    act.activation(cc[:, (k - 1) % 4], c_ps[:, :], ACT.Identity, bias=fb2[:, 0:1])
                    after(act, s["var_ps"], u - 2)
                    act.activation(csq[:, (k - 1) % 2], c_ps[:, :], ACT.Square, bias=fb2[:, 0:1])\
                       .then_inc(s["centred"], 1)
                if k % 2 == 1 and there(u - 3, UNITS):
                    act.preload_act_table_set(EXP_LN)
                    for d in (3, 2):
                        after(act, s["var_ps"], u - d + 1)
                        after(act, s["normed"], u - d - 1)
                        act.activation(rs[:, (k - d) % 2], v_ps[(k - d) % 2][:, :], ACT.Ln, bias=eps[:, 0:1])\
                           .then_inc(s["ln"], 1)
                    for d in (3, 2):
                        act.wait_ge(s["ln"], u - d + 1)
                        act.activation(rs[:, (k - d) % 2], rs[:, (k - d) % 2], ACT.Exp, scale=-0.5)\
                           .then_inc(s["rstd"], 1)

            def vector_step(dve, u, k, pairs):
                if k % 2 == 1 and there(u - 3, UNITS):
                    for d in (3, 2):
                        after(dve, s["rstd"], u - d + 1)
                        dve.tensor_tensor(cc[:, (k - d) % 4], cc[:, (k - d) % 4], rs[:, (k - d) % 2], ALU.mult)\
                           .then_inc(s["normed"], 1)
                    for d in (3, 2):
                        dve.wait_ge(s["normed"], u - d + 1)
                        after(dve, s["skipped"], u - d - 1)
                        dve.scalar_tensor_tensor(upd[:, (k - d) % 2], cc[:, (k - d) % 4], g2, xu[:, u - d],
                                                 ALU.mult, ALU.add).then_inc(s["update"], 1)
                    pair = pairs + (k - 3) // 2
                    kp = ((k - 3) // 2) % 2
                    for d in (3, 2):
                        j = 3 - d
                        if j == 0:
                            after(dve, s["x_biased"], pair + 1)
                        dve.wait_ge(s["update"], u - d + 1)
                        for pc in gather_pieces(j):
                            img, win = piece(xr[:, kp], upd[:, (k - d) % 2], *pc)
                            dst, _ = piece(x1[:, pair], upd[:, (k - d) % 2], *pc)
                            last = dve.tensor_tensor(dst, img, win, ALU.add)
                        last.then_inc(s["skipped"], 1)
                    dve.wait_ge(s["skipped"], u - 1)
                    dve.tensor_reduce(rowsum[:, pair], columns(x1[:, pair]), X, ALU.add).then_inc(s["rowsum"], 1)
                if k % 2 == 0 and there(u - 6, UNITS):
                    pair = pairs + (k - 6) // 2
                    after(dve, s["mean_ps"], pair + 1)
                    if not isinstance(u, int):
                        after(dve, s["square"], pair)
                    dve.tensor_tensor(
                        xs[:, pair].rearrange("c (h w) -> c h w", w=W),
                        x1[:, pair].rearrange("c (h w) -> c h w", w=W),
                        mean_ps[:, 0:W].unsqueeze(1).broadcast_to([128, H, W]), ALU.subtract).then_inc(s["less_mean"], 1)
                if k % 2 == 0 and there(u - 8, UNITS):
                    pair = pairs + (k - 8) // 2
                    if isinstance(u, int) and pair == PAIRS - 1:
                        after(dve, s["last_square"], 1)
                    elif isinstance(u, int):
                        after(dve, s["square"], pair + 1)
                    dve.tensor_reduce(sqsums[:, pair], columns(square[:, ((k - 8) // 2) % 2]), X, ALU.add)\
                       .then_inc(s["sqsum"], 1)

            def sync_pair(sp, p, k):
                after(sp, s["skipped"], 2 * p - 2)
                for a, (lo, hi) in enumerate(HALVES):
                    sp.dma_start(xr[lo:hi, k], x_pairs[a, :, p]).then_inc(x_back[k], 16)

            def pool_pair(pool, i, k):
                p = 2 * i + k
                if there(p, PAIRS):
                    after(pool, x_back[k], 32 * (i + 1))
                    pool.tensor_tensor(xr[:, k], xr[:, k], b2.broadcast_to([128, PIX]), ALU.add)\
                        .then_inc(s["x_biased"], 1)
                if there(p - 2, PAIRS - 1):
                    after(pool, s["less_mean"], p - 1)
                    after(pool, s["sqsum"], p - 3)
                    pool.tensor_tensor(square[:, k], xs[:, p - 2], xs[:, p - 2], ALU.mult).then_inc(s["square"], 1)

            def in_pairs(eng, step, ends=0):
                step(0)
                step(1)
                with eng.Fori(2, PAIRS // 2) as i:
                    step(i)
                for i in range(ends):
                    step(PAIRS // 2 + i)

            with nc.Block() as block:
                @block.sync
                def _(sp):
                    for lo, hi in HALVES:
                        sp.dma_start(cw_in[lo:hi, :], conv_w).then_inc(s["w_in"], 16)
                    in_pairs(sp, lambda i: (sync_pair(sp, 2 * i, 0), sync_pair(sp, 2 * i + 1, 1)))

                @block.gpsimd
                def _(pool):
                    pool.memset(turn[:, :, :], 0.0).then_inc(s["zero"], 1)
                    pool.wait_ge(s["zero"], 1)
                    pool.wait_ge(s["w_in"], 32)
                    pool.tensor_copy(turn[:, :, 0:128], ident.unsqueeze(1).broadcast_to([128, 8, 128]))\
                        .then_inc(s["zero"], 1)
                    for a, (lo, hi) in enumerate(HALVES):
                        pool.wait_ge(s["zero"], 2 + a)
                        pool.tensor_copy(
                            turn[lo:hi, :, 128:TURN].rearrange("c g (b a) -> c g b a", a=2)[:, :, :, a],
                            cw_in[lo:hi, :].rearrange("c (g b) -> c g b", b=2)).then_inc(s["zero"], 1)
                    pool.wait_ge(s["zero"], 4)
                    in_pairs(pool, lambda i: (pool_pair(pool, i, 0), pool_pair(pool, i, 1)), ends=1)

                @block.vector
                def _(dve):
                    links = [0]

                    def link(ins):
                        links[0] += 1
                        ins.then_inc(s["chain"], 1)
                        dve.wait_ge(s["chain"], links[0])

                    dve.wait_ge(forward_in, 16 * len(forward_loads))
                    link(dve.tensor_reduce(fsum[:, :, 0], fw2_in[:, :, :], X, ALU.add))
                    link(dve.tensor_scalar(fsum[:, :, 1], fsum[:, :, 0], -1.0 / C, None, ALU.mult))
                    link(dve.tensor_tensor(fw2[:, :, :], fw2_in[:, :, :],
                                           fsum[:, :, 1].unsqueeze(2).broadcast_to([128, 2, C]), ALU.add))
                    dve.wait_ge(s["b2_mean"], 1)
                    link(dve.tensor_tensor(fb2[:, :], ffn_bias, c_ps[:, 0:1], ALU.subtract))
                    steps(dve, vector_step)

                @block.tensor
                def _(pe):
                    pe.wait_ge(forward_in, 16 * len(forward_loads))
                    pe.matmul(c_ps[:, 0:1], mean_image, ffn_bias, start=True, stop=True)\
                      .then_inc(s["b2_mean"], 1)
                    steps(pe, tensor_step)

                @block.scalar
                def _(act):
                    act.wait_ge(forward_in, 16 * len(forward_loads))
                    act.wait_ge(s["chain"], FORWARD_LINKS)
                    steps(act, scalar_step)
                    act.wait_ge(s["less_mean"], PAIRS)
                    act.wait_ge(s["sqsum"], PAIRS - 2)
                    act.activation(square[:, (PAIRS - 1) % 2], xs[:, PAIRS - 1], ACT.Square).then_inc(s["last_square"], 1)

        yt = xs[:, :, :].rearrange("c p (g n) -> c p g n", g=8)
        scores = sb(whole, "scores_sb", [128, PAIRS, 8, 2])
        raw_scores = sb(whole, "raw_scores", [128, PAIRS, 8, 2 * 2])
        tail_in = sem(whole, "tail_in")
        tail_zero = sem(whole, "tail_zero")
        w1 = sb(whole, "w1", [128, TOP // 2, INDIM])
        w1s = sb(whole, "w1s", [128, INDIM])
        w2 = sb(whole, "w2", [MT, 4, OUTDIM])
        mb = sb(whole, "mb", [MT, 4])
        mb2r = sb(whole, "mb2r", [128, OUTDIM])
        ow = sb(whole, "ow", [128, 128])
        iota = sb(whole, "iota", [128, TOK])
        PICKS = 32
        r = sb(whole, "r", [128, 2, 64, PICKS])
        st_t = sb(whole, "st_t", [128, 2, 256])
        tail_loads = [(iota[:, :], c_iota),
                      (w1[:, :, :], mlp_w1[0:TOP * C].rearrange("(s k) n -> k s n", k=2 * C)),
                      (w2[:, :, :], mlp_w2.rearrange("(m k) n -> k m n", k=MT)), (mb[:, :], mlp_b1),
                      (mb2r[:, :], mlp_b2.rearrange("(a n) -> a n", a=1).broadcast_to([128, OUTDIM]))]
        for a, (lo, hi) in enumerate(HALVES):
            tail_loads += [(w1s[lo:hi, :], mlp_w1[TOP * C:INDIM]), (ow[OC * a:OC * (a + 1), lo:hi], out_w)]

        with ExitStack() as stage:
            s = {k: sem(stage, "y_" + k) for k in
                 ("var_ps", "ln", "rstd", "scaled_a", "scaled_b", "turned", "turn_copied")}
            ynow = sb(stage, "ynow", [128, 2, PIX])
            rstd = sb(stage, "rstd", [128, PAIRS, W])
            turn_ps = [ps(stage, f"turn_ps{k}", [128, 2, TURN]) for k in range(4)]
            var_ps = ps(stage, "var_ps", [128, COLS])

            POOL_ROWS, VECTOR_ROWS = range(0, 1), range(1, 4)

            def turns(eng, step):
                for p in range(2):
                    step(p, p)
                with eng.Fori(1, PAIRS // 2) as i:
                    step(2 * i, 0)
                    step(2 * i + 1, 1)

            def blocks(k, gp):
                return ynow[:, k, 128 * gp:128 * (gp + 1)]

            def scale(eng, p, k, rows_of_blocks, done):
                after(eng, s["turned"], 4 * (p - 1))
                shape = [128, 4, WS, WS]
                for gy in rows_of_blocks:
                    last = eng.tensor_tensor(
                        ynow[:, k].rearrange("c (y x h w) -> c y x h w", y=4, x=4, h=WS)[:, gy],
                        xs[:, p].rearrange("c (y h x w) -> c y x h w", y=4, x=4, h=WS)[:, gy],
                        rstd[:, p].rearrange("c (x w) -> c x w", x=4).unsqueeze(2).broadcast_to(shape), ALU.mult)
                last.then_inc(s[done], 1)

            def tensor_turn(pe, m, k):
                after(pe, s["scaled_a"], m + 1)
                after(pe, s["scaled_b"], m + 1)
                for b in range(4):
                    after(pe, s["turn_copied"], 4 * m - 3 + b)
                    for c in range(2):
                        last = pe.matmul(turn_ps[b][:, c], blocks(k, 2 * b + c), turn[:, 2 * b + c],
                                         start=True, stop=True)
                    last.then_inc(s["turned"], 1)

            def scalar_turn(act, m, k):
                for b in range(4):
                    after(act, s["turned"], 4 * m + 1 + b)
                    act.activation(yt[:, m, 2 * b:2 * b + 2], turn_ps[b][:, :, 0:128], ACT.Copy)
                    act.activation(raw_scores[:, m, 2 * b:2 * b + 2], turn_ps[b][:, :, 128:TURN], ACT.Copy)\
                       .then_inc(s["turn_copied"], 1)

            with nc.Block() as block:
                @block.sync
                def _(sp):
                    sp.wait_ge(tail_zero, 1)
                    for dst, src in tail_loads:
                        sp.dma_start(dst, src).then_inc(tail_in, 16)

                @block.gpsimd
                def _(pool):
                    pool.memset(ow[:, :], 0.0).then_inc(tail_zero, 1)
                    pool.memset(st_t[:, :, :], 0.0)
                    pool.memset(r[:, 0], 0.0)
                    pool.wait_ge(s["rstd"], 1)
                    turns(pool, lambda p, k: scale(pool, p, k, POOL_ROWS, "scaled_a"))
                    pool.memset(r[:, 1], 0.0).then_inc(tail_zero, 1)

                @block.vector
                def _(dve):
                    dve.wait_ge(s["rstd"], 1)
                    turns(dve, lambda p, k: scale(dve, p, k, VECTOR_ROWS, "scaled_b"))

                @block.scalar
                def _(act):
                    act.preload_act_table_set(EXP_LN)
                    every = rstd[:, :, :].rearrange("c p w -> c (p w)")
                    act.wait_ge(s["var_ps"], 1)
                    act.activation(every, var_ps[:, :], ACT.Ln, bias=eps[:, 0:1]).then_inc(s["ln"], 1)
                    act.wait_ge(s["ln"], 1)
                    act.activation(every, every, ACT.Exp, scale=-0.5).then_inc(s["rstd"], 1)
                    turns(act, lambda p, k: scalar_turn(act, p, k))

                @block.tensor
                def _(pe):
                    pe.matmul(var_ps[:, :], mean_group[:, :], sqsums[:, :, :].rearrange("c p w -> c (p w)"),
                              start=True, stop=True).then_inc(s["var_ps"], 1)
                    turns(pe, lambda p, k: tensor_turn(pe, p, k))

        with ExitStack() as stage:
            s = {k: sem(stage, "t_" + k) for k in (
                "own", "rows", "exped", "pick", "picked_t", "picked_a", "picked_b", "st_t", "st_copied", "gathered",
                "gathered_copied", "feat_ps", "feat_a", "feat_b", "hid_ps", "hid", "rec_ps", "rec", "mixed",
                "added", "stored")}
            rec_out = [sem(stage, f"rec_out{h}") for h in range(2)]
            rec_in = [sem(stage, f"rec_in{h}") for h in range(2)]
            e = sb(stage, "e", [128, 4, TOK])
            pr, st, cm = (sb(stage, n, [128, 4, TOK]) for n in ("pr", "st", "cm"))
            esum = sb(stage, "esum", [128, 4])
            top = sb(stage, "top", [128, 4, 8])
            tidx = sb(stage, "tidx", [128, 4, 8], U32)
            tidf = sb(stage, "tidf", [128, 4, 8])
            zeros = sb(stage, "zeros", [128, TOK])
            sel = sb(stage, "sel", [128, TOP, 4, TOK])
            picked = [sb(stage, f"picked{k}", [128, 4, 128]) for k in range(2)]
            feat = sb(stage, "feat", [128, TOP // 2, 2, 256])
            hid = sb(stage, "mlp_hid", [MT, 4, COLS])
            rec = r[:, :, :, :].rearrange("c t n x -> c (t n x)")[:, 0:4 * OUTDIM].rearrange("c (t n) -> c t n", t=4)
            grid = yt.rearrange("o p g n -> o p (g n)")
            psb = [ps(stage, f"bank{k}", [128, COLS]) for k in range(8)]
            ROW_TILES = (0, 2, 1, 3)

            def spread_picks(copy, n, t, half, b):
                lo, hi = HALVES[b]
                return copy(
                    r[lo:hi, t, :, 2 * (TOP * b + 3 * half):2 * (TOP * b + 3 * half + 3)]
                    .rearrange("c p (s a) -> c s p a", a=2),
                    psb[n % 2][lo:hi, 0:384].rearrange("c (s p a) -> c s p a", s=3, a=2))

            def spread_feat(copy, n, a):
                lo, hi = HALVES[a]
                src = psb[6 + n % 2][lo:hi, :].rearrange("c (m x) -> c m x", x=PICKS)[:, :, 0:4 * TOP]
                src = src.rearrange("c m (b s q a) -> c m b s q a", b=2, q=2, a=2)
                for q, (q_lo, q_hi) in enumerate(HALVES):
                    last = copy(feat[q_lo:q_hi, :, a, 32 * n:32 * (n + 1)].rearrange("c s (m b) -> c m b s", b=2),
                                src[:, :, :, :, q, a])
                return last

            with nc.Block() as block:
                @block.sync
                def _(sp):
                    for i, t in enumerate(ROW_TILES):
                        sp.wait_ge(s["rec"], i + 1)
                        sp.dma_start(rec_dram[128 * t:128 * (t + 1), :], rec[:, t]).then_inc(rec_out[i // 2], 16)
                        if i % 2 == 0:
                            continue
                        h = i // 2
                        sp.wait_ge(rec_out[h], 32)
                        for a in range(2):
                            rows = slice(256 * a + 128 * h, 256 * a + 128 * (h + 1))
                            sp.dma_start(grid[OC * a:OC * (a + 1), 8 * h:8 * (h + 1)]
                                         .rearrange("o p (g l) -> o (p g) l", l=TOK),
                                         rec_dram[rows].rearrange("r (o l) -> o r l", l=TOK)).then_inc(rec_in[h], 16)
                    out_pairs = out.rearrange("(a p) c h w -> a c p (h w)", a=2)

                    def store(p):
                        sp.wait_ge(s["added"], 2 * p + 2)
                        for a, (lo, hi) in enumerate(HALVES):
                            sp.dma_start(out_pairs[a, :, p], x1[lo:hi, p]).then_inc(s["stored"], 16)
                    store(0)
                    with sp.Fori(1, PAIRS) as p:
                        store(p)
                    sp.wait_ge(s["stored"], 32 * PAIRS)

                @block.vector
                def _(dve):
                    links = [0]

                    def link(ins):
                        links[0] += 1
                        ins.then_inc(s["pick"], 1)
                        dve.wait_ge(s["pick"], links[0])

                    for b, (lo, hi) in enumerate(HALVES):
                        last = dve.tensor_copy(scores[lo:hi], raw_scores[lo:hi, :, :, 2 * b:2 * b + 2])
                    last.then_inc(s["own"], 1)
                    dve.memset(zeros[:, :], 0.0)
                    dve.wait_ge(tail_in, 16 * len(tail_loads))
                    dve.wait_ge(s["exped"], 2)
                    full = [128, 4, TOK]
                    link(dve.tensor_reduce(esum[:, :], e[:, :, :], X, ALU.add))
                    link(dve.reciprocal(esum[:, :], esum[:, :]))
                    link(dve.tensor_tensor(pr[:, :, :], e[:, :, :], esum[:, :].unsqueeze(2).broadcast_to(full), ALU.mult))
                    for t in range(4):
                        last = dve.max(top[:, t], pr[:, t])
                    link(last)
                    for t in range(4):
                        last = dve.max_index(tidx[:, t], top[:, t], pr[:, t])
                    link(last)
                    link(dve.tensor_copy(tidf[:, :, :], tidx[:, :, :]))
                    for k in range(TOP):
                        last = dve.tensor_tensor(sel[:, k], iota[:, :].unsqueeze(1).broadcast_to(full),
                                                 tidf[:, :, k:k + 1].broadcast_to(full), ALU.is_equal)
                    link(last)
                    link(dve.tensor_reduce(st[:, :, :].rearrange("c t l -> c (t l)"),
                                           sel[:, :, :, :].rearrange("c k t l -> c (t l) k"), X, ALU.add))
                    for t in range(4):
                        last = dve.tensor_tensor_scan(cm[:, t], st[:, t], zeros[:, :], 0.0, ALU.add, ALU.add)
                    link(last)
                    link(dve.tensor_tensor(cm[:, :, :], cm[:, :, :], st[:, :, :], ALU.mult))
                    link(dve.tensor_tensor(st[:, :, :], st[:, :, :], pr[:, :, :], ALU.subtract))
                    link(dve.tensor_tensor(st[:, :, :], st[:, :, :], pr[:, :, :], ALU.add))
                    for k in range(TOP):
                        last = dve.scalar_tensor_tensor(sel[:, k].rearrange("c t l -> c (t l)"),
                                                        cm[:, :, :].rearrange("c t l -> c (t l)"), float(k + 1),
                                                        st[:, :, :].rearrange("c t l -> c (t l)"),
                                                        ALU.is_equal, ALU.mult)
                    link(last)
                    assert links[0] == N_PICK
                    dve.wait_ge(tail_zero, 2)
                    for n in range(4):
                        dve.wait_ge(s["picked_t"], n + 1)
                        spread_picks(dve.tensor_copy, n, n // 2, n % 2, 0).then_inc(s["picked_a"], 1)
                    dve.wait_ge(s["st_t"], 1)
                    for b, (lo, hi) in enumerate(HALVES):
                        last = dve.tensor_copy(st_t[lo:hi].rearrange("c a (n b) -> c a n b", b=2)[:, :, :, b],
                                               psb[2][lo:hi, 0:256].rearrange("c (n a) -> c a n", a=2))
                    last.then_inc(s["st_copied"], 1)
                    for n in range(8):
                        dve.wait_ge(s["feat_ps"], n + 1)
                        spread_feat(dve.tensor_copy, n, 0).then_inc(s["feat_a"], 1)
                    for i, t in enumerate(ROW_TILES):
                        dve.wait_ge(s["rec_ps"], i + 1)
                        dve.tensor_tensor(rec[:, t], psb[4 + i][:, 0:OUTDIM], mb2r[:, :], ALU.add).then_inc(s["rec"], 1)

                    def add(p):
                        for half in range(2):
                            dve.wait_ge(s["mixed"], 2 * p + half + 1)
                            v = x1[:, p, COLS * half:COLS * (half + 1)]
                            dve.tensor_tensor(v, v, psb[half][:, :], ALU.add).then_inc(s["added"], 1)
                    add(0)
                    add(1)
                    with dve.Fori(1, PAIRS // 2) as i:
                        add(2 * i)
                        add(2 * i + 1)

                @block.scalar
                def _(act):
                    def copy(dst, src):
                        return act.activation(dst, src, ACT.Copy)

                    act.preload_act_table_set(EXP_LN)
                    for t in range(2):
                        act.wait_ge(s["rows"], t + 1)
                        act.activation(e[:, 2 * t:2 * t + 2], psb[t][:, 0:128].rearrange("c (b l) -> c b l", b=2),
                                       ACT.Exp).then_inc(s["exped"], 1)
                    act.wait_ge(tail_zero, 2)
                    for n in range(4):
                        act.wait_ge(s["picked_t"], n + 1)
                        spread_picks(copy, n, n // 2, n % 2, 1).then_inc(s["picked_b"], 1)

                    def spread(n):
                        act.wait_ge(s["feat_ps"], n + 1)
                        spread_feat(copy, n, 1).then_inc(s["feat_b"], 1)
                    for n in range(8):
                        act.wait_ge(s["gathered"], n + 1)
                        after(act, s["feat_ps"], n - 1)
                        copy(picked[n % 2][:, :, :], psb[4 + n % 2][:, :].rearrange("c (m k) -> c m k", m=4))\
                            .then_inc(s["gathered_copied"], 1)
                        if n >= 1:
                            spread(n - 1)
                    spread(7)
                    for m in range(4):
                        act.wait_ge(s["hid_ps"], m + 1)
                        act.activation(hid[:, m], psb[m][0:MT, :], ACT.Relu, bias=mb[:, m:m + 1]).then_inc(s["hid"], 1)

                @block.tensor
                def _(pe):
                    pe.wait_ge(s["own"], 1)
                    for t in range(2):
                        pe.transpose(psb[t][:, 0:128], scores[:, 8 * t:8 * t + 8].rearrange("c p g a -> c (p g a)"),
                                     ident).then_inc(s["rows"], 1)
                    pe.wait_ge(s["pick"], N_PICK)
                    pe.wait_ge(s["exped"], 2)
                    for n in range(4):
                        t, half = n // 2, n % 2
                        after(pe, s["picked_a"], n - 1)
                        after(pe, s["picked_b"], n - 1)
                        for k in range(3):
                            last = pe.transpose(psb[n % 2][:, 128 * k:128 * (k + 1)],
                                                sel[:, 3 * half + k, 2 * t:2 * t + 2].rearrange("c b l -> c (b l)"),
                                                ident)
                        last.then_inc(s["picked_t"], 1)
                    for t in range(2):
                        last = pe.transpose(psb[2][:, 128 * t:128 * (t + 1)],
                                            st[:, 2 * t:2 * t + 2].rearrange("c b l -> c (b l)"), ident)
                    last.then_inc(s["st_t"], 1)
                    pe.wait_ge(s["picked_a"], 4)
                    pe.wait_ge(s["picked_b"], 4)

                    def gather(n):
                        after(pe, s["gathered_copied"], n - 1)
                        for m in range(16):
                            p, gp, j = 2 * n + m // 8, m % 8, m % 4
                            last = pe.matmul(psb[4 + n % 2][PICKS * j:PICKS * (j + 1), 128 * (m // 4):128 * (m // 4 + 1)],
                                             r[:, p // 8, 8 * (p % 8) + gp], yt[:, p, gp], start=True, stop=True)
                        last.then_inc(s["gathered"], 1)

                    def turn_back(n):
                        pe.wait_ge(s["gathered_copied"], n + 1)
                        after(pe, s["feat_a"], n - 1)
                        after(pe, s["feat_b"], n - 1)
                        for m in range(4):
                            last = pe.transpose(psb[6 + n % 2][:, 128 * m:128 * (m + 1)], picked[n % 2][:, m], ident)
                        last.then_inc(s["feat_ps"], 1)
                    gather(0)
                    for n in range(1, 8):
                        gather(n)
                        turn_back(n - 1)
                    turn_back(7)
                    pe.wait_ge(s["feat_a"], 8)
                    pe.wait_ge(s["feat_b"], 8)
                    pe.wait_ge(s["st_copied"], 1)
                    pe.wait_ge(tail_in, 16 * len(tail_loads))
                    for m in range(4):
                        cols = slice(MT * m, MT * (m + 1))
                        for k in range(TOP // 2):
                            pe.matmul(psb[m][0:MT, :], w1[:, k, cols], feat[:, k].rearrange("c a n -> c (a n)"),
                                      start=(k == 0), stop=False)
                        pe.matmul(psb[m][0:MT, :], w1s[:, cols], st_t[:, :, :].rearrange("c a n -> c (a n)"),
                                  start=False, stop=True).then_inc(s["hid_ps"], 1)
                    pe.wait_ge(s["hid"], 4)
                    for i, t in enumerate(ROW_TILES):
                        for m in range(4):
                            last = pe.matmul(psb[4 + i][:, 0:OUTDIM], hid[:, m, 128 * t:128 * (t + 1)], w2[:, m],
                                             start=(m == 0), stop=(m == 3))
                        last.then_inc(s["rec_ps"], 1)

                    def mix(p):
                        for half in range(2):
                            after(pe, s["added"], 2 * p - 1 + half)
                            for y in range(2):
                                blk = grid[:, p].rearrange("o (y x h w) -> o y h x w", y=4, x=4, h=8)[:, 2 * half + y]
                                last = pe.matmul(psb[half][:, 256 * y:256 * (y + 1)], ow[:, :], blk,
                                                 start=True, stop=True)
                            last.then_inc(s["mixed"], 1)
                    for h in range(2):
                        pe.wait_ge(rec_in[h], 32)
                        mix(8 * h)
                        mix(8 * h + 1)
                        with pe.Fori(4 * h + 1, 4 * (h + 1)) as i:
                            mix(2 * i)
                            mix(2 * i + 1)


N_PICK = 13


def shape_constants():
    rows = np.arange(128)
    ident = np.eye(128, dtype=np.float32)
    head = (rows[:, None] // DH == rows[None, :] // DH).astype(np.float32)
    image = (rows[:, None] // C == rows[None, :] // C).astype(np.float32)
    delta = ((rows[:, None] % C) // DH == np.arange(HEADS)[None, :]).astype(np.float32)
    at = np.arange(1 - WS, WS)
    rel = -np.stack(np.meshgrid(at, at, indexing="ij"), 0).reshape(2, -1).astype(np.float32)
    rel = (np.sign(rel) * np.log1p(np.abs(rel))).astype(np.float32)
    mask = np.zeros((128, 4, 2, TOK), np.float32)
    for kind in range(4):
        for w in range(2):
            low = kind // 2 == 1
            right = kind % 2 == 1 and w == 1
            ty, tx = np.arange(TOK) // WS, np.arange(TOK) % WS
            region = 2 * (low & (ty >= WS - SHIFT)) + (right & (tx >= WS - SHIFT))
            differ = region[:, None] != region[None, :]
            mask[:, kind, w] = np.tile(np.where(differ, -100.0, 0.0), (2, 1))
    iota = np.tile(np.arange(TOK, dtype=np.float32), (128, 1))
    return {"c_consts": np.concatenate([ident, head, image, delta], axis=1), "c_rel": rel, "c_mask": mask,
            "c_iota": iota}


_L0 = ["qkv_w", "proj_w", "meta_w1", "meta_b1", "meta_w2", "meta_b2", "tau", "ffn_w1", "ffn_b1", "ffn_w2"]
_VECTORS = ["qkv_b", "proj_b", "ln1_g", "ln1_b", "ln2_g", "ln2_b", "ffn_b2"]
_L1 = ["conv_w", "W1", "b1", "W2", "b2", "out_w"]
_INS = ["x"] + [f"L0_conv_{n}" for n in _L0] + [f"L1_conv_{n}" for n in _L1]


def kernel(**inputs):
    import concourse.bacc as _bacc
    from concourse.bass_utils import run_bass_kernel_spmd as _run

    nc = _bacc.Bacc("TRN2", target_bir_lowering=False, num_devices=1)
    arrays, args = {}, []
    given = {name: np.asarray(inputs[name]) for name in _INS}
    vectors = {name: np.asarray(inputs[f"L0_conv_{name}"]) for name in _VECTORS}
    given["L0_conv_ffn_b1"] = given["L0_conv_ffn_b1"].reshape(2, 128).T
    vectors = np.concatenate([vectors[name].reshape(-1, C) for name in _VECTORS]).T
    vectors = np.ascontiguousarray(np.tile(vectors, (2, 1)))
    given["L1_conv_b1"] = given["L1_conv_b1"].reshape(4, MT).T
    given["L1_conv_conv_w"] = given["L1_conv_conv_w"].T
    given["L1_conv_out_w"] = given["L1_conv_out_w"].T
    given = {name: np.ascontiguousarray(a) for name, a in given.items()}
    for name, a in (given | {"c_vecs": vectors} | shape_constants()).items():
        arrays[f"in_{name}_dram"] = a
        args.append(nc.dram_tensor(f"in_{name}_dram", a.shape, mybir.dt.from_np(a.dtype), kind="ExternalInput").ap())
    args.append(nc.dram_tensor("rec_scratch", (512, OUTDIM), F32, kind="Internal").ap())
    args.append(nc.dram_tensor("bias_scratch", (HEADS, TOK * TOK), F32, kind="Internal").ap())
    args.append(nc.dram_tensor("out_0_dram", (B, C, H, W), F32, kind="ExternalOutput").ap())
    build(nc, *args)
    r = _run(nc, [arrays], core_ids=[0])
    return r.results[0]["out_0_dram"]
```
